# Optimizing a Trainium2 kernel written in Bass

```python
import numpy as np
import jax
import jax.numpy as jnp

def _softmax(x, axis=-1):
    return jax.nn.softmax(x, axis=axis)

def _gelu(x):
    return jax.nn.gelu(x, approximate=True)

def _silu(x):
    return jax.nn.silu(x)

def _sigmoid(x):
    return jax.nn.sigmoid(x)

def _layernorm(x, axis=-1, eps=1e-05):
    m = jnp.mean(x, axis=axis, keepdims=True)
    v = jnp.var(x, axis=axis, keepdims=True)
    return (x - m) / jnp.sqrt(v + eps)

def _scatter_add(tgt, idx, src, axis=0):
    return tgt.at[idx].add(src)

def _segment_sum(src, seg, n):
    return jax.ops.segment_sum(src, seg, n)
kernel_name = 'mk_lm_tower_d1_tok_ids768_r4_c03f96'

def setup_inputs(seed: int=0):
    np.random.seed(seed)
    _w = jnp.asarray

    def _rec_inputs():
        import jax
        import jax.numpy as jnp
        _rk = jax.random.key(seed)
        x = jax.random.randint(jax.random.fold_in(_rk, 1), (8, 256), 0, 6, jnp.int32)
        mask_BS_f1_0 = jnp.where(jnp.ones((8, 256), dtype=bool), 1.0, 0.0).astype(jnp.float32)
        return (x, mask_BS_f1_0)
    x, mask_BS_f1_0 = _rec_inputs()

    def _L0_tok_setup():
        import jax, jax.numpy as jnp
        import numpy as np
        VOCAB = 6
        EPS = 1e-12

        def _conv1d_same(x, w):
            k = w.shape[-1]
            return jax.lax.conv_general_dilated(x, w, window_strides=(1,), padding=[(k // 2, k // 2)], dimension_numbers=('NCH', 'OIH', 'NCH'))
        key = jax.random.key(seed)
        k1, k2, k3, k4 = jax.random.split(key, 4)
        B, L = (32, 512)
        Cin, Cout = (VOCAB - 1, 64)
        return {'input_ids': jax.random.randint(k1, (B, L), 0, VOCAB, dtype=jnp.int64), 'attention_mask': jnp.ones((B, L), dtype=jnp.float32), 'W3': jax.random.normal(k2, (Cout, Cin, 3), dtype=jnp.float32) * 0.1, 'W5': jax.random.normal(k3, (Cout, Cin, 5), dtype=jnp.float32) * 0.1, 'W7': jax.random.normal(k4, (Cout, Cin, 7), dtype=jnp.float32) * 0.1, 'ln_gamma': jnp.ones((192,), dtype=jnp.float32), 'ln_beta': jnp.zeros((192,), dtype=jnp.float32)}
    _L0_tok_all = _L0_tok_setup()
    _L0_tok_in = {k: v for k, v in _L0_tok_all.items() if k in ('W3', 'W5', 'W7', 'ln_gamma', 'ln_beta')}
    del _L0_tok_all

    def _L0_attn_setup():
        import jax, jax.numpy as jnp
        import numpy as np
        B, T, DM = (4, 512, 192)
        H, D = (4, 64)
        DIM = H * D

        def _feature_map(x):
            return jax.nn.elu(x) + 1.0
        key = jax.random.key(seed)
        kx, kq, kk, kv, ko, kg = jax.random.split(key, 6)
        s = 0.02
        return {'x': jax.random.normal(kx, (B, T, DM), jnp.float32), 'Wq': jax.random.normal(kq, (DM, DIM), jnp.float32) * s, 'Wk': jax.random.normal(kk, (DM, DIM), jnp.float32) * s, 'Wv': jax.random.normal(kv, (DM, DIM), jnp.float32) * s, 'Wo': jax.random.normal(ko, (DIM, DM), jnp.float32) * s, 'Wg': jax.random.normal(kg, (DM, DM), jnp.float32) * s}
    _L0_attn_all = _L0_attn_setup()
    _L0_attn_in = {k: v for k, v in _L0_attn_all.items() if k in ('Wq', 'Wk', 'Wv', 'Wo', 'Wg')}
    del _L0_attn_all

    def _L0_ffn_setup():
        import jax, jax.numpy as jnp
        import numpy as np
        B, S, D = (4, 256, 192)
        E = 8
        H = 192
        HS = 768
        TOPK_ROUTED = 2
        key = jax.random.key(seed)
        ks = jax.random.split(key, 10)
        w = lambda k, shape: jax.random.normal(k, shape, dtype=jnp.float32) * 0.02
        return {'x': jax.random.normal(ks[0], (B, S, D), dtype=jnp.float32), 'router_w': w(ks[1], (D, E)), 'w_gate': w(ks[2], (E, D, H)), 'w_up': w(ks[3], (E, D, H)), 'w_down': w(ks[4], (E, H, D)), 'ws_gate': w(ks[5], (D, HS)), 'ws_up': w(ks[6], (D, HS)), 'ws_down': w(ks[7], (HS, D)), 'sg_w': w(ks[8], (D, 1)), 'sg_b': jnp.zeros((1,), jnp.float32)}
    _L0_ffn_all = _L0_ffn_setup()
    _L0_ffn_in = {k: v for k, v in _L0_ffn_all.items() if k in ('router_w', 'w_gate', 'w_up', 'w_down', 'ws_gate', 'ws_up', 'ws_down', 'sg_w', 'sg_b')}
    del _L0_ffn_all
    return {'x': x, 'mask_BS_f1_0': mask_BS_f1_0, 'L0_tok_W3': _L0_tok_in['W3'], 'L0_tok_W5': _L0_tok_in['W5'], 'L0_tok_W7': _L0_tok_in['W7'], 'L0_tok_ln_gamma': _L0_tok_in['ln_gamma'], 'L0_tok_ln_beta': _L0_tok_in['ln_beta'], 'L0_attn_Wq': _L0_attn_in['Wq'], 'L0_attn_Wk': _L0_attn_in['Wk'], 'L0_attn_Wv': _L0_attn_in['Wv'], 'L0_attn_Wo': _L0_attn_in['Wo'], 'L0_attn_Wg': _L0_attn_in['Wg'], 'L0_ffn_router_w': _L0_ffn_in['router_w'], 'L0_ffn_w_gate': _L0_ffn_in['w_gate'], 'L0_ffn_w_up': _L0_ffn_in['w_up'], 'L0_ffn_w_down': _L0_ffn_in['w_down'], 'L0_ffn_ws_gate': _L0_ffn_in['ws_gate'], 'L0_ffn_ws_up': _L0_ffn_in['ws_up'], 'L0_ffn_ws_down': _L0_ffn_in['ws_down'], 'L0_ffn_sg_w': _L0_ffn_in['sg_w'], 'L0_ffn_sg_b': _L0_ffn_in['sg_b']}

def reference(x, mask_BS_f1_0, L0_tok_W3, L0_tok_W5, L0_tok_W7, L0_tok_ln_gamma, L0_tok_ln_beta, L0_attn_Wq, L0_attn_Wk, L0_attn_Wv, L0_attn_Wo, L0_attn_Wg, L0_ffn_router_w, L0_ffn_w_gate, L0_ffn_w_up, L0_ffn_w_down, L0_ffn_ws_gate, L0_ffn_ws_up, L0_ffn_ws_down, L0_ffn_sg_w, L0_ffn_sg_b):
    import jax
    import jax.numpy as jnp

    def _L0_tok_ref(input_ids, attention_mask, W3, W5, W7, ln_gamma, ln_beta):
        import jax, jax.numpy as jnp
        import numpy as np
        VOCAB = 6
        EPS = 1e-12

        def _conv1d_same(x, w):
            k = w.shape[-1]
            return jax.lax.conv_general_dilated(x, w, window_strides=(1,), padding=[(k // 2, k // 2)], dimension_numbers=('NCH', 'OIH', 'NCH'))
        oh = jax.nn.one_hot(input_ids, VOCAB, dtype=jnp.float32)[:, :, :VOCAB - 1]
        x = jnp.transpose(oh, (0, 2, 1))
        h = jnp.concatenate([_conv1d_same(x, W3), _conv1d_same(x, W5), _conv1d_same(x, W7)], axis=1)
        h = h * attention_mask[:, None, :]
        h = jnp.transpose(h, (0, 2, 1))
        mu = jnp.mean(h, axis=-1, keepdims=True)
        var = jnp.mean(jnp.square(h - mu), axis=-1, keepdims=True)
        out = (h - mu) * jax.lax.rsqrt(var + EPS) * ln_gamma + ln_beta
        return out

    def _L0_attn_ref(x, Wq, Wk, Wv, Wo, Wg):
        import jax, jax.numpy as jnp
        import numpy as np
        B, T, DM = (4, 512, 192)
        H, D = (4, 64)
        DIM = H * D

        def _feature_map(x):
            return jax.nn.elu(x) + 1.0
        Bx, Tx, _ = x.shape
        q = _feature_map((x @ Wq).reshape(Bx, Tx, H, D))
        k = _feature_map((x @ Wk).reshape(Bx, Tx, H, D))
        v = (x @ Wv).reshape(Bx, Tx, H, D)
        qT = q.transpose(1, 0, 2, 3)
        kT = k.transpose(1, 0, 2, 3)
        vT = v.transpose(1, 0, 2, 3)
        S0 = jnp.zeros((Bx, H, D, D), x.dtype)
        z0 = jnp.zeros((Bx, H, D), x.dtype)

        def step(carry, inp):
            S, z = carry
            qi, ki, vi = inp
            S = S + ki[..., :, None] * vi[..., None, :]
            z = z + ki
            num = jnp.einsum('bhd,bhde->bhe', qi, S)
            den = jnp.maximum(jnp.sum(qi * z, axis=-1), 1e-06)
            return ((S, z), num / den[..., None])
        (_, _), outT = jax.lax.scan(step, (S0, z0), (qT, kT, vT))
        out = outT.transpose(1, 0, 2, 3).reshape(Bx, Tx, DIM)
        gate = jax.nn.sigmoid(x @ Wg)
        return out @ Wo * gate

    def _L0_ffn_ref(x, router_w, w_gate, w_up, w_down, ws_gate, ws_up, ws_down, sg_w, sg_b):
        import jax, jax.numpy as jnp
        import numpy as np
        B, S, D = (4, 256, 192)
        E = 8
        H = 192
        HS = 768
        TOPK_ROUTED = 2
        probs = jax.nn.softmax(x @ router_w, axis=-1)
        gates, idx = jax.lax.top_k(probs, TOPK_ROUTED)
        gates = gates / jnp.sum(gates, axis=-1, keepdims=True)
        n_exp = router_w.shape[1]
        dense_g = jnp.sum(jax.nn.one_hot(idx, n_exp, dtype=x.dtype) * gates[..., None], axis=-2)
        g = jax.nn.silu(jnp.einsum('bsd,edh->bseh', x, w_gate))
        u = jnp.einsum('bsd,edh->bseh', x, w_up)
        expert_out = jnp.einsum('bseh,ehd->bsed', g * u, w_down)
        routed = jnp.einsum('bse,bsed->bsd', dense_g, expert_out)
        shared = jax.nn.silu(x @ ws_gate) * (x @ ws_up) @ ws_down
        alpha = jax.nn.sigmoid(x @ sg_w + sg_b)
        return alpha * shared + (1.0 - alpha) * routed
    h = _L0_tok_ref(x, mask_BS_f1_0, L0_tok_W3, L0_tok_W5, L0_tok_W7, L0_tok_ln_gamma, L0_tok_ln_beta)
    h = h + _L0_attn_ref(_layernorm(h, axis=-1), L0_attn_Wq, L0_attn_Wk, L0_attn_Wv, L0_attn_Wo, L0_attn_Wg)
    h = h + _L0_ffn_ref(_layernorm(h, axis=-1), L0_ffn_router_w, L0_ffn_w_gate, L0_ffn_w_up, L0_ffn_w_down, L0_ffn_ws_gate, L0_ffn_ws_up, L0_ffn_ws_down, L0_ffn_sg_w, L0_ffn_sg_b)
    return h

_drawn_inputs = setup_inputs


def setup_inputs(seed=0):
    import zlib

    import numpy as np

    out = dict(_drawn_inputs(seed))
    spreads = {'L0_tok_ln_gamma': (1.0, 0.2), 'L0_tok_ln_beta': (0.0, 0.1)}
    factors = {'L0_attn_Wq': 8.0,
     'L0_attn_Wk': 8.0,
     'L0_attn_Wv': 3.351,
     'L0_attn_Wo': 3.13,
     'L0_attn_Wg': 8.0,
     'L0_ffn_router_w': 8.0,
     'L0_ffn_w_gate': 8.0,
     'L0_ffn_w_up': 8.0,
     'L0_ffn_w_down': 8.0,
     'L0_ffn_ws_gate': 5.069,
     'L0_ffn_ws_up': 5.031,
     'L0_ffn_ws_down': 4.958,
     'L0_ffn_sg_w': 8.0}
    for name, (base, spread) in spreads.items():
        noise = np.random.default_rng([zlib.crc32(name.encode()), seed]).standard_normal(out[name].shape)
        drawn = base * np.exp(spread * noise) if base else spread * noise
        out[name] = jnp.asarray(drawn.astype(out[name].dtype))
    for name, factor in factors.items():
        out[name] = (out[name] * factor).astype(out[name].dtype)
    return out
```

```python
from contextlib import ExitStack

import concourse.bass as bass
import numpy as np
from concourse import mybir

F32 = mybir.dt.float32
F32R = mybir.dt.float32r
I32 = mybir.dt.int32
U32 = mybir.dt.uint32
ALU = mybir.AluOpType
AX = mybir.AxisListType
ACT = mybir.ActivationFunctionType
AX = mybir.AxisListType

P = 128
B, S, D = 8, 256, 192
TILES = B * S // P
GROUPS = 4
GT = TILES // GROUPS
GN = GT * P
D1 = D - P
HEADS, HD = 4, 64
TAPS, CLS = 7, 5
WIN = TAPS * CLS
EXPERTS, HID = 8, 192
SLOTS = 2 * TILES + EXPERTS - 1
LANES = 3
ROUNDS = SLOTS // LANES
SHARED = 768
HTILES = SHARED // P
CHUNK = 2 * HID
CHUNKS = EXPERTS + 2 * SHARED // CHUNK
ROUTER = 32
WIN_LO = 64
UROWS = WIN_LO + WIN


def pieces(xt, blocks, cols, tok):
    for a, b in ((0, 0), (1, 0), (0, 1), (2, 2), (2, 3)):
        yield xt[:, a, tok], blocks[:, b, cols]


def tower(nc, windows, classes, conv_w, tok_mask, gamma, beta, w_qk, w_vg, w_o, ident_in, w_gu, w_dn, w_sdn,
          w_router, gate_bias, counting, out):
    ctx = ExitStack()
    with ctx:
        def sb(name, shape, dt=F32):
            return ctx.enter_context(nc.sbuf_tensor(name, shape, dt))

        def sem(name):
            return ctx.enter_context(nc.semaphore(name))

        sorted_x = nc.dram_tensor("sorted_x", [SLOTS * P, D], F32, kind="Internal").ap()
        sorted_y = nc.dram_tensor("sorted_y", [SLOTS * P, D], F32, kind="Internal").ap()
        bank = [ctx.enter_context(nc.psum_tensor(f"bank{i}", [P, 512], F32)) for i in range(8)]

        h = sb("h", [P, TILES, D])
        ident = sb("ident", [P, P])
        stat = sb("stat", [P, 3, GT, 6])
        mv = sb("mv", [P, 3, GT, 2])
        var_eps = sb("var_eps", [P, 3, GT])
        rstd = sb("rstd", [P, 2, GT])
        mean3 = sb("mean3", [P, TILES])
        rstd3 = sb("rstd3", [P, TILES])
        half_neg = sb("half_neg", [P, GT])
        zero = sb("zero", [P, D])
        wgu = sb("wgu", [P, 4, CHUNKS * CHUNK], F32R)
        stage = sb("stage", [P, LANES, 2, CHUNK])
        count = sb("count", [P, P + TILES + EXPERTS + SLOTS])
        below, steps = count[:, 0:P], count[:, P:P + TILES]
        desc, slot_no = count[:, P + TILES:P + TILES + EXPERTS], count[:, P + TILES + EXPERTS:]
        ones = sb("ones", [P, P])
        raw_r = sb("raw_r", [P, 2, ROUTER])
        wr = sb("wr", [P, 4, ROUTER], F32R)
        gb = sb("gb", [P, 1])
        half_gb = sb("half_gb", [P, 1])

        early = ExitStack()

        def sa(name, shape, dt=F32):
            return early.enter_context(nc.sbuf_tensor(name, shape, dt))

        xn = sa("xn", [P, GT, D])
        xt = sa("xt", [P, 3, GN], F32R)
        wqk = sa("wqk", [P, 4, 512], F32R)
        wvg = sa("wvg", [P, 4, 448], F32R)
        wo = sa("wo", [P, 2, D])
        ids = sa("ids", [UROWS, 2, GN], I32)
        onehot = sa("onehot", [UROWS, GN], F32R)
        cls = sa("cls", [P, 1])
        cw = sa("cw", [UROWS, D])
        cwr = sa("cwr", [UROWS, D], F32R)
        msk = sa("msk", [P, TILES])
        gam = sa("gam", [P, D])
        bet = sa("bet", [P, D])
        emb = sa("emb", [P, GT, D])
        raw_flat = stage[:, :, :, :].rearrange("p a b c -> p (a b c)")
        raw_qk = raw_flat[:, 0:1024].rearrange("p (k n) -> p k n", k=2)
        raw_vg = raw_flat[:, 1024:1920].rearrange("p (k n) -> p k n", k=2)
        kphi = sa("kphi", [P, 2, GN])
        qz = sa("qz", [P, HEADS, GN])
        xp1 = sa("xp1", [P, 2, GN])
        ex = sa("ex", [P, 2, GN])
        vp = sa("vp", [P, GT, HEADS, P])
        sT = sa("sT", [P, 4, 384])
        gt = sa("gt", [P, GT, D])
        numden = sa("numden", [P, HEADS, GN])
        den = sa("den", [P, GT, HEADS, 1])
        rec = sa("rec", [P, GT, HEADS, 1])
        recB = sa("recB", [P, GT, HEADS, HD])
        oT = sa("oT", [P, 2, GN])
        early.close()

        x3 = sb("x3", [P, TILES, D])
        x3t = sb("x3t", [P, 3, B * S], F32R)
        wdn = sb("wdn", [P, EXPERTS, 2, D])
        wsdn = sb("wsdn", [P, HTILES, D])
        lgT = sb("lgT", [ROUTER, 2, GN])
        lg = sb("lg", [P, TILES, EXPERTS + 1])
        prob = sb("prob", [P, TILES, EXPERTS])
        pick = sb("pick", [P, 2, TILES, EXPERTS])
        best = sb("best", [P, 2, TILES, 1])
        gates = sb("gates", [P, 2, TILES])
        tmp = sb("tmp", [P, TILES, EXPERTS])
        tmp2 = sb("tmp2", [P, TILES, EXPERTS])
        one = sb("one", [P, TILES, 1])
        alpha = sb("alpha", [P, 2, TILES])
        taken = sb("taken", [P, TILES, EXPERTS])
        run = sb("run", [P, 2, EXPERTS + TILES, EXPERTS])
        wide = sb("wide", [P, EXPERTS, TILES])
        ends = sb("ends", [P, 3, 4 + EXPERTS])
        at_slot = sb("at_slot", [1, SLOTS, EXPERTS])
        expert_f = sb("expert_f", [1, SLOTS, 1])
        expert = sb("expert", [1, SLOTS], I32)
        pos_f = sb("pos_f", [P, 2, TILES])
        pos = sb("pos", [P, 2, TILES], I32)
        sg = sb("sg", [P, 2, GN])
        hid = sb("hid", [P, HTILES, GN])
        xs = sb("xs", [P, 2, LANES, D])
        xst = sb("xst", [P, 3, LANES * P], F32R)
        sgs = sb("sgs", [P, LANES, HID])
        hs = sb("hs", [P, LANES, HID])
        hsT = sb("hsT", [P, 2, LANES * P])
        ys = sb("ys", [P, LANES, D])
        back = [x3, wgu[:, 0, 0:TILES * D].bitcast(F32).rearrange("p (t d) -> p t d", d=D)]

        s_win0 = sem("s_win0")
        s_win = sem("s_win")
        s_small = sem("s_small")
        s_aw = sem("s_aw")
        s_idn = sem("s_idn")
        s_const = sem("s_const")
        s_passed = sem("s_passed")
        s_mean = sem("s_mean")
        s_oh = sem("s_oh")
        s_cwr = sem("s_cwr")
        s_whi = sem("s_whi")
        s_wlo = sem("s_wlo")
        s_conv = sem("s_conv")
        s_emb = sem("s_emb")
        s_bn = [sem(f"s_bn{k}") for k in range(3)]
        s_mv = [sem(f"s_mv{k}") for k in range(3)]
        s_ve = [sem(f"s_ve{k}") for k in range(3)]
        s_rs = [sem(f"s_rs{k}") for k in range(3)]
        s_gam = sem("s_gam")
        s_h0 = sem("s_h0")
        s_xn = sem("s_xn")
        s_T = sem("s_T")
        s_hi = sem("s_hi")
        s_lo = sem("s_lo")
        s_proj = sem("s_proj")
        s_act = sem("s_act")
        s_phi = sem("s_phi")
        s_vg = sem("s_vg")
        s_sc = sem("s_sc")
        s_ev = sem("s_ev")
        s_mask = sem("s_mask")
        s_pv = sem("s_pv")
        s_nd = sem("s_nd")
        s_denT = sem("s_denT")
        s_den = sem("s_den")
        s_rec = sem("s_rec")
        s_recB = sem("s_recB")
        s_recT = sem("s_recT")
        s_nrm = sem("s_nrm")
        s_wo = sem("s_wo")
        s_wog = sem("s_wog")
        s_res = sem("s_res")
        s_zx = sem("s_zx")
        s_wst = [sem(f"s_wst{j}") for j in range(LANES)]
        s_ghi = sem("s_ghi")
        s_glo = sem("s_glo")
        s_cst = sem("s_cst")
        s_wr = sem("s_wr")
        s_wdn = sem("s_wdn")
        s_x3 = sem("s_x3")
        s_T3 = sem("s_T3")
        s_hi3 = sem("s_hi3")
        s_lo3 = sem("s_lo3")
        s_lgT = sem("s_lgT")
        s_lgc = sem("s_lgc")
        s_lg = sem("s_lg")
        s_lgv = sem("s_lgv")
        s_r = sem("s_r")
        s_diff = sem("s_diff")
        s_exp = sem("s_exp")
        s_taken = sem("s_taken")
        s_cnt = sem("s_cnt")
        s_pos = sem("s_pos")
        s_eid = sem("s_eid")
        s_scat = sem("s_scat")
        s_sgu = sem("s_sgu")
        s_sg = sem("s_sg")
        s_hid = sem("s_hid")
        s_sdn = sem("s_sdn")
        s_shr = sem("s_shr")
        s_xl = [sem(f"s_xl{j}") for j in range(2 * LANES)]
        s_xT = sem("s_xT")
        s_xhi = sem("s_xhi")
        s_xlo = sem("s_xlo")
        s_gu = sem("s_gu")
        s_si = sem("s_si")
        s_hs = sem("s_hs")
        s_hT = sem("s_hT")
        s_hTc = sem("s_hTc")
        s_dn = sem("s_dn")
        s_ys = sem("s_ys")
        s_st = [sem(f"s_st{j}") for j in range(LANES)]
        s_back = [sem(f"s_back{t}") for t in range(TILES)]
        s_sum = sem("s_sum")
        s_out = sem("s_out")

        def wait(eng, s, value):
            if not isinstance(value, int) or value > 0:
                eng.wait_ge(s, value)

        def wait_apart(eng, s, value):
            eng.wait_ge(s, value)
            eng.sem_inc(s_passed, 1)

        def down_bank(j):
            return bank[4][:, 0:D] if j == 2 else bank[7][:, j * D:(j + 1) * D]

        def tile_of(x, g, t):
            return x[:, bass.ds(g * GT + t, 1)]

        block = ctx.enter_context(nc.Block())

        @block.sync
        def _(sp):
            sp.dma_start(ids[:, 0, :], windows[:, 0:GN]).then_inc(s_win0, 16)
            sp.dma_start(cls[:, :], classes).then_inc(s_small, 16)
            sp.dma_start(msk[:, :], tok_mask).then_inc(s_small, 16)
            sp.dma_start(raw_qk, w_qk).then_inc(s_aw, 16)
            sp.dma_start(raw_vg, w_vg).then_inc(s_aw, 16)
            sp.dma_start(wo[:, :, :], w_o).then_inc(s_idn, 16)
            sp.dma_start(ids[:, 1, :], windows[:, GN:2 * GN]).then_inc(s_win, 16)
            sp.dma_start(count[:, :], counting).then_inc(s_cst, 16)
            sp.dma_start(raw_r[:, :, :], w_router).then_inc(s_cst, 16)
            sp.dma_start(gb[:, :], gate_bias).then_inc(s_cst, 16)
            sp.wait_ge(s_const, 1)
            sp.dma_start(sorted_x.rearrange("(s p) d -> p s d", p=P),
                         zero[:, :].unsqueeze(1).to_broadcast([P, SLOTS, D])).then_inc(s_zx, 16)
            sp.wait_ge(s_wlo, 2)
            for g in range(GROUPS):
                if g in (1, 2):
                    sp.wait_ge(s_oh, g)
                    sp.wait_ge(s_win, 16 * g)
                    sp.dma_start(ids[:, (g + 1) % 2, :], windows[:, (g + 1) * GN:(g + 2) * GN]).then_inc(s_win, 16)
                for j in range(LANES):
                    if g:
                        sp.wait_ge(s_glo, LANES * (g - 1) + j + 1)
                    sp.dma_start(stage[:, j, :, :], w_gu[:, LANES * g + j, :, :]).then_inc(s_wst[j], 16)
            sp.wait_ge(s_res, TILES)
            sp.dma_start(wsdn[:, :, :], w_sdn).then_inc(s_wdn, 16)
            sp.dma_start(wdn[:, :, :, :], w_dn).then_inc(s_wdn, 16)

            def load(i, odd):
                for j in range(LANES):
                    sp.dma_start(xs[:, odd, j, :], sorted_x[bass.ds((i * LANES + j) * P, P), :]
                                 ).then_inc(s_xl[odd * LANES + j], 16)

            def store(i):
                for j in range(LANES):
                    sp.wait_ge(s_ys, LANES * i + j + 1)
                    sp.dma_start(sorted_y[bass.ds((i * LANES + j) * P, P), :], ys[:, j, :]).then_inc(s_st[j], 16)

            sp.wait_ge(s_scat, 16 * 2 * TILES)
            load(0, 0)
            load(1, 1)
            sp.wait_ge(s_xT, 1)
            load(2, 0)
            with sp.Fori(0, (ROUNDS - 3) // 2) as n:
                for k in range(2):
                    sp.wait_ge(s_xT, 2 * n + k + 2)
                    load(2 * n + k + 3, 1 - k)
                    store(2 * n + k)
            for i in range(ROUNDS - 3, ROUNDS):
                store(i)
            for t in range(TILES):
                sp.wait_ge(s_sum, 2 * t + 2)
                sp.wait_ge(s_shr, t + 1)
                sp.dma_start(out[:, t * D:(t + 1) * D], h[:, t, :]).then_inc(s_out, 16)
            sp.wait_ge(s_out, 16 * TILES)

        @block.gpsimd
        def _(pool):
            pool.memset(zero[:, :], 0.0).then_inc(s_const, 1)
            pool.memset(half_neg[:, :], -0.5).then_inc(s_const, 1)
            pool.memset(qz[:, :, :], 0.0).then_inc(s_const, 1)

            def rsqrt(k, g):
                pool.wait_ge(s_ve[k], g + 1)
                out = rstd[:, k, :] if k < 2 else rstd3[:, bass.ds(g * GT, GT)]
                pool.tensor_tensor(out, var_eps[:, k, :], half_neg[:, :], ALU.pow).then_inc(s_rs[k], 1)

            def affine(g, n):
                wait_apart(pool, s_ev, 8 * g + n + 1)
                diag = sT[:, n % 4, :].rearrange("p (b q) -> p b q", q=P)[:, 0::2, :]
                pool.affine_select(out=diag, in_=diag, compare_op=ALU.is_ge, fill=0.0, base=0,
                                   pattern=[[0, 2], [1, P]], channel_multiplier=-1).then_inc(s_mask, 1)

            def low_chunk(g, j):
                pool.wait_ge(s_ghi, LANES * g + j + 1)
                at = bass.ds((LANES * g + j) * CHUNK, CHUNK)
                pool.tensor_tensor(wgu[:, 1::2, at], stage[:, j, :, :], wgu[:, 0::2, at].bitcast(F32),
                                   ALU.subtract).then_inc(s_glo, 1)

            def attention(g, before, more):
                for n in range(8):
                    affine(g, n)
                    if n in (0, 3) and more:
                        rsqrt(n // 3, g + 1)
                    if n == 1 and before:
                        rsqrt(2, g - 1)
                    if n in (2, 4, 6):
                        low_chunk(g, n // 2 - 1)

            pool.wait_ge(s_const, 2)
            rsqrt(0, 0)
            pool.memset(vp[:, :, :, :], 1.0).then_inc(s_const, 1)
            pool.memset(ones[:, :], 1.0).then_inc(s_const, 1)
            pool.wait_ge(s_whi, 2)
            pool.tensor_tensor(wvg[:, 1::2, :], raw_vg, wvg[:, 0::2, :].bitcast(F32), ALU.subtract).then_inc(s_wlo, 1)
            rsqrt(1, 0)
            attention(0, False, True)
            with pool.Fori(1, GROUPS - 1) as g:
                attention(g, True, True)
            attention(GROUPS - 1, True, False)
            rsqrt(2, GROUPS - 1)

            pool.wait_ge(s_zx, 16)
            pool.wait_ge(s_pos, 1)
            for t in range(TILES):
                for k in range(2):
                    pool.indirect_dma_start(out=sorted_x, out_offset=bass.IndirectOffsetOnAxis(
                        ap=pos[:, k, t:t + 1].bitcast(U32), axis=0), in_=x3[:, t, :], in_offset=None,
                        bounds_check=SLOTS * P - 1, oob_is_err=True).then_inc(s_scat, 16)
            for j in range(LANES):
                pool.wait_ge(s_st[j], 16 * ROUNDS)
            for t in range(TILES):
                for k in range(2):
                    pool.indirect_dma_start(out=back[k][:, t, :], out_offset=None, in_=sorted_y,
                                            in_offset=bass.IndirectOffsetOnAxis(
                        ap=pos[:, k, t:t + 1].bitcast(U32), axis=0),
                        bounds_check=SLOTS * P - 1, oob_is_err=True).then_inc(s_back[t], 16)

        @block.scalar
        def _(act):
            act.dma_start(cw[:, :], conv_w).then_inc(s_small, 16)
            act.dma_start(gam[:, :], gamma).then_inc(s_small, 16)
            act.dma_start(bet[:, :], beta).then_inc(s_small, 16)
            act.dma_start(ident[:, :], ident_in).then_inc(s_idn, 16)

            def embed(g):
                for t in range(GT):
                    if t % 2 == 0:
                        act.wait_ge(s_conv, 2 * g + t // 2 + 1)
                    act.activation(emb[:, t, :], bank[t // 2][:, (t % 2) * D:(t % 2 + 1) * D], ACT.Copy,
                                   scale=msk[:, bass.ds(g * GT + t, 1)]).then_inc(s_emb, 1)

            def high(g):
                act.wait_ge(s_T, g + 1)
                act.activation(xt[:, 0, :], bank[0][:, :], ACT.Copy).then_inc(s_hi, 1)
                act.activation(xt[0:D1, 2, :], bank[1][0:D1, :], ACT.Copy).then_inc(s_hi, 1)

            def feature_parts(g):
                for m in range(4):
                    act.wait_ge(s_proj, 8 * g + m + 1)
                    wait(act, s_phi, 6 * g + (-2, 0, 1, 3)[m])
                    act.activation(xp1[:, m % 2, :], bank[2 + m % 2][:, :], ACT.Copy, bias=1.0).then_inc(s_act, 1)
                    act.activation(ex[:, m % 2, :], bank[2 + m % 2][:, :], ACT.Exp).then_inc(s_act, 1)

            def values_gates(g):
                for t in range(GT):
                    act.wait_ge(s_proj, 8 * g + 5 + t)
                    b = bank[2 + t % 2]
                    v = vp[:, t, :, :].rearrange("p (a b) c -> p a (b c)", b=2)
                    for odd in range(2):
                        act.activation(v[:, :, 3 * HD * odd:3 * HD * odd + HD],
                                       b[:, 0:256].rearrange("p (a b c) -> p a b c", a=2, b=2)[:, :, odd, :],
                                       ACT.Copy).then_inc(s_vg, 1)
                    wait(act, s_res, GT * (g - 1) + t + 1)
                    act.activation(gt[:, t, :], b[:, 256:448], ACT.Tanh, scale=0.5).then_inc(s_vg, 1)

            def heads(g, more):
                for n in range(8):
                    act.wait_ge(s_sc, 8 * g + n + 1)
                    if n >= 4:
                        act.wait_ge(s_pv, 8 * g + n - 3)
                    act.activation(sT[:, n % 4, :], bank[4 + n % 2][:, 0:384], ACT.Copy).then_inc(s_ev, 1)
                    if n >= 3 and n % 2:
                        numerators(g, n // 2 - 1)
                    if n == 6 and more:
                        high(g + 1)
                    if n in (1, 3, 5):
                        high_chunk(g, n // 2)
                numerators(g, 3)

            def numerators(g, hd):
                act.wait_ge(s_pv, 8 * g + 2 * hd + 2)
                act.activation(numden[:, hd, :], bank[6 + hd % 2][:, :], ACT.Copy).then_inc(s_nd, 1)

            def high_chunk(g, j):
                act.wait_ge(s_wst[j], 16 * g + 16)
                act.activation(wgu[:, 0::2, bass.ds((LANES * g + j) * CHUNK, CHUNK)], stage[:, j, :, :],
                               ACT.Copy).then_inc(s_ghi, 1)

            def attention(g, more):
                feature_parts(g)
                if more:
                    embed(g + 1)
                values_gates(g)
                heads(g, more)

            act.wait_ge(s_small, 80)
            embed(0)
            act.wait_ge(s_aw, 32)
            act.activation(wqk[:, 0::2, :], raw_qk[:, :, :], ACT.Copy).then_inc(s_whi, 1)
            act.activation(wvg[:, 0::2, :], raw_vg[:, :, :], ACT.Copy).then_inc(s_whi, 1)
            high(0)
            act.wait_ge(s_const, 5)
            attention(0, True)
            with act.Fori(1, GROUPS - 1) as g:
                attention(g, True)
            attention(GROUPS - 1, False)

            act.wait_ge(s_cst, 48)
            act.activation(wr[:, 0::2, :], raw_r[:, :, :], ACT.Copy).then_inc(s_wr, 1)
            act.activation(half_gb[:, :], gb[:, :], ACT.Copy, scale=0.5).then_inc(s_wr, 1)

            def high3(g):
                act.wait_ge(s_T3, g + 1)
                tok = slice(g * GN, (g + 1) * GN)
                act.activation(x3t[:, 0, tok], bank[0][:, :], ACT.Copy).then_inc(s_hi3, 1)
                act.activation(x3t[0:D1, 2, tok], bank[1][0:D1, :], ACT.Copy).then_inc(s_hi3, 1)

            def logits(g):
                act.wait_ge(s_lgT, g + 1)
                if g >= 2:
                    act.wait_ge(s_lg, g - 1)
                act.activation(lgT[:, g % 2, :], bank[2 + g % 2][0:ROUTER, :], ACT.Copy).then_inc(s_lgc, 1)

            for g in range(GROUPS + 1):
                if g < GROUPS:
                    high3(g)
                if g >= 1:
                    logits(g - 1)
            act.wait_ge(s_wr, 3)
            act.wait_ge(s_diff, 1)
            act.activation(prob[:, :, :], tmp[:, :, :], ACT.Exp).then_inc(s_exp, 1)
            act.activation(one[:, :, 0], lg[:, :, EXPERTS], ACT.Tanh, bias=half_gb[:, 0:1], scale=0.5).then_inc(s_exp, 1)

            def shared(g, first, behind):
                for m in range(first, behind):
                    act.wait_ge(s_sgu, HTILES * g + m + 1)
                    wait(act, s_hid, HTILES * g + m - 1)
                    act.activation(sg[:, m % 2, :], bank[2 + 2 * (m % 2)][:, :], ACT.Silu).then_inc(s_sg, 1)

            shared(0, 0, HTILES)
            shared(1, 0, HTILES)
            shared(2, 0, 2)

            def high_rows(i):
                act.wait_ge(s_xT, i + 1)
                act.activation(xst[:, 0, :], bank[0][:, 0:LANES * P], ACT.Copy).then_inc(s_xhi, 1)
                act.activation(xst[0:D1, 2, :], bank[1][0:D1, 0:LANES * P], ACT.Copy).then_inc(s_xhi, 1)

            def gate(i, j):
                act.wait_ge(s_gu, LANES * i + j + 1)
                act.activation(sgs[:, j, :], bank[2 + j][:, 0:HID], ACT.Silu).then_inc(s_si, 1)

            def results(i):
                for j in range(LANES):
                    act.wait_ge(s_dn, LANES * i + (2, 2, 3)[j])
                    if not isinstance(i, int) or i:
                        act.wait_ge(s_st[j], 16 * i)
                    act.activation(ys[:, j, :], down_bank(j), ACT.Copy).then_inc(s_ys, 1)

            def round_(i, before, more):
                gate(i, 0)
                gate(i, 1)
                gate(i, 2)
                if more:
                    high_rows(i + 1)
                if before:
                    results(i - 1)
                act.wait_ge(s_hT, i + 1)
                act.activation(hsT[:, 0, :], bank[5][:, 0:LANES * P], ACT.Copy).then_inc(s_hTc, 1)
                act.activation(hsT[0:HID - P, 1, :], bank[6][0:HID - P, 0:LANES * P], ACT.Copy).then_inc(s_hTc, 1)

            high_rows(0)
            round_(0, False, True)
            with act.Fori(1, ROUNDS - 1) as i:
                round_(i, True, True)
            round_(ROUNDS - 1, True, False)
            results(ROUNDS - 1)
            shared(2, 2, HTILES)
            shared(3, 0, HTILES)

        @block.vector
        def _(dve):
            def make_onehot(g):
                dve.tensor_scalar(onehot[:, :], ids[:, bass.ds(g % 2, 1), :].rearrange("p a n -> p (a n)"), cls[0:UROWS, 0:1], None,
                                  ALU.is_equal).then_inc(s_oh, 1)

            def statistics(k, g, src, eps):
                for t in range(GT):
                    dve.bn_stats(stat[:, k, t, :], src(t)).then_inc(s_bn[k], 1)
                wait_apart(dve, s_bn[k], g * GT + GT)
                for t in range(GT):
                    dve.bn_aggr(mv[:, k, t, :], stat[:, k, t, :]).then_inc(s_mv[k], 1)
                dve.wait_ge(s_mv[k], g * GT + GT)
                dve.tensor_scalar(var_eps[:, k, :], mv[:, k, :, 1], eps, None, ALU.add).then_inc(s_ve[k], 1)
                if k == 2:
                    dve.tensor_copy(mean3[:, bass.ds(g * GT, GT)], mv[:, k, :, 0]).then_inc(s_mean, 1)

            def embedding_norm(g, n):
                dve.wait_ge(s_rs[0], g + 1)
                for t in range(GT):
                    dve.scalar_tensor_tensor(out=emb[:, t, :], in0=emb[:, t, :], scalar=mv[:, 0, t, 0:1],
                                             in1=gam[:, :], op0=ALU.subtract, op1=ALU.mult).then_inc(s_gam, 1)
                for t in range(GT):
                    dve.wait_ge(s_gam, GT * g + t + 1)
                    dve.scalar_tensor_tensor(out=tile_of(h, g, t)[:, 0, :], in0=emb[:, t, :],
                                             scalar=rstd[:, 0, t:t + 1],
                                             in1=bet[:, :], op0=ALU.mult, op1=ALU.add).then_inc(s_h0, 1)
                wait_apart(dve, s_h0, GT * g + GT)

            def normed(g):
                dve.wait_ge(s_rs[1], g + 1)
                for t in range(GT):
                    dve.tensor_scalar(xn[:, t, :], tile_of(h, g, t)[:, 0, :], mv[:, 1, t, 0:1], rstd[:, 1, t:t + 1],
                                      ALU.subtract, ALU.mult).then_inc(s_xn, 1)

            def low(g):
                dve.wait_ge(s_hi, 2 * g + 2)
                dve.tensor_tensor(xt[:, 1, :], bank[0][:, :], xt[:, 0, :].bitcast(F32), ALU.subtract).then_inc(s_lo, 1)
                dve.tensor_tensor(xt[D1:P, 2, :], bank[1][0:D1, :], xt[0:D1, 2, :].bitcast(F32),
                                  ALU.subtract).then_inc(s_lo, 1)

            def features(g):
                for m in range(4):
                    dve.wait_ge(s_act, 8 * g + 2 * m + 2)
                    pair = m // 2
                    parts = [(kphi[:, pair, :], slice(0, P))] if m % 2 == 0 else \
                        [(qz[0:HD, 2 * pair, :], slice(0, HD)), (qz[HD:P, 2 * pair + 1, :], slice(HD, P))]
                    for dst, r in parts:
                        dve.scalar_tensor_tensor(out=dst, in0=ex[r, m % 2, :], scalar=1.0, in1=xp1[r, m % 2, :],
                                                 op0=ALU.min, op1=ALU.max).then_inc(s_phi, 1)

            def reciprocals(g):
                dve.wait_ge(s_denT, g + 1)
                for odd in range(2):
                    dve.tensor_scalar(den[:, :, odd::2, 0],
                                      bank[4 + odd][:, 384:384 + 2 * GT].rearrange("p (t c) -> p t c", t=GT),
                                      1e-6, None, ALU.max).then_inc(s_den, 1)
                dve.wait_ge(s_den, 2 * g + 2)
                dve.reciprocal(rec[:, :, :, 0], den[:, :, :, 0]).then_inc(s_rec, 1)
                dve.wait_ge(s_rec, g + 1)
                dve.tensor_copy(recB[:, :, :, :], rec[:, :, :, :].to_broadcast([P, GT, HEADS, HD])).then_inc(s_recB, 1)

            def divide(g):
                for hd in range(HEADS):
                    if hd % 2 == 0:
                        dve.wait_ge(s_recT, 2 * g + hd // 2 + 1)
                    r = slice(0, HD) if hd % 2 == 0 else slice(HD, P)
                    dve.tensor_tensor(oT[r, hd // 2, :], bank[4 + hd // 2][r, :], numden[r, hd, :],
                                      ALU.mult).then_inc(s_nrm, 1)

            def residual(g):
                for t in range(GT):
                    dve.wait_ge(s_wo, 2 * g + t // 2 + 1)
                    b = bank[2 + t // 2]
                    dve.scalar_tensor_tensor(out=gt[:, t, :], in0=gt[:, t, :], scalar=1.0,
                                             in1=b[:, (t % 2) * D:(t % 2 + 1) * D], op0=ALU.add,
                                             op1=ALU.mult).then_inc(s_wog, 1)
                for t in range(GT):
                    hh = tile_of(h, g, t)
                    dve.wait_ge(s_wog, 4 * g + t + 1)
                    dve.scalar_tensor_tensor(out=hh, in0=gt[:, t:t + 1, :], scalar=0.5, in1=hh, op0=ALU.mult,
                                             op1=ALU.add).then_inc(s_res, 1)

            def attention(g, before, more):
                if more:
                    dve.wait_ge(s_win, 16 * g + 16)
                    make_onehot(g + 1)
                features(g)
                if before:
                    divide(g - 1)
                    residual(g - 1)
                if more:
                    wait_apart(dve, s_emb, GT * (g + 2))
                    statistics(0, g + 1, lambda t: emb[:, t, :], 1e-12)
                if before:
                    wait_apart(dve, s_res, GT * g)
                    statistics(2, g - 1, lambda t: tile_of(h, g - 1, t)[:, 0, :], 1e-5)
                if more:
                    embedding_norm(g + 1, 0)
                    statistics(1, g + 1, lambda t: tile_of(h, g + 1, t)[:, 0, :], 1e-5)
                    normed(g + 1)
                    low(g + 1)
                reciprocals(g)

            dve.wait_ge(s_win0, 16)
            dve.wait_ge(s_small, 80)
            make_onehot(0)
            dve.tensor_copy(cwr[:, :], cw[:, :]).then_inc(s_cwr, 1)
            dve.wait_ge(s_cwr, 1)
            dve.tensor_tensor(cwr[WIN_LO:UROWS, :], cw[WIN_LO:UROWS, :], cwr[WIN_LO:UROWS, :].bitcast(F32),
                              ALU.subtract).then_inc(s_cwr, 1)
            dve.wait_ge(s_emb, GT)
            statistics(0, 0, lambda t: emb[:, t, :], 1e-12)
            embedding_norm(0, 0)
            statistics(1, 0, lambda t: tile_of(h, 0, t)[:, 0, :], 1e-5)
            dve.wait_ge(s_whi, 1)
            dve.tensor_tensor(wqk[:, 1::2, :], raw_qk[:, :, :], wqk[:, 0::2, :].bitcast(F32),
                              ALU.subtract).then_inc(s_wlo, 1)
            normed(0)
            low(0)
            dve.wait_ge(s_const, 5)
            attention(0, False, True)
            with dve.Fori(1, GROUPS - 1) as g:
                attention(g, True, True)
            attention(GROUPS - 1, True, False)
            divide(GROUPS - 1)
            residual(GROUPS - 1)
            dve.wait_ge(s_res, GT * GROUPS)
            statistics(2, GROUPS - 1, lambda t: tile_of(h, GROUPS - 1, t)[:, 0, :], 1e-5)

            def normed3(g):
                dve.wait_ge(s_mean, g + 1)
                dve.wait_ge(s_rs[2], g + 1)
                for t in range(GT * g, GT * g + GT):
                    dve.tensor_scalar(x3[:, t, :], h[:, t, :], mean3[:, t:t + 1], rstd3[:, t:t + 1], ALU.subtract,
                                      ALU.mult).then_inc(s_x3, 1)

            def low3(g):
                dve.wait_ge(s_hi3, 2 * g + 2)
                tok = slice(g * GN, (g + 1) * GN)
                dve.tensor_tensor(x3t[:, 1, tok], bank[0][:, :], x3t[:, 0, tok].bitcast(F32),
                                  ALU.subtract).then_inc(s_lo3, 1)
                dve.tensor_tensor(x3t[D1:P, 2, tok], bank[1][0:D1, :], x3t[0:D1, 2, tok].bitcast(F32),
                                  ALU.subtract).then_inc(s_lo3, 1)

            def logits(g):
                dve.wait_ge(s_lg, g + 1)
                dve.tensor_copy(lg[:, g * GT:(g + 1) * GT, :],
                                bank[4][:, 0:GT * ROUTER].rearrange("p (t c) -> p t c", t=GT)[:, :, 0:EXPERTS + 1]
                                ).then_inc(s_lgv, 1)

            for g in range(GROUPS):
                normed3(g)
            dve.wait_ge(s_wr, 2)
            dve.tensor_tensor(wr[:, 1::2, :], raw_r[:, :, :], wr[:, 0::2, :].bitcast(F32), ALU.subtract).then_inc(s_wr, 1)
            for g in range(GROUPS):
                low3(g)
                if g >= 1:
                    logits(g - 1)
            logits(GROUPS - 1)

            chain = [0]

            def step(ins):
                chain[0] += 1
                ins.then_inc(s_r, 1)
                dve.wait_ge(s_r, chain[0])

            def shared_hidden(g, m):
                dve.wait_ge(s_sg, HTILES * g + m + 1)
                dve.tensor_tensor(hid[:, m, :], bank[3 + 2 * (m % 2)][:, :], sg[:, m % 2, :],
                                  ALU.mult).then_inc(s_hid, 1)

            all3 = [P, TILES, EXPERTS]

            def choose(k):
                step(dve.tensor_reduce(best[:, k, :, 0], prob[:, :, :], AX.X, ALU.max))
                step(dve.tensor_tensor(tmp[:, :, :], prob[:, :, :], best[:, k, :, :].to_broadcast(all3), ALU.is_equal))
                step(dve.tensor_tensor(tmp[:, :, :], tmp[:, :, :], desc.unsqueeze(1).to_broadcast(all3), ALU.mult))
                step(dve.tensor_reduce(tmp2[:, :, 0], tmp[:, :, :], AX.X, ALU.max))
                step(dve.tensor_tensor(pick[:, k, :, :], tmp[:, :, :], tmp2[:, :, 0:1].to_broadcast(all3), ALU.is_equal))

            dve.wait_ge(s_lgv, GROUPS)
            step(dve.tensor_reduce(best[:, 0, :, 0], lg[:, :, 0:EXPERTS], AX.X, ALU.max))
            dve.tensor_tensor(tmp[:, :, :], lg[:, :, 0:EXPERTS], best[:, 0, :, :].to_broadcast(all3),
                              ALU.subtract).then_inc(s_diff, 1)
            step(dve.memset(run[:, :, :, :], 0.0))
            step(dve.memset(ends[:, :, :], 0.0))
            dve.wait_ge(s_exp, 2)
            step(dve.tensor_reduce(best[:, 0, :, 0], prob[:, :, :], AX.X, ALU.add))
            step(dve.reciprocal(best[:, 1, :, 0], best[:, 0, :, 0]))
            step(dve.tensor_tensor(prob[:, :, :], prob[:, :, :], best[:, 1, :, :].to_broadcast(all3), ALU.mult))
            choose(0)
            step(dve.scalar_tensor_tensor(out=prob[:, :, :], in0=pick[:, 0, :, :], scalar=-2.0, in1=prob[:, :, :],
                                          op0=ALU.mult, op1=ALU.add))
            choose(1)
            dve.tensor_tensor(taken[:, :, :], pick[:, 0, :, :], pick[:, 1, :, :], ALU.add).then_inc(s_taken, 1)
            step(dve.tensor_scalar(alpha[:, 0, :], one[:, :, 0], 0.5, 0.5, ALU.mult, ALU.add))
            step(dve.tensor_scalar(alpha[:, 1, :], alpha[:, 0, :], -1.0, 1.0, ALU.mult, ALU.add))
            step(dve.tensor_tensor(tmp2[:, :, 1], best[:, 0, :, 0], best[:, 1, :, 0], ALU.add))
            step(dve.reciprocal(tmp2[:, :, 2], tmp2[:, :, 1]))
            step(dve.tensor_tensor(tmp2[:, :, 3], tmp2[:, :, 2], alpha[:, 1, :], ALU.mult))
            for k in range(2):
                step(dve.tensor_tensor(gates[:, k, :], best[:, k, :, 0], tmp2[:, :, 3], ALU.mult))
            shared_hidden(0, 0)
            shared_hidden(0, 1)
            dve.wait_ge(s_cnt, 1)
            step(dve.tensor_copy(run[:, 0, EXPERTS:, :], bank[0][:, P:2 * P].rearrange("p (t e) -> p t e", t=TILES)))
            for n, d in enumerate((1, 2, 4, 8)):
                a, b = n % 2, 1 - n % 2
                step(dve.tensor_tensor(run[:, b, EXPERTS:, :], run[:, a, EXPERTS:, :],
                                       run[:, a, EXPERTS - d:EXPERTS - d + TILES, :], ALU.add))
            total = run[:, 0, EXPERTS + TILES - 1, :]
            shared_hidden(0, 2)
            wide3 = [P, EXPERTS, TILES]
            step(dve.tensor_tensor(wide[:, :, :], total.unsqueeze(2).to_broadcast(wide3),
                                   steps.unsqueeze(1).to_broadcast(wide3), ALU.is_gt))
            step(dve.tensor_reduce(ends[:, 0, 4:], wide[:, :, :], AX.X, ALU.add))
            for n, d in enumerate((1, 2, 4)):
                a, b = n % 2, 1 - n % 2
                step(dve.tensor_tensor(ends[:, b, 4:], ends[:, a, 4:], ends[:, a, 4 - d:4 - d + EXPERTS], ALU.add))
            shared_hidden(0, 3)
            step(dve.scalar_tensor_tensor(out=tmp[:, :, :], in0=ends[:, 1, 3:3 + EXPERTS].unsqueeze(1).to_broadcast(all3),
                                          scalar=float(P), in1=run[:, 0, EXPERTS - 1:EXPERTS - 1 + TILES, :],
                                          op0=ALU.mult, op1=ALU.add))
            step(dve.tensor_tensor(tmp[:, :, :], bank[0][:, 0:P].rearrange("p (t e) -> p t e", t=TILES), tmp[:, :, :],
                                   ALU.add))
            for k in range(2):
                step(dve.tensor_tensor(tmp2[:, :, :], tmp[:, :, :], pick[:, k, :, :], ALU.mult))
                step(dve.tensor_reduce(pos_f[:, k, :], tmp2[:, :, :], AX.X, ALU.add))
            dve.tensor_copy(pos[:, :, :], pos_f[:, :, :]).then_inc(s_pos, 1)
            shared_hidden(0, 4)
            slot3 = [1, SLOTS, EXPERTS]
            step(dve.tensor_tensor(at_slot[:, :, :], slot_no[0:1, :].unsqueeze(2).to_broadcast(slot3),
                                   ends[0:1, 1, 4:].unsqueeze(1).to_broadcast(slot3), ALU.is_ge))
            step(dve.tensor_reduce(expert_f[:, :, 0], at_slot[:, :, :], AX.X, ALU.add))
            dve.tensor_scalar(expert[:, :], expert_f[:, :, 0], float(EXPERTS - 1), None, ALU.min).then_inc(s_eid, 1)
            shared_hidden(0, 5)

            def add_shared(g):
                for t in range(GT):
                    if t % 2 == 0:
                        dve.wait_ge(s_sdn, 2 * g + t // 2 + 1)
                    n = GT * g + t
                    dve.scalar_tensor_tensor(out=h[:, n, :], in0=bank[6 + t // 2][:, (t % 2) * D:(t % 2 + 1) * D],
                                             scalar=alpha[:, 0, n:n + 1], in1=h[:, n, :], op0=ALU.mult,
                                             op1=ALU.add).then_inc(s_shr, 1)

            add_shared(0)
            for m in range(HTILES):
                shared_hidden(1, m)
            add_shared(1)
            for m in range(2):
                shared_hidden(2, m)

            def low_rows(i):
                dve.wait_ge(s_xhi, 2 * i + 2)
                dve.tensor_tensor(xst[:, 1, :], bank[0][:, 0:LANES * P], xst[:, 0, :].bitcast(F32),
                                  ALU.subtract).then_inc(s_xlo, 1)
                dve.tensor_tensor(xst[D1:P, 2, :], bank[1][0:D1, 0:LANES * P], xst[0:D1, 2, :].bitcast(F32),
                                  ALU.subtract).then_inc(s_xlo, 1)

            def round_(i, more):
                for j in range(LANES):
                    dve.wait_ge(s_si, LANES * i + j + 1)
                    dve.tensor_tensor(hs[:, j, :], bank[2 + j][:, HID:2 * HID], sgs[:, j, :],
                                      ALU.mult).then_inc(s_hs, 1)
                if more:
                    low_rows(i + 1)

            low_rows(0)
            with dve.Fori(0, ROUNDS - 1) as i:
                round_(i, True)
            round_(ROUNDS - 1, False)

            def add_routed(t):
                dve.wait_ge(s_back[t], 32)
                for k in range(2):
                    if k:
                        dve.wait_ge(s_sum, 2 * t + 1)
                    dve.scalar_tensor_tensor(out=h[:, t, :], in0=back[k][:, t, :], scalar=gates[:, k, t:t + 1],
                                             in1=h[:, t, :], op0=ALU.mult, op1=ALU.add).then_inc(s_sum, 1)

            added = 0
            for g, m, upto in [(2, 2, 0), (2, 3, 0), (2, 4, 1), (2, 5, 4)] + \
                    [(3, m, n) for m, n in enumerate((6, 8, 10, 11, 13, TILES))]:
                shared_hidden(g, m)
                for t in range(added, upto):
                    add_routed(t)
                added = upto
                if m == HTILES - 1:
                    if g == GROUPS - 1:
                        dve.wait_ge(s_sum, 2 * TILES)
                    add_shared(g)


        @block.tensor
        def _(pe):
            def embed(g):
                pe.wait_ge(s_oh, g + 1)
                wait(pe, s_lo, 2 * g)
                for t in range(GT):
                    mm = pe.matmul(bank[t // 2][:, (t % 2) * D:(t % 2 + 1) * D], onehot[:, t * P:(t + 1) * P],
                                   cwr[:, :], start=True, stop=True)
                    if t % 2:
                        mm.then_inc(s_conv, 1)

            def transposes(g):
                pe.wait_ge(s_xn, GT * g + GT)
                for t in range(GT):
                    pe.transpose(bank[0][:, t * P:(t + 1) * P], xn[:, t, 0:P], ident[:, :])
                for t in range(GT):
                    mm = pe.transpose(bank[1][0:D1, t * P:(t + 1) * P], xn[:, t, P:D], ident[:, :])
                mm.then_inc(s_T, 1)

            def scores(g, n):
                hd, b = n // 2, n % 2
                if n >= 2:
                    pe.wait_ge(s_ev, 8 * g + n - 1)
                if n % 4 == 0:
                    pe.wait_ge(s_phi, 6 * g + (3 if n == 0 else 6))
                for kt in range(2):
                    o = b * S + kt * P
                    mm = pe.matmul(bank[4 + n % 2][:, kt * S:kt * S + S - kt * P], kphi[:, hd // 2, o:o + P],
                                   qz[:, hd, o:b * S + S], start=True, stop=True)
                mm.then_inc(s_sc, 1)

            def weighted(g, n):
                hd, b = n // 2, n % 2
                if b == 0:
                    wait(pe, s_nd, 4 * g + hd - 1)
                pe.wait_ge(s_mask, 8 * g + n + 1)
                for kt in range(2):
                    mm = pe.matmul(bank[6 + hd % 2][:, b * S + kt * P:b * S + S], vp[:, 2 * b + kt, hd, :],
                                   sT[:, n % 4, kt * S:kt * S + S - kt * P], start=kt == 0, stop=kt == 1)
                mm.then_inc(s_pv, 1)

            def denominators(g):
                for hd in range(HEADS):
                    wait_apart(pe, s_nd, 4 * g + hd + 1)
                    r = HD if hd % 2 == 0 else 0
                    for t in range(GT):
                        c = 384 + 2 * t + hd // 2
                        mm = pe.transpose(bank[4 + hd % 2][:, c:c + 1], numden[r:r + 1, hd, t * P:(t + 1) * P],
                                          ident[r:r + 1, r:r + 1])
                mm.then_inc(s_denT, 1)

            def spread(g):
                pe.wait_ge(s_recB, g + 1)
                for pair in range(2):
                    for t in range(GT):
                        mm = pe.transpose(bank[4 + pair][:, t * P:(t + 1) * P],
                                          recB[:, t, 2 * pair:2 * pair + 2, :].rearrange("p h c -> p (h c)"), ident[:, :])
                    mm.then_inc(s_recT, 1)

            def keys_queries(g):
                pe.wait_ge(s_lo, 2 * g + 2)
                for m in range(4):
                    if m < 2:
                        wait(pe, s_vg, 12 * g - 3 + 3 * m)
                    else:
                        pe.wait_ge(s_act, 8 * g + 2 * m - 2)
                    for k, (x, w) in enumerate(pieces(xt, wqk, slice(m * P, (m + 1) * P), slice(0, GN))):
                        mm = pe.matmul(bank[2 + m % 2][:, :], w, x, start=k == 0, stop=k == 4)
                    mm.then_inc(s_proj, 1)

            def values_gates(g):
                for t in range(GT):
                    if t < 2:
                        pe.wait_ge(s_act, 8 * g + 6 + 2 * t)
                        wait(pe, s_wog, 4 * g - 4 + 2 * t + 2 if not isinstance(g, int) or g else 0)
                    else:
                        pe.wait_ge(s_vg, 12 * g + 3 * t - 3)
                    for k, (x, w) in enumerate(pieces(xt, wvg, slice(0, 448), slice(t * P, (t + 1) * P))):
                        mm = pe.matmul(bank[2 + t % 2][:, 0:448], x, w, start=k == 0, stop=k == 4)
                    mm.then_inc(s_proj, 1)

            def output(g, last):
                pe.wait_ge(s_nrm, 4 * g + 4)
                for t in range(GT):
                    if t % 2 == 0 and not last:
                        pe.wait_ge(s_act, 8 * g + 8 + 6 + t)
                    for k in range(2):
                        mm = pe.matmul(bank[2 + t // 2][:, (t % 2) * D:(t % 2 + 1) * D], oT[:, k, t * P:(t + 1) * P],
                                       wo[:, k, :], start=k == 0, stop=k == 1)
                    if t % 2:
                        mm.then_inc(s_wo, 1)

            def attention(g, before, more):
                keys_queries(g)
                if more:
                    embed(g + 1)
                if before:
                    spread(g - 1)
                    output(g - 1, False)
                values_gates(g)
                for n in range(8):
                    scores(g, n)
                    if n == 6 and more:
                        transposes(g + 1)
                    if n >= 2:
                        if n == 2:
                            pe.wait_ge(s_vg, 12 * g + 12)
                        weighted(g, n - 2)
                weighted(g, 6)
                weighted(g, 7)
                denominators(g)

            pe.wait_ge(s_cwr, 2)
            embed(0)
            pe.wait_ge(s_idn, 32)
            transposes(0)
            pe.wait_ge(s_wlo, 2)
            pe.wait_ge(s_const, 5)
            attention(0, False, True)
            with pe.Fori(1, GROUPS - 1) as g:
                attention(g, True, True)
            attention(GROUPS - 1, True, False)
            spread(GROUPS - 1)
            output(GROUPS - 1, True)

            def transposes3(g):
                pe.wait_ge(s_x3, GT * g + GT)
                wait(pe, s_lo3, 2 * g)
                for t in range(GT):
                    pe.transpose(bank[0][:, t * P:(t + 1) * P], x3[:, g * GT + t, 0:P], ident[:, :])
                for t in range(GT):
                    mm = pe.transpose(bank[1][0:D1, t * P:(t + 1) * P], x3[:, g * GT + t, P:D], ident[:, :])
                mm.then_inc(s_T3, 1)

            def router(g):
                pe.wait_ge(s_lo3, 2 * g + 2)
                if g >= 2:
                    pe.wait_ge(s_lgc, g - 1)
                for k, (x, w) in enumerate(pieces(x3t, wr, slice(0, ROUTER), slice(g * GN, (g + 1) * GN))):
                    mm = pe.matmul(bank[2 + g % 2][0:ROUTER, :], w, x, start=k == 0, stop=k == 4)
                mm.then_inc(s_lgT, 1)

            def logits(g):
                pe.wait_ge(s_lgc, g + 1)
                wait(pe, s_lgv, g)
                for t in range(GT):
                    mm = pe.transpose(bank[4][:, t * ROUTER:(t + 1) * ROUTER], lgT[:, g % 2, t * P:(t + 1) * P],
                                      ident[0:ROUTER, 0:ROUTER])
                mm.then_inc(s_lg, 1)

            for g in range(GROUPS + 2):
                if g < GROUPS:
                    transposes3(g)
                if g == 1:
                    pe.wait_ge(s_wr, 3)
                if 1 <= g <= GROUPS:
                    router(g - 1)
                if g >= 2:
                    logits(g - 2)

            def counts():
                pe.wait_ge(s_taken, 1)
                m = taken[:, :, :].rearrange("p t e -> p (t e)")
                pe.matmul(bank[0][:, 0:P], below, m, start=True, stop=True)
                pe.matmul(bank[0][:, P:2 * P], ones[:, :], m, start=True, stop=True).then_inc(s_cnt, 1)

            def shared_up(g, m):
                if not isinstance(g, int) or g or m >= 2:
                    pe.wait_ge(s_hid, HTILES * g + m - 1)
                for k in range(2):
                    c = EXPERTS * CHUNK + k * SHARED + m * P
                    for n, (x, w) in enumerate(pieces(x3t, wgu, slice(c, c + P), bass.ds(g * GN, GN))):
                        mm = pe.matmul(bank[2 + 2 * (m % 2) + k][:, :], w, x, start=n == 0, stop=n == 4)
                mm.then_inc(s_sgu, 1)

            def shared_down(g):
                pe.wait_ge(s_hid, HTILES * g + HTILES)
                wait(pe, s_shr, GT * g)
                for t in range(GT):
                    for m in range(HTILES):
                        mm = pe.matmul(bank[6 + t // 2][:, (t % 2) * D:(t % 2 + 1) * D], hid[:, m, t * P:(t + 1) * P],
                                       wsdn[:, m, :], start=m == 0, stop=m == HTILES - 1)
                    if t % 2:
                        mm.then_inc(s_sdn, 1)

            pe.wait_ge(s_glo, CHUNKS)
            pe.wait_ge(s_lgv, GROUPS)
            for m in range(HTILES):
                shared_up(0, m)
                if m == 1:
                    counts()
            pe.wait_ge(s_wdn, 32)
            shared_down(0)
            for m in range(HTILES):
                shared_up(1, m)
            shared_down(1)
            for m in range(2):
                shared_up(2, m)

            def rows(i, odd, pair):
                for j in range(LANES):
                    pe.wait_ge(s_xl[odd * LANES + j], 16 * pair + 16)
                for j in range(LANES):
                    pe.transpose(bank[0][:, j * P:(j + 1) * P], xs[:, odd, j, 0:P], ident[:, :])
                for j in range(LANES):
                    mm = pe.transpose(bank[1][0:D1, j * P:(j + 1) * P], xs[:, odd, j, P:D], ident[:, :])
                mm.then_inc(s_xT, 1)

            def expert_of(i, j):
                return pe.value_load(expert[0:1, bass.ds(LANES * i + j, 1)], min_val=0, max_val=EXPERTS - 1)

            def up(i, j):
                e = expert_of(i, j)
                if j == 0:
                    pe.wait_ge(s_xlo, 2 * i + 2)
                if not isinstance(i, int) or i:
                    if j == 2:
                        pe.wait_ge(s_ys, LANES * (i - 1))
                for n, (x, w) in enumerate(pieces(xst, wgu, bass.ds(e * CHUNK, CHUNK), slice(j * P, (j + 1) * P))):
                    mm = pe.matmul(bank[2 + j][:, 0:CHUNK], x, w, start=n == 0, stop=n == 4)
                mm.then_inc(s_gu, 1)

            def turn(i):
                for j in range(LANES):
                    pe.wait_ge(s_hs, LANES * i + j + 1)
                    pe.transpose(bank[5][:, j * P:(j + 1) * P], hs[:, j, 0:P], ident[:, :])
                    mm = pe.transpose(bank[6][0:HID - P, j * P:(j + 1) * P], hs[:, j, P:HID], ident[:, :])
                mm.then_inc(s_hT, 1)

            def down(i, more):
                for j in range(LANES):
                    e = expert_of(i, j)
                    if j == 0:
                        pe.wait_ge(s_hTc, 2 * i + 2)
                    if j == 2 and more:
                        pe.wait_ge(s_hs, LANES * (i + 1) + 3)
                    for k, r in ((0, P), (1, HID - P)):
                        mm = pe.matmul(down_bank(j), hsT[0:r, k, j * P:(j + 1) * P],
                                       wdn[0:r, bass.ds(e, 1), k, :].rearrange("p a d -> p (a d)"), start=k == 0, stop=k == 1)
                    mm.then_inc(s_dn, 1)

            def round_(i, before, more, odd, pair):
                up(i, 0)
                up(i, 1)
                if more:
                    rows(i + 1, odd, pair)
                up(i, 2)
                if before:
                    down(i - 1, True)
                turn(i)

            pe.wait_ge(s_hid, 2 * HTILES + 2)
            pe.wait_ge(s_eid, 1)
            rows(0, 0, 0)
            round_(0, False, True, 1, 0)
            with pe.Fori(0, (ROUNDS - 3) // 2) as n:
                round_(2 * n + 1, True, True, 0, n + 1)
                round_(2 * n + 2, True, True, 1, n + 1)
            round_(ROUNDS - 2, True, True, 0, (ROUNDS - 1) // 2)
            round_(ROUNDS - 1, True, False, 0, 0)
            down(ROUNDS - 1, False)
            for g in (2, 3):
                for m in range(2 if g == 2 else 0, HTILES):
                    if (g, m) == (2, 3):
                        pe.wait_ge(s_ys, SLOTS)
                    shared_up(g, m)
                shared_down(g)


def lay_out(x, mask, W3, W5, W7, gamma, beta, Wq, Wk, Wv, Wo, Wg, router_w, w_gate, w_up, w_down, ws_gate,
            ws_up, ws_down, sg_w, sg_b):
    half = TAPS // 2
    padded = np.full((B, S + 2 * half), -1, x.dtype)
    padded[:, half:half + S] = x
    windows = np.stack([padded[:, k:k + S].reshape(-1) for k in range(TAPS) for _ in range(CLS)])
    conv = np.zeros((TAPS, CLS, D), W3.dtype)
    for n, w in enumerate((W3, W5, W7)):
        k = w.shape[2]
        conv[half - k // 2:half + k // 2 + 1, :, 64 * n:64 * n + 64] = w.transpose(2, 1, 0)
    classes = np.zeros((P, 1), np.float32)
    for lo in (0, WIN_LO):
        classes[lo:lo + WIN, 0] = np.tile(np.arange(CLS), TAPS)

    def doubled(w, pad):
        return np.concatenate([w, np.full((WIN_LO - WIN, w.shape[1]), pad, w.dtype), w])

    def twice(w):
        return np.ascontiguousarray(np.stack([w[:P], np.concatenate([w[P:], w[P:]])], axis=1))

    qk = np.concatenate([Wk[:, :P], Wq[:, :P], Wk[:, P:], Wq[:, P:]], axis=1)
    vg = np.concatenate([Wv, Wg], axis=1)
    gu = np.concatenate([w_gate, w_up], axis=2).transpose(1, 0, 2).reshape(D, EXPERTS * CHUNK)
    gu = np.concatenate([gu, ws_gate, ws_up], axis=1)
    dn = np.zeros((P, EXPERTS, 2, D), w_down.dtype)
    dn[:, :, 0] = w_down[:, :P].transpose(1, 0, 2)
    dn[:HID - P, :, 1] = w_down[:, P:].transpose(1, 0, 2)
    router = np.zeros((D, ROUTER), router_w.dtype)
    router[:, :EXPERTS] = router_w
    router[:, EXPERTS:EXPERTS + 1] = sg_w
    counting = np.concatenate([np.triu(np.ones((P, P)), 1)] + [
        np.broadcast_to(row, (P, len(row))) for row in
        (np.arange(TILES) * P, np.arange(EXPERTS, 0, -1), np.arange(SLOTS))], axis=1).astype(np.float32)
    return {
        "windows": doubled(windows, -1), "classes": classes, "conv_w": doubled(conv.reshape(WIN, D), 0),
        "tok_mask": np.ascontiguousarray(mask.reshape(TILES, P).T),
        "gamma": np.ascontiguousarray(np.broadcast_to(gamma, (P, D))),
        "beta": np.ascontiguousarray(np.broadcast_to(beta, (P, D))),
        "w_qk": twice(qk), "w_vg": twice(vg),
        "w_o": np.ascontiguousarray(Wo.reshape(2, P, D).transpose(1, 0, 2)),
        "ident_in": np.eye(P, dtype=np.float32),
        "w_gu": np.ascontiguousarray(twice(gu).reshape(P, 2, CHUNKS, CHUNK).transpose(0, 2, 1, 3)),
        "w_dn": dn, "w_sdn": np.ascontiguousarray(ws_down.reshape(HTILES, P, D).transpose(1, 0, 2)),
        "w_router": twice(router), "gate_bias": np.ascontiguousarray(np.broadcast_to(sg_b, (P, 1))),
        "counting": counting,
    }

_ORDER = ["x", "mask_BS_f1_0", "L0_tok_W3", "L0_tok_W5", "L0_tok_W7", "L0_tok_ln_gamma", "L0_tok_ln_beta",
          "L0_attn_Wq", "L0_attn_Wk", "L0_attn_Wv", "L0_attn_Wo", "L0_attn_Wg", "L0_ffn_router_w",
          "L0_ffn_w_gate", "L0_ffn_w_up", "L0_ffn_w_down", "L0_ffn_ws_gate", "L0_ffn_ws_up", "L0_ffn_ws_down",
          "L0_ffn_sg_w", "L0_ffn_sg_b"]


def kernel(**inputs):
    import concourse.bacc as bacc
    from concourse.bass_utils import run_bass_kernel_spmd

    nc = bacc.Bacc("TRN2", target_bir_lowering=False, num_devices=1)
    arrays = lay_out(*[np.asarray(inputs[name]) for name in _ORDER])
    args = [nc.dram_tensor(f"{name}_dram", a.shape, mybir.dt.from_np(a.dtype), kind="ExternalInput").ap()
            for name, a in arrays.items()]
    out = nc.dram_tensor("out_dram", (P, TILES * D), F32, kind="ExternalOutput").ap()
    tower(nc, *args, out)
    result = run_bass_kernel_spmd(nc, [{f"{name}_dram": a for name, a in arrays.items()}], core_ids=[0])
    y = result.results[0]["out_dram"].reshape(P, TILES, D).transpose(1, 0, 2)
    return np.ascontiguousarray(y).reshape(B, S, D)
```

```python
from contextlib import ExitStack

import concourse.bass as bass
import numpy as np
from concourse import mybir

F32 = mybir.dt.float32
F32R = mybir.dt.float32r
I32 = mybir.dt.int32
U32 = mybir.dt.uint32
ALU = mybir.AluOpType
AX = mybir.AxisListType
ACT = mybir.ActivationFunctionType

P = 128
B, S, D = 8, 256, 192
TILES = B * S // P
GROUPS = 4
GT = TILES // GROUPS
GN = GT * P
HALF = TILES // 2
D1 = D - P
HEADS, HD = 4, 64
TAPS, CLS = 7, 5
WIN = TAPS * CLS
EXPERTS, HID = 8, 192
SLOTS = 2 * TILES + EXPERTS - 1
LANES = 3
ROUNDS = SLOTS // LANES
SHARED = 768
WARM = 12
SECOND = (4, 5)
HTILES = SHARED // P
CHUNK = 2 * HID
CHUNKS = EXPERTS + 2 * SHARED // CHUNK
ROUTER = 32
WIN_LO = 64
UROWS = WIN_LO + WIN


def pieces(xt, blocks, cols, tok):
    for a, b in ((0, 0), (0, 1), (1, 0), (2, 2), (2, 3)):
        yield xt[:, a, tok], blocks[:, b, cols]


def tower(nc, windows, classes, conv_w, tok_mask, gamma, beta, w_qk, w_vg, w_o, ident_in, w_gu, w_dn, w_sdn,
          w_router, gate_bias, counting, out):
    ctx = ExitStack()
    with ctx:
        def sb(name, shape, dt=F32):
            return ctx.enter_context(nc.sbuf_tensor(name, shape, dt))

        def sem(name):
            return ctx.enter_context(nc.semaphore(name))

        sorted_x = nc.dram_tensor("sorted_x", [SLOTS * P, D + 1], F32, kind="Internal").ap()
        routed = nc.dram_tensor("routed", [1 + 2 * TILES * P + 2 * LANES * P, D], F32, kind="Internal").ap()
        bank = [ctx.enter_context(nc.psum_tensor(f"bank{i}", [P, 512], F32)) for i in range(8)]

        h = sb("h", [P, TILES, D])
        ident = sb("ident", [P, P])
        stat = sb("stat", [P, 3, GT, 6])
        mv = sb("mv", [P, 3, GT, 2])
        var_eps = sb("var_eps", [P, 2, GT])
        var_eps3 = sb("var_eps3", [P, TILES])
        rstd = sb("rstd", [P, 2, GT])
        mean3 = sb("mean3", [P, TILES])
        rstd3 = sb("rstd3", [P, TILES])
        half_neg = sb("half_neg", [P, GT])
        zero = sb("zero", [P, D + 1])
        wgu = sb("wgu", [P, 4, CHUNKS * CHUNK], F32R)
        stage = sb("stage", [P, LANES, 2, CHUNK])
        count = sb("count", [P, P + 2 * TILES + EXPERTS + SLOTS + 2 * LANES])
        below, steps = count[:, 0:P], count[:, P:P + TILES]
        desc, slot_no = count[:, P + TILES:P + TILES + EXPERTS], \
            count[:, P + TILES + EXPERTS:P + TILES + EXPERTS + SLOTS]
        token_no = count[:, P + TILES + EXPERTS + SLOTS:P + 2 * TILES + EXPERTS + SLOTS]
        spare = count[:, P + 2 * TILES + EXPERTS + SLOTS:]
        ones = sb("ones", [P, P])
        raw_r = sb("raw_r", [P, 2, ROUTER])
        wr = sb("wr", [P, 4, ROUTER], F32R)
        gb = sb("gb", [P, 1])
        half_gb = sb("half_gb", [P, 1])

        lgT = sb("lgT", [ROUTER, 2, GN])
        lg = sb("lg", [P, TILES, EXPERTS + 1])
        cls = sb("cls", [P, 1])
        msk = sb("msk", [P, TILES])

        early = ExitStack()

        def sa(name, shape, dt=F32):
            return early.enter_context(nc.sbuf_tensor(name, shape, dt))

        ids = sa("ids", [UROWS, 2, GN], I32)
        onehot = sa("onehot", [UROWS, GN], F32R)
        cw = sa("cw", [UROWS, D])
        cwr = sa("cwr", [UROWS, D], F32R)
        gam = sa("gam", [P, D])
        bet = sa("bet", [P, D])
        emb = sa("emb", [P, GT, D])
        xn = sa("xn", [P, GT, D])
        xt = sa("xt", [P, 3, GN], F32R)
        wqk = sa("wqk", [P, 4, 512], F32R)
        wvg = sa("wvg", [P, 4, 448], F32R)
        raw_flat = stage[:, :, :, :].rearrange("p a b c -> p (a b c)")
        raw_qk = raw_flat[:, 0:1024].rearrange("p (k n) -> p k n", k=2)
        raw_vg = raw_flat[:, 1024:1920].rearrange("p (k n) -> p k n", k=2)
        kphi = sa("kphi", [P, 2, GN])
        qz = sa("qz", [P, HEADS, GN])
        xp1 = sa("xp1", [P, 2, GN])
        ex = sa("ex", [P, 2, GN])
        vp = sa("vp", [P, GT, HEADS, P])
        sT = sa("sT", [P, 4, 384])
        wo = sa("wo", [P, 2, D])
        gt = sa("gt", [P, 2, GT, D])
        numden = sa("numden", [P, HEADS, GN])
        den = sa("den", [P, GT, HEADS, 1])
        rec = sa("rec", [P, GT, HEADS, 1])
        recB = sa("recB", [P, GT, HEADS, HD])
        oT = sa("oT", [P, 2, GN])
        early.close()

        x3 = sb("x3", [P, TILES, D + 1])
        x3t = sb("x3t", [P, 3, B * S], F32R)
        hid = sb("hid", [P, HTILES, GN])
        sg = sb("sg", [P, 2, GN])
        wdn = sb("wdn", [P, EXPERTS, 2, D])
        wsdn = sb("wsdn", [P, HTILES, D])
        prob = sb("prob", [P, TILES, EXPERTS])
        pick = sb("pick", [P, 2, TILES, EXPERTS])
        best = sb("best", [P, 2, TILES, 1])
        gates = sb("gates", [P, 2, TILES])
        tmp = sb("tmp", [P, TILES, EXPERTS])
        tmp2 = sb("tmp2", [P, TILES, EXPERTS])
        one = sb("one", [P, TILES, 1])
        alpha = sb("alpha", [P, 2, TILES])
        taken = sb("taken", [P, TILES, EXPERTS])
        run = sb("run", [P, 2, EXPERTS + TILES, EXPERTS])
        wide = sb("wide", [P, EXPERTS, TILES])
        ends = sb("ends", [P, 3, 4 + EXPERTS])
        at_slot = sb("at_slot", [1, SLOTS, EXPERTS])
        expert_f = sb("expert_f", [1, SLOTS, 1])
        expert = sb("expert", [1, SLOTS], I32)
        pos_f = sb("pos_f", [P, 2, TILES])
        pos = sb("pos", [P, 2, TILES], I32)
        xs = sb("xs", [P, 2, LANES, D + 1])
        pad = sb("pad", [P, LANES])
        dest_f = sb("dest_f", [P, 2, LANES])
        dest = sb("dest", [P, 2, LANES], I32)
        xst = sb("xst", [P, 3, LANES * P], F32R)
        sgs = sb("sgs", [P, LANES, HID])
        hs = sb("hs", [P, LANES, HID])
        hsT = sb("hsT", [P, 2, LANES * P])
        ys = sb("ys", [P, 2, LANES, D])
        back = [wgu[:, k, 0:TILES * D].bitcast(F32).rearrange("p (t d) -> p t d", d=D) for k in range(2)]

        s_win0 = sem("s_win0")
        s_win = sem("s_win")
        s_cls = sem("s_cls")
        s_cw = sem("s_cw")
        s_msk = sem("s_msk")
        s_gb = sem("s_gb")
        s_aw = sem("s_aw")
        s_idn = sem("s_idn")
        s_const = sem("s_const")
        s_passed = sem("s_passed")
        s_mean = sem("s_mean")
        s_oh = sem("s_oh")
        s_cwr = sem("s_cwr")
        s_whi = sem("s_whi")
        s_wlo = sem("s_wlo")
        s_conv = sem("s_conv")
        s_emb = sem("s_emb")
        s_bn = [sem(f"s_bn{k}") for k in range(3)]
        s_mv = [sem(f"s_mv{k}") for k in range(3)]
        s_ve = [sem(f"s_ve{k}") for k in range(3)]
        s_rs = [sem(f"s_rs{k}") for k in range(3)]
        s_gam = sem("s_gam")
        s_h0 = sem("s_h0")
        s_xn = sem("s_xn")
        s_T = sem("s_T")
        s_hi = sem("s_hi")
        s_lo = sem("s_lo")
        s_proj = sem("s_proj")
        s_act = sem("s_act")
        s_phi = sem("s_phi")
        s_vg = sem("s_vg")
        s_sc = sem("s_sc")
        s_ev = sem("s_ev")
        s_mask = sem("s_mask")
        s_pv = sem("s_pv")
        s_nd = sem("s_nd")
        s_denT = sem("s_denT")
        s_den = sem("s_den")
        s_rec = sem("s_rec")
        s_recB = sem("s_recB")
        s_recT = sem("s_recT")
        s_nrm = sem("s_nrm")
        s_wo = sem("s_wo")
        s_wog = sem("s_wog")
        s_res = sem("s_res")
        s_zx = sem("s_zx")
        s_wst = [sem(f"s_wst{j}") for j in range(LANES)]
        s_ghi = sem("s_ghi")
        s_glo = sem("s_glo")
        s_cst = sem("s_cst")
        s_wr = sem("s_wr")
        s_wsdn = sem("s_wsdn")
        s_wdn = sem("s_wdn")
        s_x3 = sem("s_x3")
        s_T3 = sem("s_T3")
        s_hi3 = sem("s_hi3")
        s_lo3 = sem("s_lo3")
        s_lgT = sem("s_lgT")
        s_lgc = sem("s_lgc")
        s_lg = sem("s_lg")
        s_lgv = sem("s_lgv")
        s_clear = sem("s_clear")
        s_r = sem("s_r")
        s_diff = sem("s_diff")
        s_exp = sem("s_exp")
        s_taken = sem("s_taken")
        s_cnt = sem("s_cnt")
        s_pos = sem("s_pos")
        s_eid = sem("s_eid")
        s_scat = [[sem(f"s_scat{k}{half}") for half in range(2)] for k in range(2)]
        s_no = sem("s_no")
        s_pad = sem("s_pad")
        s_kept = sem("s_kept")
        s_dest = sem("s_dest")
        s_sgu = sem("s_sgu")
        s_sg = sem("s_sg")
        s_hid = sem("s_hid")
        s_sdn = sem("s_sdn")
        s_shr = sem("s_shr")
        s_xl = [sem(f"s_xl{j}") for j in range(2 * LANES)]
        s_xT = sem("s_xT")
        s_xhi = sem("s_xhi")
        s_xlo = sem("s_xlo")
        s_gu = sem("s_gu")
        s_si = sem("s_si")
        s_hs = sem("s_hs")
        s_hT = sem("s_hT")
        s_hTc = sem("s_hTc")
        s_dn = sem("s_dn")
        s_ys = sem("s_ys")
        s_st = [sem(f"s_st{odd}") for odd in range(2)]
        s_back = [sem(f"s_back{g}") for g in range(GROUPS)]
        s_sum = [sem(f"s_sum{k}") for k in range(2)]
        s_out = sem("s_out")

        def wait(eng, s, value):
            if not isinstance(value, int) or value > 0:
                eng.wait_ge(s, value)

        def wait_apart(eng, s, value):
            eng.wait_ge(s, value)
            eng.sem_inc(s_passed, 1)

        def down_bank(j):
            return bank[4][:, 0:D] if j == 2 else bank[7][:, j * D:(j + 1) * D]

        def gate_of(g, t):
            return gt[:, bass.ds(g % 2, 1), t, :]

        def tile_of(x, g, t):
            return x[:, bass.ds(g * GT + t, 1)]

        block = ctx.enter_context(nc.Block())

        @block.sync
        def _(sp):
            sp.dma_start(cls[:, :], classes).then_inc(s_cls, 16)
            sp.dma_start(ids[:, 0, :], windows[:, 0:GN]).then_inc(s_win0, 16)
            sp.dma_start(msk[:, :], tok_mask).then_inc(s_msk, 16)
            sp.dma_start(gam[:, :], gamma).then_inc(s_gb, 16)
            sp.dma_start(bet[:, :], beta).then_inc(s_gb, 16)
            sp.dma_start(ident[:, :], ident_in).then_inc(s_idn, 16)
            sp.dma_start(raw_qk, w_qk).then_inc(s_aw, 16)
            sp.dma_start(raw_vg, w_vg).then_inc(s_aw, 16)
            sp.dma_start(wo[:, :, :], w_o).then_inc(s_idn, 16)
            sp.dma_start(ids[:, 1, :], windows[:, GN:2 * GN]).then_inc(s_win, 16)
            sp.dma_start(count[:, :], counting).then_inc(s_cst, 16)
            sp.dma_start(raw_r[:, :, :], w_router).then_inc(s_cst, 16)
            sp.dma_start(gb[:, :], gate_bias).then_inc(s_cst, 16)
            sp.wait_ge(s_const, 1)
            sp.dma_start(sorted_x.rearrange("(s p) d -> p s d", p=P),
                         zero[:, :].unsqueeze(1).to_broadcast([P, SLOTS, D + 1])).then_inc(s_zx, 16)
            sp.wait_ge(s_wlo, 2)
            for g in range(GROUPS):
                if g in (1, 2):
                    sp.wait_ge(s_oh, g)
                    sp.wait_ge(s_win, 16 * g)
                    sp.dma_start(ids[:, (g + 1) % 2, :], windows[:, (g + 1) * GN:(g + 2) * GN]).then_inc(s_win, 16)
                for j in range(LANES):
                    if g:
                        sp.wait_ge(s_glo, LANES * (g - 1) + j + 1)
                    sp.dma_start(stage[:, j, :, :], w_gu[:, LANES * g + j, :, :]).then_inc(s_wst[j], 16)
            sp.wait_ge(s_pv, 8 * GROUPS)
            sp.dma_start(wsdn[:, :, :], w_sdn).then_inc(s_wsdn, 16)
            sp.dma_start(wdn[:, :, :, :], w_dn).then_inc(s_wdn, 16)

            def load(i, odd):
                for j in range(LANES):
                    sp.dma_start(xs[:, odd, j, :], sorted_x[bass.ds((i * LANES + j) * P, P), :]
                                 ).then_inc(s_xl[odd * LANES + j], 16)

            for k in range(2):
                for half in range(2):
                    sp.wait_ge(s_scat[k][half], 16 * HALF)
            load(0, 0)
            load(1, 1)
            sp.wait_ge(s_kept, 1)
            load(2, 0)
            with sp.Fori(0, (ROUNDS - 3) // 2) as n:
                for k in range(2):
                    sp.wait_ge(s_kept, 2 * n + k + 2)
                    load(2 * n + k + 3, 1 - k)
            for odd in range(2):
                sp.wait_ge(s_st[odd], 16 * LANES * ((ROUNDS + 1 - odd) // 2))
            for g in range(GROUPS):
                for k in range(2):
                    row = 1 + (k * GROUPS + g) * GN
                    sp.dma_start(back[k][:, g * GT:(g + 1) * GT, :],
                                 routed[row:row + GN, :].rearrange("(t p) d -> p t d", p=P)).then_inc(s_back[g], 16)
            for t in range(TILES):
                sp.wait_ge(s_sum[1], t + 1)
                sp.wait_ge(s_shr, t + 1 if t >= TILES - GT else (t // GT + 1) * GT)
                sp.dma_start(out[:, t * D:(t + 1) * D], h[:, t, :]).then_inc(s_out, 16)
            sp.wait_ge(s_out, 16 * TILES)

        @block.gpsimd
        def _(pool):
            pool.memset(zero[:, :], 0.0).then_inc(s_const, 1)
            pool.memset(half_neg[:, :], -0.5).then_inc(s_const, 1)
            pool.memset(qz[:, :, :], 0.0).then_inc(s_const, 1)

            def rsqrt(k, g):
                pool.wait_ge(s_ve[k], g + 1)
                out = rstd[:, k, :] if k < 2 else rstd3[:, bass.ds(g * GT, GT)]
                var = var_eps[:, k, :] if k < 2 else var_eps3[:, bass.ds(g * GT, GT)]
                pool.tensor_tensor(out, var, half_neg[:, :], ALU.pow).then_inc(s_rs[k], 1)

            def affine(g, n):
                wait_apart(pool, s_ev, 8 * g + n + 1)
                diag = sT[:, n % 4, :].rearrange("p (b q) -> p b q", q=P)[:, 0::2, :]
                pool.affine_select(out=diag, in_=diag, compare_op=ALU.is_ge, fill=0.0, base=0,
                                   pattern=[[0, 2], [1, P]], channel_multiplier=-1).then_inc(s_mask, 1)

            def low_chunk(g, j):
                pool.wait_ge(s_ghi, LANES * g + j + 1)
                at = bass.ds((LANES * g + j) * CHUNK, CHUNK)
                pool.tensor_tensor(wgu[:, 1::2, at], stage[:, j, :, :], wgu[:, 0::2, at].bitcast(F32),
                                   ALU.subtract).then_inc(s_glo, 1)

            def attention(g, before, more):
                if before:
                    for j in range(LANES):
                        low_chunk(g - 1, j)
                if more:
                    rsqrt(0, g + 1)
                if not more:
                    low_chunk(g, 0)
                for n in range(8):
                    affine(g, n)
                    if n == 3 and not more:
                        low_chunk(g, 1)
                    if n == 3 and more:
                        rsqrt(1, g + 1)
                    if n == 4 and not more:
                        rsqrt(2, g - 1)
                if before and more:
                    rsqrt(2, g - 1)

            pool.wait_ge(s_const, 2)
            rsqrt(0, 0)
            pool.memset(vp[:, :, :, :], 1.0).then_inc(s_const, 1)
            pool.memset(ones[:, :], 1.0).then_inc(s_const, 1)
            pool.wait_ge(s_whi, 2)
            pool.tensor_tensor(wvg[:, 1::2, :], raw_vg, wvg[:, 0::2, :].bitcast(F32), ALU.subtract).then_inc(s_wlo, 1)
            rsqrt(1, 0)
            attention(0, False, True)
            with pool.Fori(1, GROUPS - 1) as g:
                attention(g, True, True)
            attention(GROUPS - 1, True, False)
            low_chunk(GROUPS - 1, 2)
            rsqrt(2, GROUPS - 1)

            pool.wait_ge(s_zx, 16)
            for k in range(2):
                pool.wait_ge(s_pos, k + 1)
                for t in range(TILES):
                    half = t // HALF
                    if k == 0:
                        pool.wait_ge(s_no, 1)
                    elif t % HALF == 0:
                        pool.wait_ge(s_no, 2 + half)
                    pool.indirect_dma_start(out=sorted_x, out_offset=bass.IndirectOffsetOnAxis(
                        ap=pos[:, k, t:t + 1].bitcast(U32), axis=0), in_=x3[:, t, :], in_offset=None,
                        bounds_check=SLOTS * P - 1, oob_is_err=True).then_inc(s_scat[k][half], 16)

            def store(i, odd):
                wait_apart(pool, s_dest, i + 1)
                for j in range(LANES):
                    wait_apart(pool, s_ys, LANES * i + j + 1)
                    pool.indirect_dma_start(out=routed, out_offset=bass.IndirectOffsetOnAxis(
                        ap=dest[:, odd, j:j + 1].bitcast(U32), axis=0), in_=ys[:, odd, j, :], in_offset=None,
                        bounds_check=2 * (TILES + LANES) * P, oob_is_err=True).then_inc(s_st[odd], 16)

            with pool.Fori(0, ROUNDS // 2) as n:
                for k in range(2):
                    store(2 * n + k, k)
            store(ROUNDS - 1, 0)

        @block.scalar
        def _(act):
            act.dma_start(cw[:, :], conv_w).then_inc(s_cw, 16)
            act.wait_ge(s_const, 1)
            act.activation(rstd3[:, 0:1], zero[:, 0:1], ACT.Exp)

            def embed(g):
                for t in range(GT):
                    if t % 2 == 0:
                        act.wait_ge(s_conv, 2 * g + t // 2 + 1)
                    act.activation(emb[:, t, :], bank[t // 2][:, (t % 2) * D:(t % 2 + 1) * D], ACT.Copy,
                                   scale=msk[:, bass.ds(g * GT + t, 1)]).then_inc(s_emb, 1)

            def high(g):
                act.wait_ge(s_T, 2 * g + 1)
                act.activation(xt[:, 0, :], bank[0][:, :], ACT.Copy).then_inc(s_hi, 1)
                act.wait_ge(s_T, 2 * g + 2)
                act.activation(xt[0:D1, 2, :], bank[1][0:D1, :], ACT.Copy).then_inc(s_hi, 1)

            def feature_parts(g):
                for m in range(4):
                    act.wait_ge(s_proj, 8 * g + m + 1)
                    wait(act, s_phi, 6 * g + (-2, 0, 1, 3)[m])
                    act.activation(xp1[:, m % 2, :], bank[2 + m % 2][:, :], ACT.Copy, bias=1.0).then_inc(s_act, 1)
                    act.activation(ex[:, m % 2, :], bank[2 + m % 2][:, :], ACT.Exp).then_inc(s_act, 1)

            def values_gates(g):
                for t in range(GT):
                    act.wait_ge(s_proj, 8 * g + 5 + t)
                    b = bank[2 + t % 2]
                    v = vp[:, t, :, :].rearrange("p (a b) c -> p a (b c)", b=2)
                    for odd in range(2):
                        act.activation(v[:, :, 3 * HD * odd:3 * HD * odd + HD],
                                       b[:, 0:256].rearrange("p (a b c) -> p a b c", a=2, b=2)[:, :, odd, :],
                                       ACT.Copy).then_inc(s_vg, 1)
                    act.activation(gate_of(g, t)[:, 0, :], b[:, 256:448], ACT.Tanh, scale=0.5).then_inc(s_vg, 1)

            def high3(g):
                act.wait_ge(s_T3, 2 * g + 1)
                tok = slice(g * GN, (g + 1) * GN)
                act.activation(x3t[:, 0, tok], bank[0][:, :], ACT.Copy).then_inc(s_hi3, 1)
                act.wait_ge(s_T3, 2 * g + 2)
                act.activation(x3t[0:D1, 2, tok], bank[1][0:D1, :], ACT.Copy).then_inc(s_hi3, 1)

            def heads(g, more):
                for n in range(8):
                    act.wait_ge(s_sc, 8 * g + n + 1)
                    if n >= 4:
                        act.wait_ge(s_pv, 8 * g + n - 3)
                    act.activation(sT[:, n % 4, :], bank[4 + n % 2][:, 0:384], ACT.Copy).then_inc(s_ev, 1)
                    if n >= 3 and n % 2:
                        numerators(g, n // 2 - 1)
                    if n == 6 and more:
                        high(g + 1)
                    if n == 3 and not more:
                        high3(0)
                    if n in (1, 3, 5) and more or n == 1:
                        high_chunk(g, n // 2 if more else 2)
                    if n == 6 and not more:
                        high3(1)
                numerators(g, 3)
                if not more:
                    high3(2)

            def numerators(g, hd):
                act.wait_ge(s_pv, 8 * g + 2 * hd + 2)
                act.activation(numden[:, hd, :], bank[6 + hd % 2][:, :], ACT.Copy).then_inc(s_nd, 1)

            def high_chunk(g, j):
                act.wait_ge(s_wst[j], 16 * g + 16)
                act.activation(wgu[:, 0::2, bass.ds((LANES * g + j) * CHUNK, CHUNK)], stage[:, j, :, :],
                               ACT.Copy).then_inc(s_ghi, 1)

            def attention(g, more):
                feature_parts(g)
                if more:
                    embed(g + 1)
                values_gates(g)
                if not more:
                    high_chunk(g, 0)
                    high_chunk(g, 1)
                heads(g, more)

            act.wait_ge(s_msk, 16)
            embed(0)
            act.wait_ge(s_aw, 32)
            act.activation(wqk[:, 0::2, :], raw_qk[:, :, :], ACT.Copy).then_inc(s_whi, 1)
            act.activation(wvg[:, 0::2, :], raw_vg[:, :, :], ACT.Copy).then_inc(s_whi, 1)
            high(0)
            act.wait_ge(s_const, 5)
            attention(0, True)
            with act.Fori(1, GROUPS - 1) as g:
                attention(g, True)
            act.wait_ge(s_cst, 48)
            act.activation(wr[:, 0::2, :], raw_r[:, :, :], ACT.Copy).then_inc(s_wr, 1)
            act.activation(half_gb[:, :], gb[:, :], ACT.Copy, scale=0.5).then_inc(s_wr, 1)
            attention(GROUPS - 1, False)

            def logits(g):
                act.wait_ge(s_lgT, g + 1)
                if g >= 2:
                    act.wait_ge(s_lg, g - 1)
                act.activation(lgT[:, g % 2, :], bank[6][0:ROUTER, :], ACT.Copy).then_inc(s_lgc, 1)

            def shared(g, first, behind):
                for m in range(first, behind):
                    act.wait_ge(s_sgu, HTILES * g + m + 1)
                    wait(act, s_hid, HTILES * g + m - 1)
                    act.activation(sg[:, m % 2, :], bank[2 + 2 * (m % 2)][:, :], ACT.Silu).then_inc(s_sg, 1)

            logits(0)
            logits(1)
            shared(0, 0, 1)
            logits(2)
            shared(0, 1, 4)
            high3(GROUPS - 1)
            shared(0, 4, 5)
            logits(GROUPS - 1)
            act.wait_ge(s_diff, 1)
            act.activation(prob[:, :, :], tmp[:, :, :], ACT.Exp).then_inc(s_exp, 1)
            act.activation(one[:, :, 0], lg[:, :, EXPERTS], ACT.Tanh, bias=half_gb[:, 0:1], scale=0.5).then_inc(s_exp, 1)
            shared(0, 5, HTILES)
            shared(1, 0, HTILES)
            shared(2, 0, HTILES)

            def high_rows(i):
                act.wait_ge(s_xT, i + 1)
                act.activation(xst[:, 0, :], bank[0][:, 0:LANES * P], ACT.Copy).then_inc(s_xhi, 1)
                act.activation(xst[0:D1, 2, :], bank[1][0:D1, 0:LANES * P], ACT.Copy).then_inc(s_xhi, 1)

            def gate(i, j):
                act.wait_ge(s_gu, LANES * i + j + 1)
                act.activation(sgs[:, j, :], bank[2 + j][:, 0:HID], ACT.Silu).then_inc(s_si, 1)

            def results(i, odd):
                act.wait_ge(s_dest, i + 1)
                for j in range(LANES):
                    act.wait_ge(s_dn, LANES * i + (2, 2, 3)[j])
                    act.activation(ys[:, odd, j, :], down_bank(j), ACT.Copy).then_inc(s_ys, 1)

            def round_(i, odd, before, more):
                gate(i, 0)
                gate(i, 1)
                gate(i, 2)
                if more:
                    high_rows(i + 1)
                if before:
                    results(i - 1, 1 - odd)
                act.wait_ge(s_hT, i + 1)
                act.activation(hsT[:, 0, :], bank[5][:, 0:LANES * P], ACT.Copy).then_inc(s_hTc, 1)
                act.activation(hsT[0:HID - P, 1, :], bank[6][0:HID - P, 0:LANES * P], ACT.Copy).then_inc(s_hTc, 1)

            high_rows(0)
            round_(0, 0, False, True)
            with act.Fori(0, (ROUNDS - 3) // 2) as n:
                round_(2 * n + 1, 1, True, True)
                round_(2 * n + 2, 0, True, True)
            round_(ROUNDS - 2, 1, True, True)
            round_(ROUNDS - 1, 0, True, False)
            results(ROUNDS - 1, 0)
            shared(3, 0, HTILES)

        @block.vector
        def _(dve):
            def make_onehot(g):
                dve.tensor_scalar(onehot[:, :], ids[:, bass.ds(g % 2, 1), :].rearrange("p a n -> p (a n)"), cls[0:UROWS, 0:1], None,
                                  ALU.is_equal).then_inc(s_oh, 1)

            def statistics(k, g, src, eps, ready=None):
                for t in range(GT):
                    if ready:
                        dve.wait_ge(ready, t + 1)
                    dve.bn_stats(stat[:, k, t, :], src(t)).then_inc(s_bn[k], 1)
                wait_apart(dve, s_bn[k], g * GT + GT)
                for t in range(GT):
                    dve.bn_aggr(mv[:, k, t, :], stat[:, k, t, :]).then_inc(s_mv[k], 1)
                dve.wait_ge(s_mv[k], g * GT + GT)
                dve.tensor_scalar(var_eps[:, k, :] if k < 2 else var_eps3[:, bass.ds(g * GT, GT)], mv[:, k, :, 1], eps, None, ALU.add).then_inc(s_ve[k], 1)
                if k == 2:
                    dve.tensor_copy(mean3[:, bass.ds(g * GT, GT)], mv[:, k, :, 0]).then_inc(s_mean, 1)

            def embedding_norm(g):
                dve.wait_ge(s_rs[0], g + 1)
                for t in range(GT):
                    dve.scalar_tensor_tensor(out=emb[:, t, :], in0=emb[:, t, :], scalar=mv[:, 0, t, 0:1],
                                             in1=gam[:, :], op0=ALU.subtract, op1=ALU.mult).then_inc(s_gam, 1)
                for t in range(GT):
                    dve.wait_ge(s_gam, GT * g + t + 1)
                    dve.scalar_tensor_tensor(out=tile_of(h, g, t)[:, 0, :], in0=emb[:, t, :],
                                             scalar=rstd[:, 0, t:t + 1],
                                             in1=bet[:, :], op0=ALU.mult, op1=ALU.add).then_inc(s_h0, 1)
                wait_apart(dve, s_h0, GT * g + GT)

            def normed(g):
                dve.wait_ge(s_rs[1], g + 1)
                for t in range(GT):
                    dve.tensor_scalar(xn[:, t, :], tile_of(h, g, t)[:, 0, :], mv[:, 1, t, 0:1], rstd[:, 1, t:t + 1],
                                      ALU.subtract, ALU.mult).then_inc(s_xn, 1)

            def low(g):
                dve.wait_ge(s_hi, 2 * g + 1)
                dve.tensor_tensor(xt[:, 1, :], bank[0][:, :], xt[:, 0, :].bitcast(F32), ALU.subtract).then_inc(s_lo, 1)
                dve.wait_ge(s_hi, 2 * g + 2)
                dve.tensor_tensor(xt[D1:P, 2, :], bank[1][0:D1, :], xt[0:D1, 2, :].bitcast(F32),
                                  ALU.subtract).then_inc(s_lo, 1)

            def features(g, pair):
                for m in (2 * pair, 2 * pair + 1):
                    dve.wait_ge(s_act, 8 * g + 2 * m + 2)
                    parts = [(kphi[:, pair, :], slice(0, P))] if m % 2 == 0 else \
                        [(qz[0:HD, 2 * pair, :], slice(0, HD)), (qz[HD:P, 2 * pair + 1, :], slice(HD, P))]
                    for dst, r in parts:
                        dve.scalar_tensor_tensor(out=dst, in0=ex[r, m % 2, :], scalar=1.0, in1=xp1[r, m % 2, :],
                                                 op0=ALU.min, op1=ALU.max).then_inc(s_phi, 1)

            def reciprocals(g):
                dve.wait_ge(s_denT, g + 1)
                for odd in range(2):
                    dve.tensor_scalar(den[:, :, odd::2, 0],
                                      bank[4 + odd][:, 384:384 + 2 * GT].rearrange("p (t c) -> p t c", t=GT),
                                      1e-6, None, ALU.max).then_inc(s_den, 1)
                dve.wait_ge(s_den, 2 * g + 2)
                dve.reciprocal(rec[:, :, :, 0], den[:, :, :, 0]).then_inc(s_rec, 1)
                dve.wait_ge(s_rec, g + 1)
                dve.tensor_copy(recB[:, :, :, :], rec[:, :, :, :].to_broadcast([P, GT, HEADS, HD])).then_inc(s_recB, 1)

            def divide(g):
                for hd in range(HEADS):
                    if hd % 2 == 0:
                        dve.wait_ge(s_recT, 2 * g + hd // 2 + 1)
                    r = slice(0, HD) if hd % 2 == 0 else slice(HD, P)
                    dve.tensor_tensor(oT[r, hd // 2, :], bank[4 + hd // 2][r, :], numden[r, hd, :],
                                      ALU.mult).then_inc(s_nrm, 1)

            def gated(g):
                for t in range(GT):
                    dve.wait_ge(s_wo, 2 * g + t // 2 + 1)
                    b = bank[2 + t // 2]
                    gg = gate_of(g, t)[:, 0, :]
                    dve.scalar_tensor_tensor(out=gg, in0=gg, scalar=1.0,
                                             in1=b[:, (t % 2) * D:(t % 2 + 1) * D], op0=ALU.add,
                                             op1=ALU.mult).then_inc(s_wog, 1)

            def residual(g):
                for t in range(GT):
                    hh = tile_of(h, g, t)
                    dve.wait_ge(s_wog, 4 * g + t + 1)
                    dve.scalar_tensor_tensor(out=hh, in0=gate_of(g, t), scalar=0.5, in1=hh, op0=ALU.mult,
                                             op1=ALU.add).then_inc(s_res, 1)

            def normed3(g):
                dve.wait_ge(s_mean, g + 1)
                dve.wait_ge(s_rs[2], g + 1)
                for t in range(GT * g, GT * g + GT):
                    dve.tensor_scalar(x3[:, t, 0:D], h[:, t, :], mean3[:, t:t + 1], rstd3[:, t:t + 1], ALU.subtract,
                                      ALU.mult).then_inc(s_x3, 1)

            def low3(g):
                dve.wait_ge(s_hi3, 2 * g + 1)
                tok = slice(g * GN, (g + 1) * GN)
                dve.tensor_tensor(x3t[:, 1, tok], bank[0][:, :], x3t[:, 0, tok].bitcast(F32),
                                  ALU.subtract).then_inc(s_lo3, 1)
                dve.wait_ge(s_hi3, 2 * g + 2)
                dve.tensor_tensor(x3t[D1:P, 2, tok], bank[1][0:D1, :], x3t[0:D1, 2, tok].bitcast(F32),
                                  ALU.subtract).then_inc(s_lo3, 1)

            def logits(g):
                dve.wait_ge(s_lg, g + 1)
                dve.tensor_copy(lg[:, g * GT:(g + 1) * GT, :],
                                bank[7][:, 0:GT * ROUTER].rearrange("p (t c) -> p t c", t=GT)[:, :, 0:EXPERTS + 1]
                                ).then_inc(s_lgv, 1)

            def shared_hidden(g, m):
                dve.wait_ge(s_sg, HTILES * g + m + 1)
                dve.tensor_tensor(hid[:, m, :], bank[3 + 2 * (m % 2)][:, :], sg[:, m % 2, :],
                                  ALU.mult).then_inc(s_hid, 1)

            def attention(g, before, more):
                if more:
                    dve.wait_ge(s_win, 16 * g + 16)
                    make_onehot(g + 1)
                features(g, 0)
                if before:
                    reciprocals(g - 1)
                features(g, 1)
                if before:
                    divide(g - 1)
                if more:
                    wait_apart(dve, s_emb, GT * (g + 2))
                    statistics(0, g + 1, lambda t: emb[:, t, :], 1e-12)
                if not more:
                    normed3(0)
                    normed3(1)
                if before:
                    gated(g - 1)
                if more:
                    embedding_norm(g + 1)
                    statistics(1, g + 1, lambda t: tile_of(h, g + 1, t)[:, 0, :], 1e-5)
                    normed(g + 1)
                if before:
                    residual(g - 1)
                if more:
                    low(g + 1)
                if before:
                    wait_apart(dve, s_res, GT * g)
                    statistics(2, g - 1, lambda t: tile_of(h, g - 1, t)[:, 0, :], 1e-5)

            dve.wait_ge(s_cw, 16)
            dve.tensor_copy(cwr[:, :], cw[:, :]).then_inc(s_cwr, 1)
            dve.wait_ge(s_cwr, 1)
            dve.tensor_tensor(cwr[WIN_LO:UROWS, :], cw[WIN_LO:UROWS, :], cwr[WIN_LO:UROWS, :].bitcast(F32),
                              ALU.subtract).then_inc(s_cwr, 1)
            dve.wait_ge(s_win0, 16)
            dve.wait_ge(s_cls, 16)
            make_onehot(0)
            statistics(0, 0, lambda t: emb[:, t, :], 1e-12, s_emb)
            dve.wait_ge(s_gb, 32)
            embedding_norm(0)
            statistics(1, 0, lambda t: tile_of(h, 0, t)[:, 0, :], 1e-5)
            dve.wait_ge(s_whi, 1)
            dve.tensor_tensor(wqk[:, 1::2, :], raw_qk[:, :, :], wqk[:, 0::2, :].bitcast(F32),
                              ALU.subtract).then_inc(s_wlo, 1)
            normed(0)
            low(0)
            dve.wait_ge(s_const, 5)
            attention(0, False, True)
            with dve.Fori(1, GROUPS - 1) as g:
                attention(g, True, True)
            dve.wait_ge(s_cst, 48)
            dve.tensor_copy(x3[:, :, D], token_no).then_inc(s_no, 1)
            dve.wait_ge(s_wr, 2)
            dve.tensor_tensor(wr[:, 1::2, :], raw_r[:, :, :], wr[:, 0::2, :].bitcast(F32), ALU.subtract).then_inc(s_wr, 1)
            attention(GROUPS - 1, True, False)
            low3(0)
            normed3(2)
            low3(1)
            reciprocals(GROUPS - 1)
            low3(2)
            divide(GROUPS - 1)
            shared_hidden(0, 0)
            logits(0)
            gated(GROUPS - 1)
            residual(GROUPS - 1)
            logits(1)
            dve.wait_ge(s_res, GT * GROUPS)
            statistics(2, GROUPS - 1, lambda t: tile_of(h, GROUPS - 1, t)[:, 0, :], 1e-5)
            shared_hidden(0, 1)
            dve.memset(run[:, :, :, :], 0.0).then_inc(s_clear, 1)
            dve.memset(ends[:, :, :], 0.0).then_inc(s_clear, 1)
            normed3(GROUPS - 1)
            shared_hidden(0, 2)
            logits(2)
            shared_hidden(0, 3)
            low3(GROUPS - 1)
            logits(GROUPS - 1)

            chain = [0]

            def step(ins):
                chain[0] += 1
                ins.then_inc(s_r, 1)
                dve.wait_ge(s_r, chain[0])

            all3 = [P, TILES, EXPERTS]

            def choose(k):
                step(dve.tensor_reduce(best[:, k, :, 0], prob[:, :, :], AX.X, ALU.max))
                step(dve.tensor_tensor(tmp[:, :, :], prob[:, :, :], best[:, k, :, :].to_broadcast(all3), ALU.is_equal))
                step(dve.tensor_tensor(tmp[:, :, :], tmp[:, :, :], desc.unsqueeze(1).to_broadcast(all3), ALU.mult))
                step(dve.tensor_reduce(tmp2[:, :, 0], tmp[:, :, :], AX.X, ALU.max))
                if k == 0:
                    shared_hidden(0, HTILES - 1)
                step(dve.tensor_tensor(pick[:, k, :, :], tmp[:, :, :], tmp2[:, :, 0:1].to_broadcast(all3), ALU.is_equal))

            dve.wait_ge(s_lgv, GROUPS)
            step(dve.tensor_reduce(best[:, 0, :, 0], lg[:, :, 0:EXPERTS], AX.X, ALU.max))
            dve.tensor_tensor(tmp[:, :, :], lg[:, :, 0:EXPERTS], best[:, 0, :, :].to_broadcast(all3),
                              ALU.subtract).then_inc(s_diff, 1)
            shared_hidden(0, 4)
            dve.wait_ge(s_exp, 2)
            step(dve.tensor_reduce(best[:, 0, :, 0], prob[:, :, :], AX.X, ALU.add))
            step(dve.reciprocal(best[:, 1, :, 0], best[:, 0, :, 0]))
            step(dve.tensor_tensor(prob[:, :, :], prob[:, :, :], best[:, 1, :, :].to_broadcast(all3), ALU.mult))
            choose(0)
            step(dve.scalar_tensor_tensor(out=prob[:, :, :], in0=pick[:, 0, :, :], scalar=-2.0, in1=prob[:, :, :],
                                          op0=ALU.mult, op1=ALU.add))
            choose(1)
            dve.tensor_tensor(taken[:, :, :], pick[:, 0, :, :], pick[:, 1, :, :], ALU.add).then_inc(s_taken, 1)
            dve.wait_ge(s_clear, 2)
            dve.wait_ge(s_cnt, 1)
            step(dve.tensor_copy(run[:, 0, EXPERTS:, :], bank[0][:, P:2 * P].rearrange("p (t e) -> p t e", t=TILES)))
            for n, d in enumerate((1, 2, 4, 8)):
                a, b = n % 2, 1 - n % 2
                step(dve.tensor_tensor(run[:, b, EXPERTS:, :], run[:, a, EXPERTS:, :],
                                       run[:, a, EXPERTS - d:EXPERTS - d + TILES, :], ALU.add))
            total = run[:, 0, EXPERTS + TILES - 1, :]
            wide3 = [P, EXPERTS, TILES]
            step(dve.tensor_tensor(wide[:, :, :], total.unsqueeze(2).to_broadcast(wide3),
                                   steps.unsqueeze(1).to_broadcast(wide3), ALU.is_gt))
            step(dve.tensor_reduce(ends[:, 0, 4:], wide[:, :, :], AX.X, ALU.add))
            for n, d in enumerate((1, 2, 4)):
                a, b = n % 2, 1 - n % 2
                step(dve.tensor_tensor(ends[:, b, 4:], ends[:, a, 4:], ends[:, a, 4 - d:4 - d + EXPERTS], ALU.add))
            step(dve.scalar_tensor_tensor(out=tmp[:, :, :], in0=ends[:, 1, 3:3 + EXPERTS].unsqueeze(1).to_broadcast(all3),
                                          scalar=float(P), in1=run[:, 0, EXPERTS - 1:EXPERTS - 1 + TILES, :],
                                          op0=ALU.mult, op1=ALU.add))
            step(dve.tensor_tensor(tmp[:, :, :], bank[0][:, 0:P].rearrange("p (t e) -> p t e", t=TILES), tmp[:, :, :],
                                   ALU.add))
            for k in range(2):
                step(dve.tensor_tensor(tmp2[:, :, :], tmp[:, :, :], pick[:, k, :, :], ALU.mult))
                step(dve.tensor_reduce(pos_f[:, k, :], tmp2[:, :, :], AX.X, ALU.add))
                dve.tensor_copy(pos[:, k, :], pos_f[:, k, :]).then_inc(s_pos, 1)
            dve.wait_ge(s_sdn, 2)
            shared_hidden(1, 0)
            slot3 = [1, SLOTS, EXPERTS]
            step(dve.tensor_tensor(at_slot[:, :, :], slot_no[0:1, :].unsqueeze(2).to_broadcast(slot3),
                                   ends[0:1, 1, 4:].unsqueeze(1).to_broadcast(slot3), ALU.is_ge))
            step(dve.tensor_reduce(expert_f[:, :, 0], at_slot[:, :, :], AX.X, ALU.add))
            dve.tensor_scalar(expert[:, :], expert_f[:, :, 0], float(EXPERTS - 1), None, ALU.min).then_inc(s_eid, 1)
            shared_hidden(1, 1)
            step(dve.tensor_scalar(alpha[:, 0, :], one[:, :, 0], 0.5, 0.5, ALU.mult, ALU.add))
            step(dve.tensor_scalar(alpha[:, 1, :], alpha[:, 0, :], -1.0, 1.0, ALU.mult, ALU.add))
            step(dve.tensor_tensor(tmp2[:, :, 1], best[:, 0, :, 0], best[:, 1, :, 0], ALU.add))
            step(dve.reciprocal(tmp2[:, :, 2], tmp2[:, :, 1]))
            step(dve.tensor_tensor(tmp2[:, :, 3], tmp2[:, :, 2], alpha[:, 1, :], ALU.mult))
            for k in range(2):
                step(dve.tensor_tensor(gates[:, k, :], best[:, k, :, 0], tmp2[:, :, 3], ALU.mult))

            def add_shared(g, tiles, products):
                dve.wait_ge(s_sdn, products)
                for t in tiles:
                    n = GT * g + t
                    dve.scalar_tensor_tensor(out=h[:, n, :], in0=bank[6 + t // 2][:, (t % 2) * D:(t % 2 + 1) * D],
                                             scalar=alpha[:, 0, n:n + 1], in1=h[:, n, :], op0=ALU.mult,
                                             op1=ALU.add).then_inc(s_shr, 1)

            def second_rows(half):
                dve.wait_ge(s_scat[0][half], 16 * HALF)
                no = x3[:, half * HALF:(half + 1) * HALF, D]
                dve.tensor_scalar(no, no, float(TILES * P), None, ALU.add).then_inc(s_no, 1)

            for m in range(2, HTILES):
                shared_hidden(1, m)
                if m == 2:
                    add_shared(0, range(GT), 2)
                if m in SECOND:
                    second_rows(SECOND.index(m))
            add_shared(1, range(GT), 4)
            for m in range(HTILES):
                shared_hidden(2, m)

            def low_rows(i, odd):
                dve.wait_ge(s_xhi, 2 * i + 2)
                dve.scalar_tensor_tensor(out=pad[:, :], in0=xs[:, odd, :, D], scalar=0.0,
                                         in1=spare[:, odd * LANES:(odd + 1) * LANES], op0=ALU.is_equal,
                                         op1=ALU.mult).then_inc(s_pad, 1)
                dve.tensor_tensor(xst[:, 1, :], bank[0][:, 0:LANES * P], xst[:, 0, :].bitcast(F32),
                                  ALU.subtract).then_inc(s_xlo, 1)
                dve.tensor_tensor(xst[D1:P, 2, :], bank[1][0:D1, 0:LANES * P], xst[0:D1, 2, :].bitcast(F32),
                                  ALU.subtract).then_inc(s_xlo, 1)
                dve.wait_ge(s_pad, i + 1)
                dve.tensor_tensor(dest_f[:, odd, :], pad[:, :], xs[:, odd, :, D], ALU.add).then_inc(s_kept, 1)

            def round_(i, more, odd, before):
                for j in range(LANES):
                    dve.wait_ge(s_si, LANES * i + j + 1)
                    dve.tensor_tensor(hs[:, j, :], bank[2 + j][:, HID:2 * HID], sgs[:, j, :],
                                      ALU.mult).then_inc(s_hs, 1)
                dve.wait_ge(s_kept, i + 1)
                if not isinstance(before, int) or before:
                    dve.wait_ge(s_st[odd], 16 * LANES * before)
                dve.tensor_copy(dest[:, odd, :], dest_f[:, odd, :]).then_inc(s_dest, 1)
                if more:
                    low_rows(i + 1, 1 - odd)

            low_rows(0, 0)
            add_shared(2, (0, 1, 2), 6)
            round_(0, True, 0, 0)
            add_shared(2, (3,), 7)
            round_(1, True, 1, 0)
            with dve.Fori(1, ROUNDS // 2) as n:
                for k in range(2):
                    round_(2 * n + k, True, k, n)
            round_(ROUNDS - 1, False, 0, ROUNDS // 2)

            def add_routed(tiles):
                for k in range(2):
                    for t in tiles:
                        if k == 0:
                            dve.wait_ge(s_back[t // GT], 32)
                        else:
                            dve.wait_ge(s_sum[0], t + 1)
                        dve.scalar_tensor_tensor(out=h[:, t, :], in0=back[k][:, t, :], scalar=gates[:, k, t:t + 1],
                                                 in1=h[:, t, :], op0=ALU.mult, op1=ALU.add).then_inc(s_sum[k], 1)

            for m in range(HTILES):
                shared_hidden(3, m)
                if m in (3, 4):
                    add_routed(range(2 * m - 6, 2 * m - 4))
            for g in range(1, GROUPS):
                add_routed(range(g * GT, (g + 1) * GT))
            dve.wait_ge(s_sum[1], TILES)
            add_shared(3, (0, 1), 8)
            add_shared(3, (2, 3), 9)

        @block.tensor
        def _(pe):
            def embed(g):
                pe.wait_ge(s_oh, g + 1)
                wait(pe, s_lo, 2 * g)
                for t in range(GT):
                    mm = pe.matmul(bank[t // 2][:, (t % 2) * D:(t % 2 + 1) * D], onehot[:, t * P:(t + 1) * P],
                                   cwr[:, :], start=True, stop=True)
                    if t % 2:
                        mm.then_inc(s_conv, 1)

            def transposes(g):
                pe.wait_ge(s_xn, GT * g + GT)
                for t in range(GT):
                    mm = pe.transpose(bank[0][:, t * P:(t + 1) * P], xn[:, t, 0:P], ident[:, :])
                mm.then_inc(s_T, 1)
                for t in range(GT):
                    mm = pe.transpose(bank[1][0:D1, t * P:(t + 1) * P], xn[:, t, P:D], ident[:, :])
                mm.then_inc(s_T, 1)

            def scores(g, n):
                hd, b = n // 2, n % 2
                if n >= 2:
                    pe.wait_ge(s_ev, 8 * g + n - 1)
                if n % 4 == 0:
                    pe.wait_ge(s_phi, 6 * g + (3 if n == 0 else 6))
                for kt in range(2):
                    o = b * S + kt * P
                    mm = pe.matmul(bank[4 + n % 2][:, kt * S:kt * S + S - kt * P], kphi[:, hd // 2, o:o + P],
                                   qz[:, hd, o:b * S + S], start=True, stop=True)
                mm.then_inc(s_sc, 1)

            def weighted(g, n):
                hd, b = n // 2, n % 2
                if b == 0:
                    wait(pe, s_nd, 4 * g + hd - 1)
                pe.wait_ge(s_mask, 8 * g + n + 1)
                for kt in range(2):
                    mm = pe.matmul(bank[6 + hd % 2][:, b * S + kt * P:b * S + S], vp[:, 2 * b + kt, hd, :],
                                   sT[:, n % 4, kt * S:kt * S + S - kt * P], start=kt == 0, stop=kt == 1)
                mm.then_inc(s_pv, 1)

            def denominators(g):
                for hd in range(HEADS):
                    wait_apart(pe, s_nd, 4 * g + hd + 1)
                    r = HD if hd % 2 == 0 else 0
                    for t in range(GT):
                        c = 384 + 2 * t + hd // 2
                        mm = pe.transpose(bank[4 + hd % 2][:, c:c + 1], numden[r:r + 1, hd, t * P:(t + 1) * P],
                                          ident[r:r + 1, r:r + 1])
                mm.then_inc(s_denT, 1)

            def spread(g):
                pe.wait_ge(s_recB, g + 1)
                for pair in range(2):
                    for t in range(GT):
                        mm = pe.transpose(bank[4 + pair][:, t * P:(t + 1) * P],
                                          recB[:, t, 2 * pair:2 * pair + 2, :].rearrange("p h c -> p (h c)"), ident[:, :])
                    mm.then_inc(s_recT, 1)

            def keys_queries(g, pair):
                if pair == 0:
                    pe.wait_ge(s_hi, 2 * g + 1)
                for m in (2 * pair, 2 * pair + 1):
                    if m < 2:
                        wait(pe, s_vg, 12 * g - 3 + 3 * m)
                    else:
                        pe.wait_ge(s_act, 8 * g + 2 * m - 2)
                    for k, (x, w) in enumerate(pieces(xt, wqk, slice(m * P, (m + 1) * P), slice(0, GN))):
                        if m == 0 and k in (2, 3):
                            pe.wait_ge(s_lo, 2 * g + k - 1)
                        mm = pe.matmul(bank[2 + m % 2][:, :], w, x, start=k == 0, stop=k == 4)
                    mm.then_inc(s_proj, 1)

            def values_gates(g):
                for t in range(GT):
                    if t < 2:
                        pe.wait_ge(s_act, 8 * g + 6 + 2 * t)
                    else:
                        pe.wait_ge(s_vg, 12 * g + 3 * t - 3)
                    for k, (x, w) in enumerate(pieces(xt, wvg, slice(0, 448), slice(t * P, (t + 1) * P))):
                        mm = pe.matmul(bank[2 + t % 2][:, 0:448], x, w, start=k == 0, stop=k == 4)
                    mm.then_inc(s_proj, 1)

            def output(g, last):
                pe.wait_ge(s_nrm, 4 * g + 4)
                for t in range(GT):
                    if t % 2 == 0 and not last:
                        pe.wait_ge(s_vg, 12 * (g + 1) + (9, 12)[t // 2])
                    for k in range(2):
                        mm = pe.matmul(bank[2 + t // 2][:, (t % 2) * D:(t % 2 + 1) * D], oT[:, k, t * P:(t + 1) * P],
                                       wo[:, k, :], start=k == 0, stop=k == 1)
                    if t % 2:
                        mm.then_inc(s_wo, 1)

            def transposes3(g):
                pe.wait_ge(s_x3, GT * g + GT)
                wait(pe, s_lo3, 2 * g)
                for t in range(GT):
                    mm = pe.transpose(bank[0][:, t * P:(t + 1) * P], x3[:, g * GT + t, 0:P], ident[:, :])
                mm.then_inc(s_T3, 1)
                for t in range(GT):
                    mm = pe.transpose(bank[1][0:D1, t * P:(t + 1) * P], x3[:, g * GT + t, P:D], ident[:, :])
                mm.then_inc(s_T3, 1)

            def router(g):
                pe.wait_ge(s_lo3, 2 * g + 2)
                wait(pe, s_lgc, g)
                for k, (x, w) in enumerate(pieces(x3t, wr, slice(0, ROUTER), slice(g * GN, (g + 1) * GN))):
                    mm = pe.matmul(bank[6][0:ROUTER, :], w, x, start=k == 0, stop=k == 4)
                mm.then_inc(s_lgT, 1)

            def logits(g):
                pe.wait_ge(s_lgc, g + 1)
                wait(pe, s_lgv, g)
                for t in range(GT):
                    mm = pe.transpose(bank[7][:, t * ROUTER:(t + 1) * ROUTER], lgT[:, g % 2, t * P:(t + 1) * P],
                                      ident[0:ROUTER, 0:ROUTER])
                mm.then_inc(s_lg, 1)

            def counts():
                pe.wait_ge(s_taken, 1)
                m = taken[:, :, :].rearrange("p t e -> p (t e)")
                pe.matmul(bank[0][:, 0:P], below, m, start=True, stop=True)
                pe.matmul(bank[0][:, P:2 * P], ones[:, :], m, start=True, stop=True).then_inc(s_cnt, 1)

            def shared_up(g, m):
                if not isinstance(g, int) or g or m >= 2:
                    pe.wait_ge(s_hid, HTILES * g + m - 1)
                for k in range(2):
                    c = EXPERTS * CHUNK + k * SHARED + m * P
                    for n, (x, w) in enumerate(pieces(x3t, wgu, slice(c, c + P), bass.ds(g * GN, GN))):
                        mm = pe.matmul(bank[2 + 2 * (m % 2) + k][:, :], w, x, start=n == 0, stop=n == 4)
                mm.then_inc(s_sgu, 1)

            def shared_down(g, tiles):
                if 0 in tiles:
                    wait(pe, s_shr, GT * g)
                together = tiles[0] // 2 != tiles[-1] // 2
                steps = [(t, m) for ms in (range(HTILES - 1), (HTILES - 1,)) for t in tiles for m in ms] \
                    if together else [(t, m) for t in tiles for m in range(HTILES)]
                for n, (t, m) in enumerate(steps):
                    if m == HTILES - 1:
                        pe.wait_ge(s_hid, HTILES * g + HTILES)
                    elif n == 0:
                        pe.wait_ge(s_hid, HTILES * g + HTILES - 1)
                    mm = pe.matmul(bank[6 + t // 2][:, (t % 2) * D:(t % 2 + 1) * D], hid[:, m, t * P:(t + 1) * P],
                                   wsdn[:, m, :], start=m == 0, stop=m == HTILES - 1)
                mm.then_inc(s_sdn, 1)

            def attention(g, before, more):
                keys_queries(g, 0)
                if before:
                    denominators(g - 1)
                keys_queries(g, 1)
                if more:
                    embed(g + 1)
                if before:
                    spread(g - 1)
                values_gates(g)
                if before:
                    output(g - 1, False)
                for n in range(8):
                    scores(g, n)
                    if n == 6 and more:
                        transposes(g + 1)
                    if n in (2, 6) and not more:
                        transposes3(n // 4)
                    if n >= 2:
                        if n == 2:
                            pe.wait_ge(s_vg, 12 * g + 12)
                        weighted(g, n - 2)
                weighted(g, 6)
                weighted(g, 7)

            def experts_of(i, rounds):
                n = rounds * LANES
                _, es = nc.values_load_multi_w_load_instructions(
                    expert[0:1, bass.ds(LANES * i, n)], engines=(mybir.EngineType.PE,), min_val=0, max_val=EXPERTS - 1,
                    skip_runtime_bounds_check_because="VectorE limits it to EXPERTS - 1, and a count is not negative")
                return [es[k:k + LANES] for k in range(0, n, LANES)]

            pe.wait_ge(s_cwr, 2)
            embed(0)
            pe.wait_ge(s_gam, 1)
            for _ in range(WARM):
                pe.matmul(bank[7][:, 0:D], zero[:, 0:P], zero[:, 0:D], start=True, stop=True)
            pe.wait_ge(s_idn, 32)
            transposes(0)
            pe.wait_ge(s_wlo, 2)
            pe.wait_ge(s_const, 5)
            attention(0, False, True)
            with pe.Fori(1, GROUPS - 1) as g:
                attention(g, True, True)
            attention(GROUPS - 1, True, False)

            transposes3(2)
            pe.wait_ge(s_wr, 3)
            pe.wait_ge(s_nd, HEADS * GROUPS - 1)
            router(0)
            denominators(GROUPS - 1)
            router(1)
            spread(GROUPS - 1)
            pe.wait_ge(s_glo, CHUNKS)
            shared_up(0, 0)
            logits(0)
            router(2)
            pe.wait_ge(s_hid, 1)
            output(GROUPS - 1, True)
            logits(1)
            shared_up(0, 1)
            pe.wait_ge(s_wog, TILES)
            shared_up(0, 2)
            logits(2)
            shared_up(0, 3)
            transposes3(GROUPS - 1)
            shared_up(0, 4)
            router(GROUPS - 1)
            logits(GROUPS - 1)
            shared_up(0, 5)
            pe.wait_ge(s_lgv, GROUPS)
            pe.wait_ge(s_wsdn, 16)
            shared_down(0, (0, 2))
            counts()
            shared_up(1, 0)
            shared_down(0, (1, 3))
            for m in range(1, HTILES):
                shared_up(1, m)
            shared_down(1, (0, 2))
            shared_down(1, (1, 3))
            for m in range(HTILES):
                shared_up(2, m)
            shared_down(2, (0, 2))
            pe.wait_ge(s_eid, 1)
            first, = experts_of(0, 1)
            pe.wait_ge(s_wdn, 16)

            def rows(i, odd, pair):
                for j in range(LANES):
                    pe.wait_ge(s_xl[odd * LANES + j], 16 * pair + 16)
                for j in range(LANES):
                    pe.transpose(bank[0][:, j * P:(j + 1) * P], xs[:, odd, j, 0:P], ident[:, :])
                for j in range(LANES):
                    mm = pe.transpose(bank[1][0:D1, j * P:(j + 1) * P], xs[:, odd, j, P:D], ident[:, :])
                mm.then_inc(s_xT, 1)

            def up(i, j, e):
                if j == 0:
                    pe.wait_ge(s_xlo, 2 * i + 2)
                if j == 2 and not (isinstance(i, int) and i == 0):
                    pe.wait_ge(s_hTc, 2 * i)
                for n, (x, w) in enumerate(pieces(xst, wgu, bass.ds(e * CHUNK, CHUNK), slice(j * P, (j + 1) * P))):
                    mm = pe.matmul(bank[2 + j][:, 0:CHUNK], x, w, start=n == 0, stop=n == 4)
                mm.then_inc(s_gu, 1)

            def turn(i):
                for j in range(LANES):
                    pe.wait_ge(s_hs, LANES * i + j + 1)
                    pe.transpose(bank[5][:, j * P:(j + 1) * P], hs[:, j, 0:P], ident[:, :])
                    mm = pe.transpose(bank[6][0:HID - P, j * P:(j + 1) * P], hs[:, j, P:HID], ident[:, :])
                mm.then_inc(s_hT, 1)

            def down(i, more, es):
                for j in range(LANES):
                    if j == 0:
                        pe.wait_ge(s_hTc, 2 * i + 2)
                    if j == 2 and more:
                        pe.wait_ge(s_hs, LANES * (i + 1) + 3)
                    for k, r in ((0, P), (1, HID - P)):
                        mm = pe.matmul(down_bank(j), hsT[0:r, k, j * P:(j + 1) * P],
                                       wdn[0:r, bass.ds(es[j], 1), k, :].rearrange("p a d -> p (a d)"), start=k == 0, stop=k == 1)
                    mm.then_inc(s_dn, 1)

            def round_(i, es, before, more, odd, pair):
                up(i, 0, es[0])
                up(i, 1, es[1])
                if more:
                    rows(i + 1, odd, pair)
                up(i, 2, es[2])
                if not before:
                    pe.wait_ge(s_shr, 2 * GT + 3)
                    shared_down(2, (3,))
                if before:
                    down(i - 1, True, before)
                turn(i)

            rows(0, 0, 0)
            shared_down(2, (1,))
            round_(0, first, None, True, 1, 0)
            pe.wait_ge(s_shr, 3 * GT)
            with pe.Fori(0, (ROUNDS - 3) // 2) as n:
                e0, e1, e2 = experts_of(2 * n, 3)
                round_(2 * n + 1, e1, e0, True, 0, n + 1)
                round_(2 * n + 2, e2, e1, True, 1, n + 1)
            e0, e1, e2 = experts_of(ROUNDS - 3, 3)
            round_(ROUNDS - 2, e1, e0, True, 0, (ROUNDS - 1) // 2)
            round_(ROUNDS - 1, e2, e1, False, 0, 0)
            down(ROUNDS - 1, False, e2)
            for m in range(HTILES):
                if m == 1:
                    pe.wait_ge(s_ys, SLOTS)
                shared_up(3, m)
            shared_down(3, (0, 1))
            shared_down(3, (2, 3))


def lay_out(x, mask, W3, W5, W7, gamma, beta, Wq, Wk, Wv, Wo, Wg, router_w, w_gate, w_up, w_down, ws_gate,
            ws_up, ws_down, sg_w, sg_b):
    half = TAPS // 2
    padded = np.full((B, S + 2 * half), -1, x.dtype)
    padded[:, half:half + S] = x
    windows = np.stack([padded[:, k:k + S].reshape(-1) for k in range(TAPS) for _ in range(CLS)])
    conv = np.zeros((TAPS, CLS, D), W3.dtype)
    for n, w in enumerate((W3, W5, W7)):
        k = w.shape[2]
        conv[half - k // 2:half + k // 2 + 1, :, 64 * n:64 * n + 64] = w.transpose(2, 1, 0)
    classes = np.zeros((P, 1), np.float32)
    for lo in (0, WIN_LO):
        classes[lo:lo + WIN, 0] = np.tile(np.arange(CLS), TAPS)

    def doubled(w, pad):
        return np.concatenate([w, np.full((WIN_LO - WIN, w.shape[1]), pad, w.dtype), w])

    def twice(w):
        return np.ascontiguousarray(np.stack([w[:P], np.concatenate([w[P:], w[P:]])], axis=1))

    qk = np.concatenate([Wk[:, :P], Wq[:, :P], Wk[:, P:], Wq[:, P:]], axis=1)
    vg = np.concatenate([Wv, Wg], axis=1)
    gu = np.concatenate([w_gate, w_up], axis=2).transpose(1, 0, 2).reshape(D, EXPERTS * CHUNK)
    gu = np.concatenate([gu, ws_gate, ws_up], axis=1)
    dn = np.zeros((P, EXPERTS, 2, D), w_down.dtype)
    dn[:, :, 0] = w_down[:, :P].transpose(1, 0, 2)
    dn[:HID - P, :, 1] = w_down[:, P:].transpose(1, 0, 2)
    router = np.zeros((D, ROUTER), router_w.dtype)
    router[:, :EXPERTS] = router_w
    router[:, EXPERTS:EXPERTS + 1] = sg_w
    counting = np.concatenate([np.triu(np.ones((P, P)), 1)] + [
        np.broadcast_to(row, (P, len(row))) for row in
        (np.arange(TILES) * P, np.arange(EXPERTS, 0, -1), np.arange(SLOTS))]
        + [1 + np.arange(TILES * P).reshape(TILES, P).T]
        + [1 + 2 * TILES * P + np.arange(2 * LANES * P).reshape(2 * LANES, P).T], axis=1).astype(np.float32)
    return {
        "windows": doubled(windows, -1), "classes": classes, "conv_w": doubled(conv.reshape(WIN, D), 0),
        "tok_mask": np.ascontiguousarray(mask.reshape(TILES, P).T),
        "gamma": np.ascontiguousarray(np.broadcast_to(gamma, (P, D))),
        "beta": np.ascontiguousarray(np.broadcast_to(beta, (P, D))),
        "w_qk": twice(qk), "w_vg": twice(vg),
        "w_o": np.ascontiguousarray(Wo.reshape(2, P, D).transpose(1, 0, 2)),
        "ident_in": np.eye(P, dtype=np.float32),
        "w_gu": np.ascontiguousarray(twice(gu).reshape(P, 2, CHUNKS, CHUNK).transpose(0, 2, 1, 3)),
        "w_dn": dn, "w_sdn": np.ascontiguousarray(ws_down.reshape(HTILES, P, D).transpose(1, 0, 2)),
        "w_router": twice(router), "gate_bias": np.ascontiguousarray(np.broadcast_to(sg_b, (P, 1))),
        "counting": counting,
    }

_ORDER = ["x", "mask_BS_f1_0", "L0_tok_W3", "L0_tok_W5", "L0_tok_W7", "L0_tok_ln_gamma", "L0_tok_ln_beta",
          "L0_attn_Wq", "L0_attn_Wk", "L0_attn_Wv", "L0_attn_Wo", "L0_attn_Wg", "L0_ffn_router_w",
          "L0_ffn_w_gate", "L0_ffn_w_up", "L0_ffn_w_down", "L0_ffn_ws_gate", "L0_ffn_ws_up", "L0_ffn_ws_down",
          "L0_ffn_sg_w", "L0_ffn_sg_b"]


def kernel(**inputs):
    import concourse.bacc as bacc
    from concourse.bass_utils import run_bass_kernel_spmd

    nc = bacc.Bacc("TRN2", target_bir_lowering=False, num_devices=1)
    arrays = lay_out(*[np.asarray(inputs[name]) for name in _ORDER])
    args = [nc.dram_tensor(f"{name}_dram", a.shape, mybir.dt.from_np(a.dtype), kind="ExternalInput").ap()
            for name, a in arrays.items()]
    out = nc.dram_tensor("out_dram", (P, TILES * D), F32, kind="ExternalOutput").ap()
    tower(nc, *args, out)
    result = run_bass_kernel_spmd(nc, [{f"{name}_dram": a for name, a in arrays.items()}], core_ids=[0])
    y = result.results[0]["out_dram"].reshape(P, TILES, D).transpose(1, 0, 2)
    return np.ascontiguousarray(y).reshape(B, S, D)
```

```python
from contextlib import ExitStack

import concourse.bass as bass
import numpy as np
from concourse import mybir

F32 = mybir.dt.float32
F32R = mybir.dt.float32r
I32 = mybir.dt.int32
U32 = mybir.dt.uint32
ALU = mybir.AluOpType
AX = mybir.AxisListType
ACT = mybir.ActivationFunctionType

P = 128
B, S, D = 8, 256, 192
TILES = B * S // P
GROUPS = 4
GT = TILES // GROUPS
GN = GT * P
HALF = TILES // 2
D1 = D - P
HEADS, HD = 4, 64
TAPS, CLS = 7, 5
WIN = TAPS * CLS
EXPERTS, HID = 8, 192
SLOTS = 2 * TILES + EXPERTS - 1
LANES = 3
ROUNDS = SLOTS // LANES
SHARED = 768
WARM = 12
SECOND = (4, 5)
HELPED = (6, 7, 10, 11, 13)
HTILES = SHARED // P
CHUNK = 2 * HID
CHUNKS = EXPERTS + 2 * SHARED // CHUNK
DOWN_CHUNKS = EXPERTS * D // CHUNK
ROUTER = 32
WIN_LO = 64
UROWS = WIN_LO + WIN


def pieces(xt, blocks, cols, tok):
    for a, b in ((0, 0), (0, 1), (1, 0), (2, 2), (2, 3)):
        yield xt[:, a, tok], blocks[:, b, cols]


def tower(nc, windows, classes, conv_w, tok_mask, gamma, beta, w_qk, w_vg, w_o, ident_in, w_gu, w_dn, w_sdn,
          w_router, gate_bias, counting, out):
    ctx = ExitStack()
    with ctx:
        def sb(name, shape, dt=F32):
            return ctx.enter_context(nc.sbuf_tensor(name, shape, dt))

        def sem(name):
            return ctx.enter_context(nc.semaphore(name))

        sorted_x = nc.dram_tensor("sorted_x", [SLOTS * P, D + 1], F32, kind="Internal").ap()
        routed = nc.dram_tensor("routed", [1 + 2 * TILES * P + 2 * LANES * P, D], F32, kind="Internal").ap()
        bank = [ctx.enter_context(nc.psum_tensor(f"bank{i}", [P, 512], F32)) for i in range(8)]

        h = sb("h", [P, TILES, D])
        ident = sb("ident", [P, P])
        stat = sb("stat", [P, 3, GT, 6])
        mv = sb("mv", [P, 3, GT, 2])
        var_eps = sb("var_eps", [P, 2, GT])
        var_eps3 = sb("var_eps3", [P, TILES])
        rstd = sb("rstd", [P, 2, GT])
        mean3 = sb("mean3", [P, TILES])
        rstd3 = sb("rstd3", [P, TILES])
        half_neg = sb("half_neg", [P, GT])
        zero = sb("zero", [P, D + 1])
        wgu = sb("wgu", [P, 4, CHUNKS * CHUNK], F32R)
        stage = sb("stage", [P, LANES, 2, CHUNK])
        count = sb("count", [P, P + 2 * TILES + EXPERTS + SLOTS + 2 * LANES])
        below, steps = count[:, 0:P], count[:, P:P + TILES]
        desc, slot_no = count[:, P + TILES:P + TILES + EXPERTS], \
            count[:, P + TILES + EXPERTS:P + TILES + EXPERTS + SLOTS]
        token_no = count[:, P + TILES + EXPERTS + SLOTS:P + 2 * TILES + EXPERTS + SLOTS]
        spare = count[:, P + 2 * TILES + EXPERTS + SLOTS:]
        ones = sb("ones", [P, P])
        raw_r = sb("raw_r", [P, 2, ROUTER])
        wr = sb("wr", [P, 4, ROUTER], F32R)
        gb = sb("gb", [P, 1])
        half_gb = sb("half_gb", [P, 1])

        lg = sb("lg", [P, TILES, EXPERTS + 1])
        cls = sb("cls", [P, 1])
        msk = sb("msk", [P, TILES])

        early = ExitStack()

        def sa(name, shape, dt=F32):
            return early.enter_context(nc.sbuf_tensor(name, shape, dt))

        ids = sa("ids", [UROWS, 2, GN], I32)
        onehot = sa("onehot", [UROWS, GN], F32R)
        cw = sa("cw", [UROWS, D])
        cwr = sa("cwr", [UROWS, D], F32R)
        gam = sa("gam", [P, D])
        bet = sa("bet", [P, D])
        emb = sa("emb", [P, GT, D])
        xn = sa("xn", [P, GT, D])
        xt = sa("xt", [P, 3, GN], F32R)
        wqk = sa("wqk", [P, 4, 512], F32R)
        wvg = sa("wvg", [P, 4, 448], F32R)
        raw_flat = stage[:, :, :, :].rearrange("p a b c -> p (a b c)")
        raw_qk = raw_flat[:, 0:1024].rearrange("p (k n) -> p k n", k=2)
        raw_vg = raw_flat[:, 1024:1920].rearrange("p (k n) -> p k n", k=2)
        kphi = sa("kphi", [P, 2, GN])
        qz = sa("qz", [P, HEADS, GN])
        xp1 = sa("xp1", [P, 2, GN])
        ex = sa("ex", [P, 2, GN])
        vp = sa("vp", [P, GT, HEADS, P])
        sT = sa("sT", [P, 4, 384])
        wo = sa("wo", [P, 2, D])
        gt = sa("gt", [P, 2, GT, D])
        numden = sa("numden", [P, HEADS, GN])
        den = sa("den", [P, GT, HEADS, 1])
        rec = sa("rec", [P, GT, HEADS, 1])
        recB = sa("recB", [P, GT, HEADS, HD])
        oT = sa("oT", [P, 2, GN])
        early.close()

        with nc.sbuf_tensor("x3", [P, TILES, D + 1], F32) as x3:
            pass
        xst_odd = sb("xst_odd", [P, 3, LANES * P], F32R)
        sb("x3_rest", [P, TILES * (D + 1) - 3 * LANES * P])
        x3t = sb("x3t", [P, 3, B * S], F32R)
        hid = sb("hid", [P, HTILES, GN])
        sg = sb("sg", [P, 2, GN])
        wsdn = sb("wsdn", [P, HTILES, D])
        wdn = sb("wdn", [P, 4, EXPERTS * D], F32R)
        prob = sb("prob", [P, TILES, EXPERTS])
        pick = sb("pick", [P, 2, TILES, EXPERTS])
        best = sb("best", [P, 2, TILES, 1])
        gates = sb("gates", [P, 2, TILES])
        tmp = sb("tmp", [P, TILES, EXPERTS])
        tmp2 = sb("tmp2", [P, TILES, EXPERTS])
        one = sb("one", [P, TILES, 1])
        alpha = sb("alpha", [P, 2, TILES])
        run = sb("run", [P, 2, EXPERTS + TILES, EXPERTS])
        wide = sb("wide", [P, EXPERTS, TILES])
        ends = sb("ends", [P, 3, 4 + EXPERTS])
        expert_f = sb("expert_f", [1, SLOTS, 1])
        expert = sb("expert", [1, SLOTS], I32)
        pos_f = sb("pos_f", [P, 2, TILES])
        pos = sb("pos", [P, 2, TILES], I32)
        xs = sb("xs", [P, 2, LANES, D + 1])
        pad = sb("pad", [P, 2, LANES])
        dest_f = sb("dest_f", [P, 2, LANES])
        dest = sb("dest", [P, 2, LANES], I32)
        xst_even = sb("xst_even", [P, 3, LANES * P], F32R)
        xst = [xst_even, xst_odd]
        sgs = sb("sgs", [P, LANES, HID])
        hs = sb("hs", [P, LANES, HID])
        hsT = sb("hsT", [P, 3, LANES * P], F32R)
        ys = sb("ys", [P, 2, LANES, D])
        lgT = ys[0:ROUTER, :, :, :].rearrange("p a b c -> p (a b c)")[:, 0:2 * GN].rearrange("p (a n) -> p a n", a=2)
        at_slot = xs[0:1, :, :, :].rearrange("p a b c -> p (a b c)")[:, 0:SLOTS * EXPERTS].rearrange(
            "p (s e) -> p s e", e=EXPERTS)
        back = [wgu[:, k, 0:TILES * D].bitcast(F32).rearrange("p (t d) -> p t d", d=D) for k in range(2)]
        scaled = raw_flat[:, 0:2 * len(HELPED) * D].rearrange("p (k n d) -> p k n d", k=2, d=D)

        s_win0 = sem("s_win0")
        s_win = sem("s_win")
        s_cls = sem("s_cls")
        s_cw = sem("s_cw")
        s_msk = sem("s_msk")
        s_gb = sem("s_gb")
        s_aw = sem("s_aw")
        s_idn = sem("s_idn")
        s_const = sem("s_const")
        s_passed = sem("s_passed")
        s_mean = sem("s_mean")
        s_oh = sem("s_oh")
        s_cwr = sem("s_cwr")
        s_whi = sem("s_whi")
        s_wlo = sem("s_wlo")
        s_conv = sem("s_conv")
        s_emb = sem("s_emb")
        s_bn = [sem(f"s_bn{k}") for k in range(3)]
        s_mv = [sem(f"s_mv{k}") for k in range(3)]
        s_ve = [sem(f"s_ve{k}") for k in range(3)]
        s_rs = [sem(f"s_rs{k}") for k in range(3)]
        s_gam = sem("s_gam")
        s_h0 = sem("s_h0")
        s_xn = sem("s_xn")
        s_T = sem("s_T")
        s_hi = sem("s_hi")
        s_lo = sem("s_lo")
        s_proj = sem("s_proj")
        s_act = sem("s_act")
        s_phi = sem("s_phi")
        s_vg = sem("s_vg")
        s_sc = sem("s_sc")
        s_ev = sem("s_ev")
        s_mask = sem("s_mask")
        s_pv = sem("s_pv")
        s_nd = sem("s_nd")
        s_denT = sem("s_denT")
        s_den = sem("s_den")
        s_rec = sem("s_rec")
        s_recB = sem("s_recB")
        s_recT = sem("s_recT")
        s_nrm = sem("s_nrm")
        s_wo = sem("s_wo")
        s_wog = sem("s_wog")
        s_res = sem("s_res")
        s_zx = sem("s_zx")
        s_wst = [sem(f"s_wst{j}") for j in range(LANES)]
        s_ghi = sem("s_ghi")
        s_glo = sem("s_glo")
        s_cst = sem("s_cst")
        s_wr = sem("s_wr")
        s_wsdn = sem("s_wsdn")
        s_dlo = sem("s_dlo")
        s_x3 = sem("s_x3")
        s_T3 = sem("s_T3")
        s_hi3 = sem("s_hi3")
        s_lo3 = sem("s_lo3")
        s_lgT = sem("s_lgT")
        s_lgc = sem("s_lgc")
        s_lg = sem("s_lg")
        s_lgv = sem("s_lgv")
        s_clear = sem("s_clear")
        s_r = sem("s_r")
        s_diff = sem("s_diff")
        s_exp = sem("s_exp")
        s_pick = sem("s_pick")
        s_cnt = sem("s_cnt")
        s_pos = sem("s_pos")
        s_eid = sem("s_eid")
        s_scat = [[sem(f"s_scat{k}{half}") for half in range(2)] for k in range(2)]
        s_no = sem("s_no")
        s_pad = sem("s_pad")
        s_kept = sem("s_kept")
        s_dest = sem("s_dest")
        s_sgu = sem("s_sgu")
        s_sg = sem("s_sg")
        s_hid = sem("s_hid")
        s_sdn = sem("s_sdn")
        s_shr = sem("s_shr")
        s_xl = [sem(f"s_xl{j}") for j in range(2 * LANES)]
        s_xT = sem("s_xT")
        s_xhi = sem("s_xhi")
        s_xlo = sem("s_xlo")
        s_gu = sem("s_gu")
        s_si = sem("s_si")
        s_hs = sem("s_hs")
        s_hT = sem("s_hT")
        s_hTc = sem("s_hTc")
        s_hTl = sem("s_hTl")
        s_dn = sem("s_dn")
        s_ys = sem("s_ys")
        s_st = [sem(f"s_st{odd}") for odd in range(2)]
        s_back = [sem(f"s_back{g}") for g in range(GROUPS)]
        s_sum = [sem(f"s_sum{k}") for k in range(2)]
        s_scaled = sem("s_scaled")
        s_add = [sem(f"s_add{k}") for k in range(2)]
        s_out = sem("s_out")

        def wait(eng, s, value):
            if not isinstance(value, int) or value > 0:
                eng.wait_ge(s, value)

        def wait_apart(eng, s, value):
            eng.wait_ge(s, value)
            eng.sem_inc(s_passed, 1)

        def down_bank(j, last=False):
            return bank[6 if last else 4][:, 0:D] if j == 2 else bank[7][:, j * D:(j + 1) * D]

        def added_before(t):
            return sum(n not in HELPED for n in range(t))

        def shared_at(g, t):
            return bank[(6, 7, 0, 1)[t]][:, 0:D] if g == GROUPS - 1 else \
                bank[6 + t // 2][:, (t % 2) * D:(t % 2 + 1) * D]

        def gate_of(g, t):
            return gt[:, bass.ds(g % 2, 1), t, :]

        def tile_of(x, g, t):
            return x[:, bass.ds(g * GT + t, 1)]

        block = ctx.enter_context(nc.Block())

        @block.sync
        def _(sp):
            sp.dma_start(cls[:, :], classes).then_inc(s_cls, 16)
            sp.dma_start(ids[:, 0, :], windows[:, 0:GN]).then_inc(s_win0, 16)
            sp.dma_start(msk[:, :], tok_mask).then_inc(s_msk, 16)
            sp.dma_start(gam[:, :], gamma).then_inc(s_gb, 16)
            sp.dma_start(bet[:, :], beta).then_inc(s_gb, 16)
            sp.dma_start(ident[:, :], ident_in).then_inc(s_idn, 16)
            sp.dma_start(raw_qk, w_qk).then_inc(s_aw, 16)
            sp.dma_start(raw_vg, w_vg).then_inc(s_aw, 16)
            sp.dma_start(wo[:, :, :], w_o).then_inc(s_idn, 16)
            sp.dma_start(ids[:, 1, :], windows[:, GN:2 * GN]).then_inc(s_win, 16)
            sp.dma_start(count[:, :], counting).then_inc(s_cst, 16)
            sp.dma_start(raw_r[:, :, :], w_router).then_inc(s_cst, 16)
            sp.dma_start(gb[:, :], gate_bias).then_inc(s_cst, 16)
            sp.wait_ge(s_const, 1)
            sp.dma_start(sorted_x.rearrange("(s p) d -> p s d", p=P),
                         zero[:, :].unsqueeze(1).to_broadcast([P, SLOTS, D + 1])).then_inc(s_zx, 16)
            sp.wait_ge(s_wlo, 2)
            for g in range(GROUPS):
                if g in (1, 2):
                    sp.wait_ge(s_oh, g)
                    sp.wait_ge(s_win, 16 * g)
                    sp.dma_start(ids[:, (g + 1) % 2, :], windows[:, (g + 1) * GN:(g + 2) * GN]).then_inc(s_win, 16)
                for j in range(LANES):
                    if g:
                        sp.wait_ge(s_glo, LANES * (g - 1) + j + 1)
                    sp.dma_start(stage[:, j, :, :], w_gu[:, LANES * g + j, :, :]).then_inc(s_wst[j], 16)
            sp.wait_ge(s_pv, 8 * GROUPS)
            sp.dma_start(wsdn[:, :, :], w_sdn).then_inc(s_wsdn, 16)
            for n in range(DOWN_CHUNKS):
                sp.wait_ge(s_glo, CHUNKS - LANES + n + 1)
                sp.dma_start(stage[:, n % LANES, :, :], w_dn[:, n, :, :]).then_inc(s_wst[n % LANES], 16)

            def load(i, odd):
                for j in range(LANES):
                    sp.dma_start(xs[:, odd, j, :], sorted_x[bass.ds((i * LANES + j) * P, P), :]
                                 ).then_inc(s_xl[odd * LANES + j], 16)

            for k in range(2):
                for half in range(2):
                    sp.wait_ge(s_scat[k][half], 16 * HALF)
            load(0, 0)
            load(1, 1)
            sp.wait_ge(s_kept, 1)
            load(2, 0)
            with sp.Fori(0, (ROUNDS - 3) // 2) as n:
                for k in range(2):
                    sp.wait_ge(s_kept, 2 * n + k + 2)
                    load(2 * n + k + 3, 1 - k)
            for odd in range(2):
                sp.wait_ge(s_st[odd], 16 * LANES * ((ROUNDS + 1 - odd) // 2))
            for g in range(GROUPS):
                for k in range(2):
                    row = 1 + (k * GROUPS + g) * GN
                    sp.dma_start(back[k][:, g * GT:(g + 1) * GT, :],
                                 routed[row:row + GN, :].rearrange("(t p) d -> p t d", p=P)).then_inc(s_back[g], 16)
            for t in range(TILES):
                if t in HELPED:
                    sp.wait_ge(s_add[1], HELPED.index(t) + 1)
                else:
                    sp.wait_ge(s_sum[1], added_before(t) + 1)
                sp.wait_ge(s_shr, t + 1 if t >= TILES - GT else (t // GT + 1) * GT)
                sp.dma_start(out[:, t * D:(t + 1) * D], h[:, t, :]).then_inc(s_out, 16)
            sp.wait_ge(s_out, 16 * TILES)

        @block.gpsimd
        def _(pool):
            pool.memset(zero[:, :], 0.0).then_inc(s_const, 1)
            pool.memset(half_neg[:, :], -0.5).then_inc(s_const, 1)
            pool.memset(qz[:, :, :], 0.0).then_inc(s_const, 1)

            def rsqrt(k, g):
                pool.wait_ge(s_ve[k], g + 1)
                out = rstd[:, k, :] if k < 2 else rstd3[:, bass.ds(g * GT, GT)]
                var = var_eps[:, k, :] if k < 2 else var_eps3[:, bass.ds(g * GT, GT)]
                pool.tensor_tensor(out, var, half_neg[:, :], ALU.pow).then_inc(s_rs[k], 1)

            def affine(g, n):
                wait_apart(pool, s_ev, 8 * g + n + 1)
                diag = sT[:, n % 4, :].rearrange("p (b q) -> p b q", q=P)[:, 0::2, :]
                pool.affine_select(out=diag, in_=diag, compare_op=ALU.is_ge, fill=0.0, base=0,
                                   pattern=[[0, 2], [1, P]], channel_multiplier=-1).then_inc(s_mask, 1)

            def low_chunk(g, j):
                pool.wait_ge(s_ghi, LANES * g + j + 1)
                at = bass.ds((LANES * g + j) * CHUNK, CHUNK)
                pool.tensor_tensor(wgu[:, 1::2, at], stage[:, j, :, :], wgu[:, 0::2, at].bitcast(F32),
                                   ALU.subtract).then_inc(s_glo, 1)

            def attention(g, before, more):
                if before:
                    for j in range(LANES):
                        low_chunk(g - 1, j)
                if more:
                    rsqrt(0, g + 1)
                if not more:
                    low_chunk(g, 0)
                for n in range(8):
                    affine(g, n)
                    if n == 3 and not more:
                        low_chunk(g, 1)
                    if n == 3 and more:
                        rsqrt(1, g + 1)
                    if n == 4 and not more:
                        rsqrt(2, g - 1)
                if before and more:
                    rsqrt(2, g - 1)

            pool.wait_ge(s_const, 2)
            rsqrt(0, 0)
            pool.memset(vp[:, :, :, :], 1.0).then_inc(s_const, 1)
            pool.memset(ones[:, :], 1.0).then_inc(s_const, 1)
            pool.wait_ge(s_whi, 2)
            pool.tensor_tensor(wvg[:, 1::2, :], raw_vg, wvg[:, 0::2, :].bitcast(F32), ALU.subtract).then_inc(s_wlo, 1)
            rsqrt(1, 0)
            attention(0, False, True)
            with pool.Fori(1, GROUPS - 1) as g:
                attention(g, True, True)
            attention(GROUPS - 1, True, False)
            low_chunk(GROUPS - 1, 2)
            rsqrt(2, GROUPS - 1)

            for n in range(DOWN_CHUNKS - 1):
                pool.wait_ge(s_ghi, CHUNKS + n + 1)
                pool.tensor_tensor(wdn[:, 1::2, n * CHUNK:(n + 1) * CHUNK], stage[:, n % LANES, :, :],
                                   wdn[:, 0::2, n * CHUNK:(n + 1) * CHUNK].bitcast(F32),
                                   ALU.subtract).then_inc(s_glo, 1)

            pool.wait_ge(s_zx, 16)
            for k in range(2):
                pool.wait_ge(s_pos, k + 1)
                for t in range(TILES):
                    half = t // HALF
                    if k == 0:
                        pool.wait_ge(s_no, 1)
                    elif t % HALF == 0:
                        pool.wait_ge(s_no, 2 + half)
                    pool.indirect_dma_start(out=sorted_x, out_offset=bass.IndirectOffsetOnAxis(
                        ap=pos[:, k, t:t + 1].bitcast(U32), axis=0), in_=x3[:, t, :], in_offset=None,
                        bounds_check=SLOTS * P - 1, oob_is_err=True).then_inc(s_scat[k][half], 16)

            def store(i, odd):
                wait_apart(pool, s_dest, i + 1)
                for j in range(LANES):
                    wait_apart(pool, s_ys, LANES * i + j + 1)
                    pool.indirect_dma_start(out=routed, out_offset=bass.IndirectOffsetOnAxis(
                        ap=dest[:, odd, j:j + 1].bitcast(U32), axis=0), in_=ys[:, odd, j, :], in_offset=None,
                        bounds_check=2 * (TILES + LANES) * P, oob_is_err=True).then_inc(s_st[odd], 16)

            with pool.Fori(0, ROUNDS // 2) as n:
                for k in range(2):
                    store(2 * n + k, k)
            store(ROUNDS - 1, 0)
            pool.wait_ge(s_shr, GT * (GROUPS - 1))
            for n, k in [(n, k) for g in range(GROUPS) for k in range(2) for n in range(len(HELPED))
                         if HELPED[n] // GT == g]:
                    t = HELPED[n]
                    if k == 0:
                        pool.wait_ge(s_scaled, 2 * n + 2)
                    else:
                        pool.wait_ge(s_add[0], n + 1)
                    pool.tensor_tensor(h[:, t, :], scaled[:, k, n, :], h[:, t, :], ALU.add).then_inc(s_add[k], 1)

        @block.scalar
        def _(act):
            act.dma_start(cw[:, :], conv_w).then_inc(s_cw, 16)
            act.wait_ge(s_const, 1)
            act.activation(rstd3[:, 0:1], zero[:, 0:1], ACT.Exp)

            def embed(g):
                for t in range(GT):
                    if t % 2 == 0:
                        act.wait_ge(s_conv, 2 * g + t // 2 + 1)
                    act.activation(emb[:, t, :], bank[t // 2][:, (t % 2) * D:(t % 2 + 1) * D], ACT.Copy,
                                   scale=msk[:, bass.ds(g * GT + t, 1)]).then_inc(s_emb, 1)

            def high(g):
                act.wait_ge(s_T, 2 * g + 1)
                act.activation(xt[:, 0, :], bank[0][:, :], ACT.Copy).then_inc(s_hi, 1)
                act.wait_ge(s_T, 2 * g + 2)
                act.activation(xt[0:D1, 2, :], bank[1][0:D1, :], ACT.Copy).then_inc(s_hi, 1)

            def feature_parts(g):
                for m in range(4):
                    act.wait_ge(s_proj, 8 * g + m + 1)
                    wait(act, s_phi, 6 * g + (-2, 0, 1, 3)[m])
                    act.activation(xp1[:, m % 2, :], bank[2 + m % 2][:, :], ACT.Copy, bias=1.0).then_inc(s_act, 1)
                    act.activation(ex[:, m % 2, :], bank[2 + m % 2][:, :], ACT.Exp).then_inc(s_act, 1)

            def values_gates(g):
                for t in range(GT):
                    act.wait_ge(s_proj, 8 * g + 5 + t)
                    b = bank[2 + t % 2]
                    v = vp[:, t, :, :].rearrange("p (a b) c -> p a (b c)", b=2)
                    for odd in range(2):
                        act.activation(v[:, :, 3 * HD * odd:3 * HD * odd + HD],
                                       b[:, 0:256].rearrange("p (a b c) -> p a b c", a=2, b=2)[:, :, odd, :],
                                       ACT.Copy).then_inc(s_vg, 1)
                    act.activation(gate_of(g, t)[:, 0, :], b[:, 256:448], ACT.Tanh, scale=0.5).then_inc(s_vg, 1)

            def high3(g):
                act.wait_ge(s_T3, 2 * g + 1)
                tok = slice(g * GN, (g + 1) * GN)
                act.activation(x3t[:, 0, tok], bank[0][:, :], ACT.Copy).then_inc(s_hi3, 1)
                act.wait_ge(s_T3, 2 * g + 2)
                act.activation(x3t[0:D1, 2, tok], bank[1][0:D1, :], ACT.Copy).then_inc(s_hi3, 1)

            def heads(g, more):
                for n in range(8):
                    act.wait_ge(s_sc, 8 * g + n + 1)
                    if n >= 4:
                        act.wait_ge(s_pv, 8 * g + n - 3)
                    act.activation(sT[:, n % 4, :], bank[4 + n % 2][:, 0:384], ACT.Copy).then_inc(s_ev, 1)
                    if n >= 3 and n % 2:
                        numerators(g, n // 2 - 1)
                    if n == 6 and more:
                        high(g + 1)
                    if n == 3 and not more:
                        high3(0)
                    if n in (1, 3, 5) and more or n == 1:
                        high_chunk(g, n // 2 if more else 2)
                    if n == 6 and not more:
                        high3(1)
                numerators(g, 3)
                if not more:
                    high3(2)

            def numerators(g, hd):
                act.wait_ge(s_pv, 8 * g + 2 * hd + 2)
                act.activation(numden[:, hd, :], bank[6 + hd % 2][:, :], ACT.Copy).then_inc(s_nd, 1)

            def high_chunk(g, j):
                act.wait_ge(s_wst[j], 16 * g + 16)
                act.activation(wgu[:, 0::2, bass.ds((LANES * g + j) * CHUNK, CHUNK)], stage[:, j, :, :],
                               ACT.Copy).then_inc(s_ghi, 1)

            def attention(g, more):
                feature_parts(g)
                if more:
                    embed(g + 1)
                values_gates(g)
                if not more:
                    high_chunk(g, 0)
                    high_chunk(g, 1)
                heads(g, more)

            act.wait_ge(s_msk, 16)
            embed(0)
            act.wait_ge(s_aw, 32)
            act.activation(wqk[:, 0::2, :], raw_qk[:, :, :], ACT.Copy).then_inc(s_whi, 1)
            act.activation(wvg[:, 0::2, :], raw_vg[:, :, :], ACT.Copy).then_inc(s_whi, 1)
            high(0)
            act.wait_ge(s_const, 5)
            attention(0, True)
            with act.Fori(1, GROUPS - 1) as g:
                attention(g, True)
            act.wait_ge(s_cst, 48)
            act.activation(wr[:, 0::2, :], raw_r[:, :, :], ACT.Copy).then_inc(s_wr, 1)
            act.activation(half_gb[:, :], gb[:, :], ACT.Copy, scale=0.5).then_inc(s_wr, 1)
            attention(GROUPS - 1, False)

            def logits(g):
                act.wait_ge(s_lgT, g + 1)
                if g >= 2:
                    act.wait_ge(s_lg, g - 1)
                act.activation(lgT[:, g % 2, :], bank[6][0:ROUTER, :], ACT.Copy).then_inc(s_lgc, 1)

            def shared(g, first, behind):
                for m in range(first, behind):
                    act.wait_ge(s_sgu, HTILES * g + m + 1)
                    wait(act, s_hid, HTILES * g + m - 1)
                    act.activation(sg[:, m % 2, :], bank[2 + 2 * (m % 2)][:, :], ACT.Silu).then_inc(s_sg, 1)

            logits(0)
            logits(1)
            shared(0, 0, 1)
            logits(2)
            shared(0, 1, 4)
            high3(GROUPS - 1)
            shared(0, 4, 5)
            logits(GROUPS - 1)
            act.wait_ge(s_diff, 1)
            act.activation(prob[:, :, :], tmp[:, :, :], ACT.Exp).then_inc(s_exp, 1)
            act.activation(one[:, :, 0], lg[:, :, EXPERTS], ACT.Tanh, bias=half_gb[:, 0:1],
                           scale=0.5).then_inc(s_exp, 1)
            shared(0, 5, HTILES)

            def high_down(n):
                act.wait_ge(s_wst[n % LANES], 16 * (CHUNKS // LANES + n // LANES) + 16)
                act.activation(wdn[:, 0::2, n * CHUNK:(n + 1) * CHUNK], stage[:, n % LANES, :, :],
                               ACT.Copy).then_inc(s_ghi, 1)

            act.wait_ge(s_res, TILES)
            for n in range(DOWN_CHUNKS - 1):
                high_down(n)
            shared(1, 0, 1)
            high_down(DOWN_CHUNKS - 1)
            shared(1, 1, HTILES)
            shared(2, 0, HTILES)

            def high_rows(i, odd):
                act.wait_ge(s_xT, i + 1)
                act.activation(xst[odd][:, 0, :], bank[0][:, 0:LANES * P], ACT.Copy).then_inc(s_xhi, 1)
                act.activation(xst[odd][0:D1, 2, :], bank[1][0:D1, 0:LANES * P], ACT.Copy).then_inc(s_xhi, 1)

            def gate(i, j):
                act.wait_ge(s_gu, LANES * i + j + 1)
                act.activation(sgs[:, j, :], bank[2 + j][:, 0:HID], ACT.Silu).then_inc(s_si, 1)

            def results(i, odd, last=False):
                act.wait_ge(s_dest, i + 1)
                for j in range(LANES):
                    act.wait_ge(s_dn, LANES * i + (2, 2, 3)[j])
                    act.activation(ys[:, odd, j, :], down_bank(j, last), ACT.Copy).then_inc(s_ys, 1)

            def round_(i, odd, before, more):
                gate(i, 0)
                gate(i, 1)
                if more:
                    high_rows(i + 1, 1 - odd)
                gate(i, 2)
                if before:
                    results(i - 1, 1 - odd)
                act.wait_ge(s_hT, i + 1)
                act.activation(hsT[:, 0, :], bank[5][:, 0:LANES * P], ACT.Copy).then_inc(s_hTc, 1)
                act.activation(hsT[0:HID - P, 2, :], bank[6][0:HID - P, 0:LANES * P], ACT.Copy).then_inc(s_hTc, 1)

            high_rows(0, 0)
            round_(0, 0, False, True)
            with act.Fori(0, (ROUNDS - 3) // 2) as n:
                round_(2 * n + 1, 1, True, True)
                round_(2 * n + 2, 0, True, True)
            round_(ROUNDS - 2, 1, True, True)
            round_(ROUNDS - 1, 0, True, False)
            shared(3, 0, 1)
            results(ROUNDS - 1, 0, True)
            shared(3, 1, HTILES)
            for n, t in enumerate(HELPED):
                act.wait_ge(s_back[t // GT], 32)
                for k in range(2):
                    act.activation(scaled[:, k, n, :], back[k][:, t, :], ACT.Copy,
                                   scale=gates[:, k, t:t + 1]).then_inc(s_scaled, 1)

        @block.vector
        def _(dve):
            def make_onehot(g):
                dve.tensor_scalar(onehot[:, :], ids[:, bass.ds(g % 2, 1), :].rearrange("p a n -> p (a n)"),
                                  cls[0:UROWS, 0:1], None, ALU.is_equal).then_inc(s_oh, 1)

            def statistics(k, g, src, eps, ready=None):
                for t in range(GT):
                    if ready:
                        dve.wait_ge(ready, t + 1)
                    dve.bn_stats(stat[:, k, t, :], src(t)).then_inc(s_bn[k], 1)
                wait_apart(dve, s_bn[k], g * GT + GT)
                for t in range(GT):
                    dve.bn_aggr(mv[:, k, t, :], stat[:, k, t, :]).then_inc(s_mv[k], 1)
                dve.wait_ge(s_mv[k], g * GT + GT)
                dve.tensor_scalar(var_eps[:, k, :] if k < 2 else var_eps3[:, bass.ds(g * GT, GT)], mv[:, k, :, 1],
                                  eps, None, ALU.add).then_inc(s_ve[k], 1)
                if k == 2:
                    dve.tensor_copy(mean3[:, bass.ds(g * GT, GT)], mv[:, k, :, 0]).then_inc(s_mean, 1)

            def scaled_by_gamma(g):
                dve.wait_ge(s_rs[0], g + 1)
                for t in range(GT):
                    dve.scalar_tensor_tensor(out=emb[:, t, :], in0=emb[:, t, :], scalar=mv[:, 0, t, 0:1],
                                             in1=gam[:, :], op0=ALU.subtract, op1=ALU.mult).then_inc(s_gam, 1)

            def embedding_norm(g):
                for t in range(GT):
                    dve.wait_ge(s_gam, GT * g + t + 1)
                    dve.scalar_tensor_tensor(out=tile_of(h, g, t)[:, 0, :], in0=emb[:, t, :],
                                             scalar=rstd[:, 0, t:t + 1],
                                             in1=bet[:, :], op0=ALU.mult, op1=ALU.add).then_inc(s_h0, 1)
                wait_apart(dve, s_h0, GT * g + GT)

            def normed(g):
                dve.wait_ge(s_rs[1], g + 1)
                for t in range(GT):
                    dve.tensor_scalar(xn[:, t, :], tile_of(h, g, t)[:, 0, :], mv[:, 1, t, 0:1], rstd[:, 1, t:t + 1],
                                      ALU.subtract, ALU.mult).then_inc(s_xn, 1)

            def low(g):
                dve.wait_ge(s_hi, 2 * g + 1)
                dve.tensor_tensor(xt[:, 1, :], bank[0][:, :], xt[:, 0, :].bitcast(F32), ALU.subtract).then_inc(s_lo, 1)
                dve.wait_ge(s_hi, 2 * g + 2)
                dve.tensor_tensor(xt[D1:P, 2, :], bank[1][0:D1, :], xt[0:D1, 2, :].bitcast(F32),
                                  ALU.subtract).then_inc(s_lo, 1)

            def features(g, pair):
                for m in (2 * pair, 2 * pair + 1):
                    dve.wait_ge(s_act, 8 * g + 2 * m + 2)
                    parts = [(kphi[:, pair, :], slice(0, P))] if m % 2 == 0 else \
                        [(qz[0:HD, 2 * pair, :], slice(0, HD)), (qz[HD:P, 2 * pair + 1, :], slice(HD, P))]
                    for dst, r in parts:
                        dve.scalar_tensor_tensor(out=dst, in0=ex[r, m % 2, :], scalar=1.0, in1=xp1[r, m % 2, :],
                                                 op0=ALU.min, op1=ALU.max).then_inc(s_phi, 1)

            def reciprocals(g):
                dve.wait_ge(s_denT, g + 1)
                for odd in range(2):
                    dve.tensor_scalar(den[:, :, odd::2, 0],
                                      bank[4 + odd][:, 384:384 + 2 * GT].rearrange("p (t c) -> p t c", t=GT),
                                      1e-6, None, ALU.max).then_inc(s_den, 1)
                dve.wait_ge(s_den, 2 * g + 2)
                dve.reciprocal(rec[:, :, :, 0], den[:, :, :, 0]).then_inc(s_rec, 1)
                dve.wait_ge(s_rec, g + 1)
                dve.tensor_copy(recB[:, :, :, :], rec[:, :, :, :].to_broadcast([P, GT, HEADS, HD])).then_inc(s_recB, 1)

            def divide(g):
                for hd in range(HEADS):
                    if hd % 2 == 0:
                        dve.wait_ge(s_recT, 2 * g + hd // 2 + 1)
                    r = slice(0, HD) if hd % 2 == 0 else slice(HD, P)
                    dve.tensor_tensor(oT[r, hd // 2, :], bank[4 + hd // 2][r, :], numden[r, hd, :],
                                      ALU.mult).then_inc(s_nrm, 1)

            def gated(g, tiles=range(GT)):
                for t in tiles:
                    dve.wait_ge(s_wo, 2 * g + t // 2 + 1)
                    b = bank[2 + t // 2]
                    gg = gate_of(g, t)[:, 0, :]
                    dve.scalar_tensor_tensor(out=gg, in0=gg, scalar=1.0,
                                             in1=b[:, (t % 2) * D:(t % 2 + 1) * D], op0=ALU.add,
                                             op1=ALU.mult).then_inc(s_wog, 1)

            def residual(g):
                for t in range(GT):
                    hh = tile_of(h, g, t)
                    dve.wait_ge(s_wog, 4 * g + t + 1)
                    dve.scalar_tensor_tensor(out=hh, in0=gate_of(g, t), scalar=0.5, in1=hh, op0=ALU.mult,
                                             op1=ALU.add).then_inc(s_res, 1)

            def normed3(g):
                dve.wait_ge(s_mean, g + 1)
                dve.wait_ge(s_rs[2], g + 1)
                for t in range(GT * g, GT * g + GT):
                    dve.tensor_scalar(x3[:, t, 0:D], h[:, t, :], mean3[:, t:t + 1], rstd3[:, t:t + 1], ALU.subtract,
                                      ALU.mult).then_inc(s_x3, 1)

            def low3(g):
                dve.wait_ge(s_hi3, 2 * g + 1)
                tok = slice(g * GN, (g + 1) * GN)
                dve.tensor_tensor(x3t[:, 1, tok], bank[0][:, :], x3t[:, 0, tok].bitcast(F32),
                                  ALU.subtract).then_inc(s_lo3, 1)
                dve.wait_ge(s_hi3, 2 * g + 2)
                dve.tensor_tensor(x3t[D1:P, 2, tok], bank[1][0:D1, :], x3t[0:D1, 2, tok].bitcast(F32),
                                  ALU.subtract).then_inc(s_lo3, 1)

            def logits(g):
                dve.wait_ge(s_lg, g + 1)
                dve.tensor_copy(lg[:, g * GT:(g + 1) * GT, :],
                                bank[7][:, 0:GT * ROUTER].rearrange("p (t c) -> p t c", t=GT)[:, :, 0:EXPERTS + 1]
                                ).then_inc(s_lgv, 1)

            def shared_hidden(g, m):
                dve.wait_ge(s_sg, HTILES * g + m + 1)
                dve.tensor_tensor(hid[:, m, :], bank[3 + 2 * (m % 2)][:, :], sg[:, m % 2, :],
                                  ALU.mult).then_inc(s_hid, 1)

            def attention(g, before, more):
                if more:
                    dve.wait_ge(s_win, 16 * g + 16)
                    make_onehot(g + 1)
                features(g, 0)
                if before:
                    reciprocals(g - 1)
                features(g, 1)
                if before:
                    divide(g - 1)
                if more:
                    wait_apart(dve, s_emb, GT * (g + 2))
                    statistics(0, g + 1, lambda t: emb[:, t, :], 1e-12)
                if not more:
                    normed3(0)
                    normed3(1)
                if before:
                    gated(g - 1, (0, 1))
                if more:
                    scaled_by_gamma(g + 1)
                if before:
                    gated(g - 1, (2, 3))
                if more:
                    embedding_norm(g + 1)
                    statistics(1, g + 1, lambda t: tile_of(h, g + 1, t)[:, 0, :], 1e-5)
                    normed(g + 1)
                if before:
                    residual(g - 1)
                if more:
                    low(g + 1)
                if before:
                    wait_apart(dve, s_res, GT * g)
                    statistics(2, g - 1, lambda t: tile_of(h, g - 1, t)[:, 0, :], 1e-5)

            dve.wait_ge(s_cw, 16)
            dve.tensor_copy(cwr[:, :], cw[:, :]).then_inc(s_cwr, 1)
            dve.wait_ge(s_cwr, 1)
            dve.tensor_tensor(cwr[WIN_LO:UROWS, :], cw[WIN_LO:UROWS, :], cwr[WIN_LO:UROWS, :].bitcast(F32),
                              ALU.subtract).then_inc(s_cwr, 1)
            dve.wait_ge(s_win0, 16)
            dve.wait_ge(s_cls, 16)
            make_onehot(0)
            statistics(0, 0, lambda t: emb[:, t, :], 1e-12, s_emb)
            dve.wait_ge(s_gb, 32)
            scaled_by_gamma(0)
            embedding_norm(0)
            statistics(1, 0, lambda t: tile_of(h, 0, t)[:, 0, :], 1e-5)
            dve.wait_ge(s_whi, 1)
            dve.tensor_tensor(wqk[:, 1::2, :], raw_qk[:, :, :], wqk[:, 0::2, :].bitcast(F32),
                              ALU.subtract).then_inc(s_wlo, 1)
            normed(0)
            low(0)
            dve.wait_ge(s_const, 5)
            attention(0, False, True)
            with dve.Fori(1, GROUPS - 1) as g:
                attention(g, True, True)
            dve.wait_ge(s_cst, 48)
            dve.tensor_copy(x3[:, :, D], token_no).then_inc(s_no, 1)
            dve.wait_ge(s_wr, 2)
            dve.tensor_tensor(wr[:, 1::2, :], raw_r[:, :, :], wr[:, 0::2, :].bitcast(F32),
                              ALU.subtract).then_inc(s_wr, 1)
            attention(GROUPS - 1, True, False)
            low3(0)
            normed3(2)
            low3(1)
            reciprocals(GROUPS - 1)
            low3(2)
            divide(GROUPS - 1)
            shared_hidden(0, 0)
            logits(0)
            gated(GROUPS - 1)
            residual(GROUPS - 1)
            logits(1)
            dve.wait_ge(s_res, GT * GROUPS)
            statistics(2, GROUPS - 1, lambda t: tile_of(h, GROUPS - 1, t)[:, 0, :], 1e-5)
            shared_hidden(0, 1)
            dve.memset(run[:, :, :, :], 0.0).then_inc(s_clear, 1)
            dve.memset(ends[:, :, :], 0.0).then_inc(s_clear, 1)
            normed3(GROUPS - 1)
            shared_hidden(0, 2)
            logits(2)
            shared_hidden(0, 3)
            low3(GROUPS - 1)
            logits(GROUPS - 1)

            chain = [0]

            def aside(ins):
                chain[0] += 1
                ins.then_inc(s_r, 1)

            def step(ins):
                aside(ins)
                dve.wait_ge(s_r, chain[0])

            all3 = [P, TILES, EXPERTS]

            def choose(k):
                step(dve.tensor_reduce(best[:, k, :, 0], prob[:, :, :], AX.X, ALU.max))
                step(dve.tensor_tensor(tmp[:, :, :], prob[:, :, :], best[:, k, :, :].to_broadcast(all3), ALU.is_equal))
                step(dve.tensor_tensor(tmp[:, :, :], tmp[:, :, :], desc.unsqueeze(1).to_broadcast(all3), ALU.mult))
                step(dve.tensor_reduce(tmp2[:, :, 0], tmp[:, :, :], AX.X, ALU.max))
                dve.tensor_tensor(pick[:, k, :, :], tmp[:, :, :], tmp2[:, :, 0:1].to_broadcast(all3),
                                  ALU.is_equal).then_inc(s_pick, 1)

            dve.wait_ge(s_lgv, GROUPS)
            step(dve.tensor_reduce(best[:, 0, :, 0], lg[:, :, 0:EXPERTS], AX.X, ALU.max))
            dve.tensor_tensor(tmp[:, :, :], lg[:, :, 0:EXPERTS], best[:, 0, :, :].to_broadcast(all3),
                              ALU.subtract).then_inc(s_diff, 1)
            shared_hidden(0, 4)
            dve.wait_ge(s_exp, 2)
            step(dve.tensor_reduce(best[:, 0, :, 0], prob[:, :, :], AX.X, ALU.add))
            step(dve.reciprocal(best[:, 1, :, 0], best[:, 0, :, 0]))
            step(dve.tensor_tensor(prob[:, :, :], prob[:, :, :], best[:, 1, :, :].to_broadcast(all3), ALU.mult))
            choose(0)
            dve.wait_ge(s_pick, 1)
            step(dve.scalar_tensor_tensor(out=prob[:, :, :], in0=pick[:, 0, :, :], scalar=-2.0, in1=prob[:, :, :],
                                          op0=ALU.mult, op1=ALU.add))
            choose(1)
            shared_hidden(0, HTILES - 1)
            dve.wait_ge(s_clear, 2)
            dve.wait_ge(s_cnt, 1)
            step(dve.tensor_copy(run[:, 0, EXPERTS:, :], bank[1][:, 0:P].rearrange("p (t e) -> p t e", t=TILES)))
            for n, d in enumerate((1, 2, 4, 8)):
                a, b = n % 2, 1 - n % 2
                step(dve.tensor_tensor(run[:, b, EXPERTS:, :], run[:, a, EXPERTS:, :],
                                       run[:, a, EXPERTS - d:EXPERTS - d + TILES, :], ALU.add))
            total = run[:, 0, EXPERTS + TILES - 1, :]
            wide3 = [P, EXPERTS, TILES]
            aside(dve.tensor_tensor(wide[:, :, :], total.unsqueeze(2).to_broadcast(wide3),
                                    steps.unsqueeze(1).to_broadcast(wide3), ALU.is_gt))
            step(dve.tensor_tensor(tmp[:, :, :], bank[0][:, 0:P].rearrange("p (t e) -> p t e", t=TILES),
                                   run[:, 0, EXPERTS - 1:EXPERTS - 1 + TILES, :], ALU.add))
            step(dve.tensor_reduce(ends[:, 0, 4:], wide[:, :, :], AX.X, ALU.add))
            for n, d in enumerate((1, 2, 4)):
                a, b = n % 2, 1 - n % 2
                step(dve.tensor_tensor(ends[:, b, 4:], ends[:, a, 4:], ends[:, a, 4 - d:4 - d + EXPERTS], ALU.add))
            step(dve.scalar_tensor_tensor(out=tmp[:, :, :],
                                          in0=ends[:, 1, 3:3 + EXPERTS].unsqueeze(1).to_broadcast(all3),
                                          scalar=float(P), in1=tmp[:, :, :], op0=ALU.mult, op1=ALU.add))
            for k in range(2):
                step(dve.tensor_tensor(tmp2[:, :, :], tmp[:, :, :], pick[:, k, :, :], ALU.mult))
                step(dve.tensor_reduce(pos_f[:, k, :], tmp2[:, :, :], AX.X, ALU.add))
                dve.tensor_copy(pos[:, k, :], pos_f[:, k, :]).then_inc(s_pos, 1)
            dve.wait_ge(s_sdn, 2)
            shared_hidden(1, 0)
            slot3 = [1, SLOTS, EXPERTS]
            step(dve.tensor_tensor(at_slot[:, :, :], slot_no[0:1, :].unsqueeze(2).to_broadcast(slot3),
                                   ends[0:1, 1, 4:].unsqueeze(1).to_broadcast(slot3), ALU.is_ge))
            step(dve.tensor_reduce(expert_f[:, :, 0], at_slot[:, :, :], AX.X, ALU.add))
            dve.tensor_scalar(expert[:, :], expert_f[:, :, 0], float(EXPERTS - 1), None, ALU.min).then_inc(s_eid, 1)
            shared_hidden(1, 1)
            step(dve.tensor_scalar(alpha[:, 0, :], one[:, :, 0], 0.5, 0.5, ALU.mult, ALU.add))
            step(dve.tensor_scalar(alpha[:, 1, :], alpha[:, 0, :], -1.0, 1.0, ALU.mult, ALU.add))
            step(dve.tensor_tensor(tmp2[:, :, 1], best[:, 0, :, 0], best[:, 1, :, 0], ALU.add))
            step(dve.reciprocal(tmp2[:, :, 2], tmp2[:, :, 1]))
            step(dve.tensor_tensor(tmp2[:, :, 3], tmp2[:, :, 2], alpha[:, 1, :], ALU.mult))
            for k in range(2):
                step(dve.tensor_tensor(gates[:, k, :], best[:, k, :, 0], tmp2[:, :, 3], ALU.mult))

            def add_shared(g, tiles, products):
                dve.wait_ge(s_sdn, products)
                if g == GROUPS - 1 and tiles[-1] == HELPED[-1] - GT * g:
                    dve.wait_ge(s_add[1], len(HELPED))
                for t in tiles:
                    n = GT * g + t
                    dve.scalar_tensor_tensor(out=h[:, n, :], in0=shared_at(g, t),
                                             scalar=alpha[:, 0, n:n + 1], in1=h[:, n, :], op0=ALU.mult,
                                             op1=ALU.add).then_inc(s_shr, 1)

            def second_rows(half):
                dve.wait_ge(s_scat[0][half], 16 * HALF)
                no = x3[:, half * HALF:(half + 1) * HALF, D]
                dve.tensor_scalar(no, no, float(TILES * P), None, ALU.add).then_inc(s_no, 1)

            for m in range(2, HTILES):
                shared_hidden(1, m)
                if m == 2:
                    add_shared(0, range(GT), 2)
                if m == HTILES - 1:
                    n = DOWN_CHUNKS - 1
                    dve.wait_ge(s_ghi, CHUNKS + n + 1)
                    dve.tensor_tensor(wdn[:, 1::2, n * CHUNK:(n + 1) * CHUNK], stage[:, n % LANES, :, :],
                                      wdn[:, 0::2, n * CHUNK:(n + 1) * CHUNK].bitcast(F32),
                                      ALU.subtract).then_inc(s_dlo, 1)
                if m in SECOND:
                    second_rows(SECOND.index(m))
            add_shared(1, range(GT), 4)
            for m in range(HTILES):
                shared_hidden(2, m)

            def low_rows(i, odd):
                dve.wait_ge(s_xhi, 2 * i + 2)
                dve.scalar_tensor_tensor(out=pad[:, odd, :], in0=xs[:, odd, :, D], scalar=0.0,
                                         in1=spare[:, odd * LANES:(odd + 1) * LANES], op0=ALU.is_equal,
                                         op1=ALU.mult).then_inc(s_pad, 1)
                dve.tensor_tensor(xst[odd][:, 1, :], bank[0][:, 0:LANES * P], xst[odd][:, 0, :].bitcast(F32),
                                  ALU.subtract).then_inc(s_xlo, 1)
                dve.tensor_tensor(xst[odd][D1:P, 2, :], bank[1][0:D1, 0:LANES * P], xst[odd][0:D1, 2, :].bitcast(F32),
                                  ALU.subtract).then_inc(s_xlo, 1)
                dve.wait_ge(s_pad, i + 1)
                dve.tensor_tensor(dest_f[:, odd, :], pad[:, odd, :], xs[:, odd, :, D], ALU.add).then_inc(s_kept, 1)

            def round_(i, more, odd, before):
                for j in range(LANES):
                    dve.wait_ge(s_si, LANES * i + j + 1)
                    dve.tensor_tensor(hs[:, j, :], bank[2 + j][:, HID:2 * HID], sgs[:, j, :],
                                      ALU.mult).then_inc(s_hs, 1)
                if more:
                    low_rows(i + 1, 1 - odd)
                dve.wait_ge(s_kept, i + 1)
                if not isinstance(before, int) or before:
                    dve.wait_ge(s_st[odd], 16 * LANES * before)
                dve.tensor_copy(dest[:, odd, :], dest_f[:, odd, :]).then_inc(s_dest, 1)
                if isinstance(i, int) and i == 0:
                    add_shared(2, (3,), 7)
                dve.wait_ge(s_hTc, 2 * i + 1)
                dve.tensor_tensor(hsT[:, 1, :], bank[5][:, 0:LANES * P], hsT[:, 0, :].bitcast(F32),
                                  ALU.subtract).then_inc(s_hTl, 1)
                dve.wait_ge(s_hTc, 2 * i + 2)
                dve.tensor_tensor(hsT[HID - P:P, 2, :], bank[6][0:HID - P, 0:LANES * P],
                                  hsT[0:HID - P, 2, :].bitcast(F32), ALU.subtract).then_inc(s_hTl, 1)

            low_rows(0, 0)
            add_shared(2, (0, 1, 2), 6)
            round_(0, True, 0, 0)
            round_(1, True, 1, 0)
            with dve.Fori(1, ROUNDS // 2) as n:
                for k in range(2):
                    round_(2 * n + k, True, k, n)
            round_(ROUNDS - 1, False, 0, ROUNDS // 2)

            def add_routed(tiles):
                for k in range(2):
                    for t in tiles:
                        if k == 0:
                            dve.wait_ge(s_back[t // GT], 32)
                        else:
                            dve.wait_ge(s_sum[0], added_before(t) + 1)
                        dve.scalar_tensor_tensor(out=h[:, t, :], in0=back[k][:, t, :], scalar=gates[:, k, t:t + 1],
                                                 in1=h[:, t, :], op0=ALU.mult, op1=ALU.add).then_inc(s_sum[k], 1)

            for m in range(HTILES):
                shared_hidden(3, m)
                if m >= HTILES - 2:
                    add_routed(range(2 * (m - HTILES + 2), 2 * (m - HTILES + 2) + 2))
            for g in range(1, GROUPS):
                add_routed([t for t in range(g * GT, (g + 1) * GT) if t not in HELPED])
            dve.wait_ge(s_sum[1], TILES - len(HELPED))
            add_shared(3, (0, 1), 8)
            add_shared(3, (2,), 9)
            add_shared(3, (3,), 10)

        @block.tensor
        def _(pe):
            def embed(g):
                pe.wait_ge(s_oh, g + 1)
                wait(pe, s_lo, 2 * g)
                for t in range(GT):
                    mm = pe.matmul(bank[t // 2][:, (t % 2) * D:(t % 2 + 1) * D], onehot[:, t * P:(t + 1) * P],
                                   cwr[:, :], start=True, stop=True)
                    if t % 2:
                        mm.then_inc(s_conv, 1)

            def transposes(g):
                pe.wait_ge(s_xn, GT * g + GT)
                for t in range(GT):
                    mm = pe.transpose(bank[0][:, t * P:(t + 1) * P], xn[:, t, 0:P], ident[:, :])
                mm.then_inc(s_T, 1)
                for t in range(GT):
                    mm = pe.transpose(bank[1][0:D1, t * P:(t + 1) * P], xn[:, t, P:D], ident[:, :])
                mm.then_inc(s_T, 1)

            def scores(g, n):
                hd, b = n // 2, n % 2
                if n >= 2:
                    pe.wait_ge(s_ev, 8 * g + n - 1)
                if n % 4 == 0:
                    pe.wait_ge(s_phi, 6 * g + (3 if n == 0 else 6))
                for kt in range(2):
                    o = b * S + kt * P
                    mm = pe.matmul(bank[4 + n % 2][:, kt * S:kt * S + S - kt * P], kphi[:, hd // 2, o:o + P],
                                   qz[:, hd, o:b * S + S], start=True, stop=True)
                mm.then_inc(s_sc, 1)

            def weighted(g, n):
                hd, b = n // 2, n % 2
                if b == 0:
                    wait(pe, s_nd, 4 * g + hd - 1)
                pe.wait_ge(s_mask, 8 * g + n + 1)
                for kt in range(2):
                    mm = pe.matmul(bank[6 + hd % 2][:, b * S + kt * P:b * S + S], vp[:, 2 * b + kt, hd, :],
                                   sT[:, n % 4, kt * S:kt * S + S - kt * P], start=kt == 0, stop=kt == 1)
                mm.then_inc(s_pv, 1)

            def denominators(g):
                for hd in range(HEADS):
                    wait_apart(pe, s_nd, 4 * g + hd + 1)
                    r = HD if hd % 2 == 0 else 0
                    for t in range(GT):
                        c = 384 + 2 * t + hd // 2
                        mm = pe.transpose(bank[4 + hd % 2][:, c:c + 1], numden[r:r + 1, hd, t * P:(t + 1) * P],
                                          ident[r:r + 1, r:r + 1])
                mm.then_inc(s_denT, 1)

            def spread(g):
                pe.wait_ge(s_recB, g + 1)
                for pair in range(2):
                    for t in range(GT):
                        mm = pe.transpose(bank[4 + pair][:, t * P:(t + 1) * P],
                                          recB[:, t, 2 * pair:2 * pair + 2, :].rearrange("p h c -> p (h c)"),
                                          ident[:, :])
                    mm.then_inc(s_recT, 1)

            def keys_queries(g, pair):
                if pair == 0:
                    pe.wait_ge(s_hi, 2 * g + 1)
                for m in (2 * pair, 2 * pair + 1):
                    if m < 2:
                        wait(pe, s_vg, 12 * g - 3 + 3 * m)
                    else:
                        pe.wait_ge(s_act, 8 * g + 2 * m - 2)
                    for k, (x, w) in enumerate(pieces(xt, wqk, slice(m * P, (m + 1) * P), slice(0, GN))):
                        if m == 0 and k in (2, 3):
                            pe.wait_ge(s_lo, 2 * g + k - 1)
                        mm = pe.matmul(bank[2 + m % 2][:, :], w, x, start=k == 0, stop=k == 4)
                    mm.then_inc(s_proj, 1)

            def values_gates(g):
                for t in range(GT):
                    if t < 2:
                        pe.wait_ge(s_act, 8 * g + 6 + 2 * t)
                    else:
                        pe.wait_ge(s_vg, 12 * g + 3 * t - 3)
                    for k, (x, w) in enumerate(pieces(xt, wvg, slice(0, 448), slice(t * P, (t + 1) * P))):
                        mm = pe.matmul(bank[2 + t % 2][:, 0:448], x, w, start=k == 0, stop=k == 4)
                    mm.then_inc(s_proj, 1)

            def output(g, last):
                pe.wait_ge(s_nrm, 4 * g + 4)
                for t in range(GT):
                    if t % 2 == 0 and not last:
                        pe.wait_ge(s_vg, 12 * (g + 1) + (9, 12)[t // 2])
                    for k in range(2):
                        mm = pe.matmul(bank[2 + t // 2][:, (t % 2) * D:(t % 2 + 1) * D], oT[:, k, t * P:(t + 1) * P],
                                       wo[:, k, :], start=k == 0, stop=k == 1)
                    if t % 2:
                        mm.then_inc(s_wo, 1)

            def transposes3(g):
                pe.wait_ge(s_x3, GT * g + GT)
                wait(pe, s_lo3, 2 * g)
                for t in range(GT):
                    mm = pe.transpose(bank[0][:, t * P:(t + 1) * P], x3[:, g * GT + t, 0:P], ident[:, :])
                mm.then_inc(s_T3, 1)
                for t in range(GT):
                    mm = pe.transpose(bank[1][0:D1, t * P:(t + 1) * P], x3[:, g * GT + t, P:D], ident[:, :])
                mm.then_inc(s_T3, 1)

            def router(g):
                pe.wait_ge(s_lo3, 2 * g + 2)
                wait(pe, s_lgc, g)
                for k, (x, w) in enumerate(pieces(x3t, wr, slice(0, ROUTER), slice(g * GN, (g + 1) * GN))):
                    mm = pe.matmul(bank[6][0:ROUTER, :], w, x, start=k == 0, stop=k == 4)
                mm.then_inc(s_lgT, 1)

            def logits(g):
                pe.wait_ge(s_lgc, g + 1)
                wait(pe, s_lgv, g)
                for t in range(GT):
                    mm = pe.transpose(bank[7][:, t * ROUTER:(t + 1) * ROUTER], lgT[:, g % 2, t * P:(t + 1) * P],
                                      ident[0:ROUTER, 0:ROUTER])
                mm.then_inc(s_lg, 1)

            def counts():
                for k in range(2):
                    pe.wait_ge(s_pick, k + 1)
                    for n, w in ((1, ones[:, :]), (0, below)):
                        mm = pe.matmul(bank[n][:, 0:P], w, pick[:, k, :, :].rearrange("p t e -> p (t e)"),
                                       start=k == 0, stop=k == 1)
                mm.then_inc(s_cnt, 1)

            def shared_up(g, m):
                if not isinstance(g, int) or g or m >= 2:
                    pe.wait_ge(s_hid, HTILES * g + m - 1)
                for k in range(2):
                    c = EXPERTS * CHUNK + k * SHARED + m * P
                    for n, (x, w) in enumerate(pieces(x3t, wgu, slice(c, c + P), bass.ds(g * GN, GN))):
                        mm = pe.matmul(bank[2 + 2 * (m % 2) + k][:, :], w, x, start=n == 0, stop=n == 4)
                mm.then_inc(s_sgu, 1)

            def shared_down(g, tiles, between=None):
                if 0 in tiles:
                    wait(pe, s_shr, GT * g)
                together = len(tiles) > 1
                steps = [(t, m) for ms in (range(HTILES - 1), (HTILES - 1,)) for t in tiles for m in ms] \
                    if together else [(t, m) for t in tiles for m in range(HTILES)]
                for n, (t, m) in enumerate(steps):
                    if between and n == len(tiles) * (HTILES - 1):
                        between()
                    if m == HTILES - 1:
                        pe.wait_ge(s_hid, HTILES * g + HTILES)
                    elif n == 0:
                        pe.wait_ge(s_hid, HTILES * g + HTILES - 1)
                    mm = pe.matmul(shared_at(g, t), hid[:, m, t * P:(t + 1) * P],
                                   wsdn[:, m, :], start=m == 0, stop=m == HTILES - 1)
                mm.then_inc(s_sdn, 1)

            def attention(g, before, more):
                keys_queries(g, 0)
                if before:
                    denominators(g - 1)
                keys_queries(g, 1)
                if more:
                    embed(g + 1)
                if before:
                    spread(g - 1)
                values_gates(g)
                if before:
                    output(g - 1, False)
                for n in range(8):
                    scores(g, n)
                    if n == 6 and more:
                        transposes(g + 1)
                    if n in (2, 6) and not more:
                        transposes3(n // 4)
                    if n >= 2:
                        if n == 2:
                            pe.wait_ge(s_vg, 12 * g + 12)
                        weighted(g, n - 2)
                weighted(g, 6)
                weighted(g, 7)

            def experts_of(i, rounds):
                n = rounds * LANES
                _, es = nc.values_load_multi_w_load_instructions(
                    expert[0:1, bass.ds(LANES * i, n)], engines=(mybir.EngineType.PE,), min_val=0, max_val=EXPERTS - 1,
                    skip_runtime_bounds_check_because="VectorE limits it to EXPERTS - 1, and a count is not negative")
                return [es[k:k + LANES] for k in range(0, n, LANES)]

            pe.wait_ge(s_cwr, 2)
            embed(0)
            pe.wait_ge(s_gam, 1)
            for _ in range(WARM):
                pe.matmul(bank[7][:, 0:D], zero[:, 0:P], zero[:, 0:D], start=True, stop=True)
            pe.wait_ge(s_idn, 32)
            transposes(0)
            pe.wait_ge(s_wlo, 2)
            pe.wait_ge(s_const, 5)
            attention(0, False, True)
            with pe.Fori(1, GROUPS - 1) as g:
                attention(g, True, True)
            attention(GROUPS - 1, True, False)

            transposes3(2)
            pe.wait_ge(s_wr, 3)
            pe.wait_ge(s_nd, HEADS * GROUPS - 1)
            router(0)
            denominators(GROUPS - 1)
            router(1)
            spread(GROUPS - 1)
            pe.wait_ge(s_glo, CHUNKS)
            shared_up(0, 0)
            logits(0)
            router(2)
            pe.wait_ge(s_hid, 1)
            output(GROUPS - 1, True)
            logits(1)
            shared_up(0, 1)
            pe.wait_ge(s_wog, TILES)
            shared_up(0, 2)
            logits(2)
            shared_up(0, 3)
            transposes3(GROUPS - 1)
            shared_up(0, 4)
            router(GROUPS - 1)
            logits(GROUPS - 1)
            shared_up(0, 5)
            pe.wait_ge(s_lgv, GROUPS)
            pe.wait_ge(s_wsdn, 16)
            shared_down(0, (0, 2), counts)
            shared_up(1, 0)
            shared_down(0, (1, 3))
            for m in range(1, HTILES):
                shared_up(1, m)
            shared_down(1, (0, 2))
            shared_down(1, (1, 3))
            for m in range(HTILES):
                shared_up(2, m)
            shared_down(2, (0, 2))
            pe.wait_ge(s_eid, 1)
            first, = experts_of(0, 1)
            pe.wait_ge(s_glo, CHUNKS + DOWN_CHUNKS - 1)
            pe.wait_ge(s_dlo, 1)

            def rows(i, odd, pair):
                for j in range(LANES):
                    pe.wait_ge(s_xl[odd * LANES + j], 16 * pair + 16)
                for j in range(LANES):
                    pe.transpose(bank[0][:, j * P:(j + 1) * P], xs[:, odd, j, 0:P], ident[:, :])
                for j in range(LANES):
                    mm = pe.transpose(bank[1][0:D1, j * P:(j + 1) * P], xs[:, odd, j, P:D], ident[:, :])
                mm.then_inc(s_xT, 1)

            def up(i, j, e, odd):
                if j == 0:
                    pe.wait_ge(s_xlo, 2 * i + 2)
                if j == 2 and not (isinstance(i, int) and i == 0):
                    pe.wait_ge(s_hTc, 2 * i)
                for n, (x, w) in enumerate(pieces(xst[odd], wgu, bass.ds(e * CHUNK, CHUNK), slice(j * P, (j + 1) * P))):
                    mm = pe.matmul(bank[2 + j][:, 0:CHUNK], x, w, start=n == 0, stop=n == 4)
                mm.then_inc(s_gu, 1)

            def turn(i):
                for j in range(LANES):
                    pe.wait_ge(s_hs, LANES * i + j + 1)
                    pe.transpose(bank[5][:, j * P:(j + 1) * P], hs[:, j, 0:P], ident[:, :])
                    mm = pe.transpose(bank[6][0:HID - P, j * P:(j + 1) * P], hs[:, j, P:HID], ident[:, :])
                mm.then_inc(s_hT, 1)

            def down(i, more, es):
                for j in range(LANES):
                    if j == 0:
                        pe.wait_ge(s_hTl, 2 * i + 2)
                    if j == 2 and more:
                        pe.wait_ge(s_hs, LANES * (i + 1) + 3)
                    for n, (x, w) in enumerate(pieces(hsT, wdn, bass.ds(es[j] * D, D), slice(j * P, (j + 1) * P))):
                        mm = pe.matmul(down_bank(j, not more), x, w, start=n == 0, stop=n == 4)
                    mm.then_inc(s_dn, 1)

            def round_(i, es, before, more, odd, pair):
                up(i, 0, es[0], 1 - odd)
                up(i, 1, es[1], 1 - odd)
                if more:
                    rows(i + 1, odd, pair)
                up(i, 2, es[2], 1 - odd)
                if not before:
                    pe.wait_ge(s_shr, 2 * GT + 3)
                    shared_down(2, (3,))
                if before:
                    down(i - 1, True, before)
                turn(i)

            rows(0, 0, 0)
            shared_down(2, (1,))
            round_(0, first, None, True, 1, 0)
            pe.wait_ge(s_shr, 3 * GT)

            def pair_of_rounds(n):
                e0, e1, e2 = experts_of(2 * n, 3)
                round_(2 * n + 1, e1, e0, True, 0, n + 1)
                round_(2 * n + 2, e2, e1, True, 1, n + 1)

            with pe.Fori(0, (ROUNDS - 3) // 4) as n:
                pair_of_rounds(2 * n)
                pair_of_rounds(2 * n + 1)
            if (ROUNDS - 3) // 2 % 2:
                pair_of_rounds((ROUNDS - 3) // 2 - 1)
            e0, e1, e2 = experts_of(ROUNDS - 3, 3)
            round_(ROUNDS - 2, e1, e0, True, 0, (ROUNDS - 1) // 2)
            round_(ROUNDS - 1, e2, e1, False, 1, 0)
            shared_up(3, 0)
            down(ROUNDS - 1, False, e2)
            pe.wait_ge(s_ys, SLOTS - LANES)
            for m in range(1, HTILES):
                shared_up(3, m)
            pe.wait_ge(s_ys, SLOTS)
            shared_down(3, (0, 1))
            shared_down(3, (2,))
            shared_down(3, (3,))


def lay_out(x, mask, W3, W5, W7, gamma, beta, Wq, Wk, Wv, Wo, Wg, router_w, w_gate, w_up, w_down, ws_gate,
            ws_up, ws_down, sg_w, sg_b):
    half = TAPS // 2
    padded = np.full((B, S + 2 * half), -1, x.dtype)
    padded[:, half:half + S] = x
    windows = np.stack([padded[:, k:k + S].reshape(-1) for k in range(TAPS) for _ in range(CLS)])
    conv = np.zeros((TAPS, CLS, D), W3.dtype)
    for n, w in enumerate((W3, W5, W7)):
        k = w.shape[2]
        conv[half - k // 2:half + k // 2 + 1, :, 64 * n:64 * n + 64] = w.transpose(2, 1, 0)
    classes = np.zeros((P, 1), np.float32)
    for lo in (0, WIN_LO):
        classes[lo:lo + WIN, 0] = np.tile(np.arange(CLS), TAPS)

    def doubled(w, pad):
        return np.concatenate([w, np.full((WIN_LO - WIN, w.shape[1]), pad, w.dtype), w])

    def twice(w):
        return np.ascontiguousarray(np.stack([w[:P], np.concatenate([w[P:], w[P:]])], axis=1))

    qk = np.concatenate([Wk[:, :P], Wq[:, :P], Wk[:, P:], Wq[:, P:]], axis=1)
    vg = np.concatenate([Wv, Wg], axis=1)
    gu = np.concatenate([w_gate, w_up], axis=2).transpose(1, 0, 2).reshape(D, EXPERTS * CHUNK)
    gu = np.concatenate([gu, ws_gate, ws_up], axis=1)
    dn = w_down.transpose(1, 0, 2).reshape(HID, EXPERTS * D)
    router = np.zeros((D, ROUTER), router_w.dtype)
    router[:, :EXPERTS] = router_w
    router[:, EXPERTS:EXPERTS + 1] = sg_w
    counting = np.concatenate([np.triu(np.ones((P, P)), 1)] + [
        np.broadcast_to(row, (P, len(row))) for row in
        (np.arange(TILES) * P, np.arange(EXPERTS, 0, -1), np.arange(SLOTS))]
        + [1 + np.arange(TILES * P).reshape(TILES, P).T]
        + [1 + 2 * TILES * P + np.arange(2 * LANES * P).reshape(2 * LANES, P).T], axis=1).astype(np.float32)
    return {
        "windows": doubled(windows, -1), "classes": classes, "conv_w": doubled(conv.reshape(WIN, D), 0),
        "tok_mask": np.ascontiguousarray(mask.reshape(TILES, P).T),
        "gamma": np.ascontiguousarray(np.broadcast_to(gamma, (P, D))),
        "beta": np.ascontiguousarray(np.broadcast_to(beta, (P, D))),
        "w_qk": twice(qk), "w_vg": twice(vg),
        "w_o": np.ascontiguousarray(Wo.reshape(2, P, D).transpose(1, 0, 2)),
        "ident_in": np.eye(P, dtype=np.float32),
        "w_gu": np.ascontiguousarray(twice(gu).reshape(P, 2, CHUNKS, CHUNK).transpose(0, 2, 1, 3)),
        "w_dn": np.ascontiguousarray(twice(dn).reshape(P, 2, DOWN_CHUNKS, CHUNK).transpose(0, 2, 1, 3)),
        "w_sdn": np.ascontiguousarray(ws_down.reshape(HTILES, P, D).transpose(1, 0, 2)),
        "w_router": twice(router), "gate_bias": np.ascontiguousarray(np.broadcast_to(sg_b, (P, 1))),
        "counting": counting,
    }

_ORDER = ["x", "mask_BS_f1_0", "L0_tok_W3", "L0_tok_W5", "L0_tok_W7", "L0_tok_ln_gamma", "L0_tok_ln_beta",
          "L0_attn_Wq", "L0_attn_Wk", "L0_attn_Wv", "L0_attn_Wo", "L0_attn_Wg", "L0_ffn_router_w",
          "L0_ffn_w_gate", "L0_ffn_w_up", "L0_ffn_w_down", "L0_ffn_ws_gate", "L0_ffn_ws_up", "L0_ffn_ws_down",
          "L0_ffn_sg_w", "L0_ffn_sg_b"]


def kernel(**inputs):
    import concourse.bacc as bacc
    from concourse.bass_utils import run_bass_kernel_spmd

    nc = bacc.Bacc("TRN2", target_bir_lowering=False, num_devices=1)
    arrays = lay_out(*[np.asarray(inputs[name]) for name in _ORDER])
    args = [nc.dram_tensor(f"{name}_dram", a.shape, mybir.dt.from_np(a.dtype), kind="ExternalInput").ap()
            for name, a in arrays.items()]
    out = nc.dram_tensor("out_dram", (P, TILES * D), F32, kind="ExternalOutput").ap()
    tower(nc, *args, out)
    result = run_bass_kernel_spmd(nc, [{f"{name}_dram": a for name, a in arrays.items()}], core_ids=[0])
    y = result.results[0]["out_dram"].reshape(P, TILES, D).transpose(1, 0, 2)
    return np.ascontiguousarray(y).reshape(B, S, D)
```
